# Optimizing a Trainium2 kernel written in Bass

```python
import numpy as np
import jax
import jax.numpy as jnp

def _softmax(x, axis=-1):
    return jax.nn.softmax(x, axis=axis)

def _gelu(x):
    return jax.nn.gelu(x, approximate=True)

def _silu(x):
    return jax.nn.silu(x)

def _sigmoid(x):
    return jax.nn.sigmoid(x)

def _layernorm(x, axis=-1, eps=1e-05):
    m = jnp.mean(x, axis=axis, keepdims=True)
    v = jnp.var(x, axis=axis, keepdims=True)
    return (x - m) / jnp.sqrt(v + eps)

def _scatter_add(tgt, idx, src, axis=0):
    return tgt.at[idx].add(src)

def _segment_sum(src, seg, n):
    return jax.ops.segment_sum(src, seg, n)
kernel_name = 'mk_gnn_preln_d4_gnn_r32_9f4384'

def setup_inputs(seed: int=0):
    np.random.seed(seed)
    _w = jnp.asarray

    def _rec_inputs():
        import jax
        import jax.numpy as jnp
        _gk = jax.random.key(seed)
        x = -0.0003713 + 1 * jax.random.normal(jax.random.fold_in(_gk, 1), (3125, 128), jnp.float32)
        src = jax.random.randint(jax.random.fold_in(_gk, 2), (50000,), 0, 3125, jnp.int32)
        dst = jax.random.randint(jax.random.fold_in(_gk, 3), (50000,), 0, 3125, jnp.int32)
        _o = jnp.argsort(dst, stable=True)
        src = src[_o]
        dst = dst[_o]
        edge_attr_128 = -8.16379e-05 + 0.999858 * jax.random.normal(jax.random.fold_in(_gk, 12), (50000, 128), jnp.float32)
        return (x, src, dst, edge_attr_128)
    x, src, dst, edge_attr_128 = _rec_inputs()

    def _L0_gnn_setup():
        import jax, jax.numpy as jnp
        import numpy as np
        N = 3125

        def gcn_conv(x, W, b, src, dst, n):
            loop = jnp.arange(n, dtype=src.dtype)
            s = jnp.concatenate([src, loop])
            d = jnp.concatenate([dst, loop])
            deg = jax.ops.segment_sum(jnp.ones_like(d, dtype=x.dtype), d, num_segments=n)
            dinv = jnp.where(deg > 0, deg ** (-0.5), 0.0)
            norm = dinv[s] * dinv[d]
            h = x @ W
            msg = h[s] * norm[:, None]
            out = jax.ops.segment_sum(msg, d, num_segments=n)
            return out + b
        key = jax.random.key(seed)
        k1, k2, k3, k4 = jax.random.split(key, 4)
        x = jax.random.normal(k1, (N, 128), dtype=jnp.float32)
        edge_index = jax.random.randint(k2, (2, 50000), 0, N, dtype=jnp.int64)
        glorot = (6.0 / (128 + 128)) ** 0.5
        W1 = jax.random.uniform(k3, (128, 128), jnp.float32, -glorot, glorot)
        W2 = jax.random.uniform(k4, (128, 128), jnp.float32, -glorot, glorot)
        b1 = jnp.zeros((128,), jnp.float32)
        b2 = jnp.zeros((128,), jnp.float32)
        return {'x': x, 'edge_index': edge_index, 'W1': W1, 'b1': b1, 'W2': W2, 'b2': b2}
    _L0_gnn_all = _L0_gnn_setup()
    _L0_gnn_in = {k: v for k, v in _L0_gnn_all.items() if k in ('W1', 'b1', 'W2', 'b2')}
    del _L0_gnn_all

    def _L1_gnn_setup():
        import jax, jax.numpy as jnp
        import numpy as np
        EMBED_DIM = 128
        NUM_LAYERS = 3
        MSG_FACTOR = 2
        LN_EPS = 1e-05

        def _layer_norm(x, scale, offset):
            m = jnp.mean(x, axis=-1, keepdims=True)
            v = jnp.var(x, axis=-1, keepdims=True)
            return (x - m) * jax.lax.rsqrt(v + LN_EPS) * scale + offset
        key = jax.random.key(seed)
        ks = jax.random.split(key, 16)
        N, E, d = (50000, 25000, EMBED_DIM)
        h = d * MSG_FACTOR
        L = NUM_LAYERS
        s = 0.02
        inp = {'nodes': jax.random.normal(ks[0], (N, d), jnp.float32), 'edges': jax.random.normal(ks[1], (E, d), jnp.float32), 'senders': jax.random.randint(ks[2], (E,), 0, N, jnp.int32), 'receivers': jax.random.randint(ks[3], (E,), 0, N, jnp.int32), 'w_node': jax.random.normal(ks[4], (d, d), jnp.float32) * s, 'b_node': jnp.zeros((d,), jnp.float32), 'w_edge': jax.random.normal(ks[5], (d, d), jnp.float32) * s, 'b_edge': jnp.zeros((d,), jnp.float32), 'ln_n_scale': jnp.ones((d,), jnp.float32), 'ln_n_offset': jnp.zeros((d,), jnp.float32), 'ln_e_scale': jnp.ones((d,), jnp.float32), 'ln_e_offset': jnp.zeros((d,), jnp.float32), 'msg_w1': jax.random.normal(ks[6], (L, 3 * d, h), jnp.float32) * s, 'msg_b1': jnp.zeros((L, h), jnp.float32), 'msg_w2': jax.random.normal(ks[7], (L, h, d), jnp.float32) * s, 'msg_b2': jnp.zeros((L, d), jnp.float32), 'upd_w': jax.random.normal(ks[8], (L, 2 * d, d), jnp.float32) * s, 'upd_b': jnp.zeros((L, d), jnp.float32), 'ln_scale': jnp.ones((L, d), jnp.float32), 'ln_offset': jnp.zeros((L, d), jnp.float32)}
        return inp
    _L1_gnn_all = _L1_gnn_setup()
    _L1_gnn_in = {k: v for k, v in _L1_gnn_all.items() if k in ('w_node', 'b_node', 'w_edge', 'b_edge', 'ln_n_scale', 'ln_n_offset', 'ln_e_scale', 'ln_e_offset', 'msg_w1', 'msg_b1', 'msg_w2', 'msg_b2', 'upd_w', 'upd_b', 'ln_scale', 'ln_offset')}
    del _L1_gnn_all

    def _L2_gnn_setup():
        import jax, jax.numpy as jnp
        import numpy as np
        N_NODES = 3125
        N_INCID = 62500
        HIDDEN = 128
        N_HE = 3125
        key = jax.random.key(seed)
        k1, k2, k3 = jax.random.split(key, 3)
        node_feats = jax.random.normal(k1, (N_NODES, HIDDEN), dtype=jnp.float32)
        hyperedge_index = jax.random.randint(k2, (2, N_INCID), 0, N_HE, dtype=jnp.int64)
        bound = float(np.sqrt(6.0 / (HIDDEN + 1)))
        W = jax.random.uniform(k3, (1, HIDDEN), dtype=jnp.float32, minval=-bound, maxval=bound)
        return {'node_feats': node_feats, 'hyperedge_index': hyperedge_index, 'num_hyperedges': N_HE, 'W': W}
    _L2_gnn_all = _L2_gnn_setup()
    _L2_gnn_in = {k: v for k, v in _L2_gnn_all.items() if k in ('W',)}
    del _L2_gnn_all

    def _L3_gnn_setup():
        import jax, jax.numpy as jnp
        import numpy as np
        N_NODES = 50000
        N_EDGES = 50000
        D_IN, D_HID, D_OUT = (128, 128, 128)

        def _gcn_conv(x, src, dst, W, b):
            n = x.shape[0]
            h = x @ W.T
            loop = jnp.arange(n)
            src_a = jnp.concatenate([src, loop])
            dst_a = jnp.concatenate([dst, loop])
            deg = jax.ops.segment_sum(jnp.ones_like(dst_a, dtype=h.dtype), dst_a, num_segments=n)
            dinv = jnp.where(deg > 0, jax.lax.rsqrt(deg), 0.0)
            norm = dinv[src_a] * dinv[dst_a]
            msg = h[src_a] * norm[:, None]
            out = jax.ops.segment_sum(msg, dst_a, num_segments=n)
            return out + b
        key = jax.random.key(seed)
        k1, k2, k3, k4, k5, k6, k7 = jax.random.split(key, 7)
        x = jax.random.normal(k1, (N_NODES, D_IN), dtype=jnp.float32)
        src = jax.random.randint(k2, (N_EDGES,), 0, N_NODES)
        dst = jax.random.randint(k3, (N_EDGES,), 0, N_NODES)
        edge_index = jnp.stack([src, dst]).astype(jnp.int64)
        W1 = jax.random.normal(k4, (D_HID, D_IN), dtype=jnp.float32) / np.sqrt(D_IN)
        b1 = jnp.zeros((D_HID,), dtype=jnp.float32)
        W2 = jax.random.normal(k5, (D_OUT, D_HID), dtype=jnp.float32) / np.sqrt(D_HID)
        b2 = jnp.zeros((D_OUT,), dtype=jnp.float32)
        return {'x': x, 'edge_index': edge_index, 'W1': W1, 'b1': b1, 'W2': W2, 'b2': b2}
    _L3_gnn_all = _L3_gnn_setup()
    _L3_gnn_in = {k: v for k, v in _L3_gnn_all.items() if k in ('W1', 'b1', 'W2', 'b2')}
    del _L3_gnn_all
    return {'x': x, 'src': src, 'dst': dst, 'edge_attr_128': edge_attr_128, 'L0_gnn_W1': _L0_gnn_in['W1'], 'L0_gnn_b1': _L0_gnn_in['b1'], 'L0_gnn_W2': _L0_gnn_in['W2'], 'L0_gnn_b2': _L0_gnn_in['b2'], 'L1_gnn_w_node': _L1_gnn_in['w_node'], 'L1_gnn_b_node': _L1_gnn_in['b_node'], 'L1_gnn_w_edge': _L1_gnn_in['w_edge'], 'L1_gnn_b_edge': _L1_gnn_in['b_edge'], 'L1_gnn_ln_n_scale': _L1_gnn_in['ln_n_scale'], 'L1_gnn_ln_n_offset': _L1_gnn_in['ln_n_offset'], 'L1_gnn_ln_e_scale': _L1_gnn_in['ln_e_scale'], 'L1_gnn_ln_e_offset': _L1_gnn_in['ln_e_offset'], 'L1_gnn_msg_w1': _L1_gnn_in['msg_w1'], 'L1_gnn_msg_b1': _L1_gnn_in['msg_b1'], 'L1_gnn_msg_w2': _L1_gnn_in['msg_w2'], 'L1_gnn_msg_b2': _L1_gnn_in['msg_b2'], 'L1_gnn_upd_w': _L1_gnn_in['upd_w'], 'L1_gnn_upd_b': _L1_gnn_in['upd_b'], 'L1_gnn_ln_scale': _L1_gnn_in['ln_scale'], 'L1_gnn_ln_offset': _L1_gnn_in['ln_offset'], 'L2_gnn_W': _L2_gnn_in['W'], 'L3_gnn_W1': _L3_gnn_in['W1'], 'L3_gnn_b1': _L3_gnn_in['b1'], 'L3_gnn_W2': _L3_gnn_in['W2'], 'L3_gnn_b2': _L3_gnn_in['b2']}

def reference(x, src, dst, edge_attr_128, L0_gnn_W1, L0_gnn_b1, L0_gnn_W2, L0_gnn_b2, L1_gnn_w_node, L1_gnn_b_node, L1_gnn_w_edge, L1_gnn_b_edge, L1_gnn_ln_n_scale, L1_gnn_ln_n_offset, L1_gnn_ln_e_scale, L1_gnn_ln_e_offset, L1_gnn_msg_w1, L1_gnn_msg_b1, L1_gnn_msg_w2, L1_gnn_msg_b2, L1_gnn_upd_w, L1_gnn_upd_b, L1_gnn_ln_scale, L1_gnn_ln_offset, L2_gnn_W, L3_gnn_W1, L3_gnn_b1, L3_gnn_W2, L3_gnn_b2):
    import jax
    import jax.numpy as jnp

    def _L0_gnn_ref(x, edge_index, W1, b1, W2, b2):
        import jax, jax.numpy as jnp
        import numpy as np
        N = 3125

        def gcn_conv(x, W, b, src, dst, n):
            loop = jnp.arange(n, dtype=src.dtype)
            s = jnp.concatenate([src, loop])
            d = jnp.concatenate([dst, loop])
            deg = jax.ops.segment_sum(jnp.ones_like(d, dtype=x.dtype), d, num_segments=n)
            dinv = jnp.where(deg > 0, deg ** (-0.5), 0.0)
            norm = dinv[s] * dinv[d]
            h = x @ W
            msg = h[s] * norm[:, None]
            out = jax.ops.segment_sum(msg, d, num_segments=n)
            return out + b
        src, dst = (edge_index[0], edge_index[1])
        h = jax.nn.relu(gcn_conv(x, W1, b1, src, dst, N))
        out = gcn_conv(h, W2, b2, src, dst, N)
        return out

    def _L1_gnn_ref(nodes, edges, senders, receivers, w_node, b_node, w_edge, b_edge, ln_n_scale, ln_n_offset, ln_e_scale, ln_e_offset, msg_w1, msg_b1, msg_w2, msg_b2, upd_w, upd_b, ln_scale, ln_offset):
        import jax, jax.numpy as jnp
        import numpy as np
        EMBED_DIM = 128
        NUM_LAYERS = 3
        MSG_FACTOR = 2
        LN_EPS = 1e-05

        def _layer_norm(x, scale, offset):
            m = jnp.mean(x, axis=-1, keepdims=True)
            v = jnp.var(x, axis=-1, keepdims=True)
            return (x - m) * jax.lax.rsqrt(v + LN_EPS) * scale + offset
        N = nodes.shape[0]
        n = _layer_norm(jax.nn.gelu(nodes @ w_node + b_node), ln_n_scale, ln_n_offset)
        e = _layer_norm(jax.nn.gelu(edges @ w_edge + b_edge), ln_e_scale, ln_e_offset)
        for l in range(NUM_LAYERS):
            x = jnp.concatenate([n[senders], n[receivers], e], axis=-1)
            m = jax.nn.relu(x @ msg_w1[l] + msg_b1[l])
            m = jax.nn.relu(m @ msg_w2[l] + msg_b2[l])
            agg = jax.ops.segment_sum(m, receivers, num_segments=N)
            upd = jnp.concatenate([n, agg], axis=-1) @ upd_w[l] + upd_b[l]
            upd = _layer_norm(upd, ln_scale[l], ln_offset[l])
            n = n + upd
        return n

    def _L2_gnn_ref(node_feats, hyperedge_index, num_hyperedges, W):
        import jax, jax.numpy as jnp
        import numpy as np
        N_NODES = 3125
        N_INCID = 62500
        HIDDEN = 128
        N_HE = 3125
        node_idx = hyperedge_index[0]
        he_idx = hyperedge_index[1]
        gathered = node_feats[node_idx]
        scores = jnp.einsum('ed,d->e', gathered, W[0])
        seg_max = jax.ops.segment_max(scores, he_idx, num_segments=num_hyperedges)
        seg_max = jnp.where(jnp.isfinite(seg_max), seg_max, 0.0)
        w = jnp.exp(scores - seg_max[he_idx])
        denom = jax.ops.segment_sum(w, he_idx, num_segments=num_hyperedges)
        w_norm = w / jnp.maximum(denom, 1e-20)[he_idx]
        out = jax.ops.segment_sum(w_norm[:, None] * gathered, he_idx, num_segments=num_hyperedges)
        return out

    def _L3_gnn_ref(x, edge_index, W1, b1, W2, b2):
        import jax, jax.numpy as jnp
        import numpy as np
        N_NODES = 50000
        N_EDGES = 50000
        D_IN, D_HID, D_OUT = (128, 128, 128)

        def _gcn_conv(x, src, dst, W, b):
            n = x.shape[0]
            h = x @ W.T
            loop = jnp.arange(n)
            src_a = jnp.concatenate([src, loop])
            dst_a = jnp.concatenate([dst, loop])
            deg = jax.ops.segment_sum(jnp.ones_like(dst_a, dtype=h.dtype), dst_a, num_segments=n)
            dinv = jnp.where(deg > 0, jax.lax.rsqrt(deg), 0.0)
            norm = dinv[src_a] * dinv[dst_a]
            msg = h[src_a] * norm[:, None]
            out = jax.ops.segment_sum(msg, dst_a, num_segments=n)
            return out + b
        src, dst = (edge_index[0], edge_index[1])
        h = _gcn_conv(x, src, dst, W1, b1)
        h = jax.nn.relu(h)
        out = _gcn_conv(h, src, dst, W2, b2)
        return out
    edge_index = jnp.stack([src, dst])
    h = jnp.maximum(_layernorm(x, axis=-1), 0.0)
    x = x + _L0_gnn_ref(h, edge_index, L0_gnn_W1, L0_gnn_b1, L0_gnn_W2, L0_gnn_b2)
    h = jnp.maximum(_layernorm(x, axis=-1), 0.0)
    x = x + _L1_gnn_ref(h, edge_attr_128, src, dst, L1_gnn_w_node, L1_gnn_b_node, L1_gnn_w_edge, L1_gnn_b_edge, L1_gnn_ln_n_scale, L1_gnn_ln_n_offset, L1_gnn_ln_e_scale, L1_gnn_ln_e_offset, L1_gnn_msg_w1, L1_gnn_msg_b1, L1_gnn_msg_w2, L1_gnn_msg_b2, L1_gnn_upd_w, L1_gnn_upd_b, L1_gnn_ln_scale, L1_gnn_ln_offset)
    h = jnp.maximum(_layernorm(x, axis=-1), 0.0)
    x = x + _L2_gnn_ref(h, edge_index, 3125, L2_gnn_W)
    h = jnp.maximum(_layernorm(x, axis=-1), 0.0)
    x = x + _L3_gnn_ref(h, edge_index, L3_gnn_W1, L3_gnn_b1, L3_gnn_W2, L3_gnn_b2)
    return x

_drawn_inputs = setup_inputs


def setup_inputs(seed=0):
    import zlib

    import numpy as np

    out = dict(_drawn_inputs(seed))
    spreads = {'L0_gnn_b1': (0.0, 0.1),
     'L0_gnn_b2': (0.0, 0.1),
     'L1_gnn_b_node': (0.0, 0.1),
     'L1_gnn_b_edge': (0.0, 0.1),
     'L1_gnn_ln_n_scale': (1.0, 0.2),
     'L1_gnn_ln_n_offset': (0.0, 0.1),
     'L1_gnn_ln_e_scale': (1.0, 0.6),
     'L1_gnn_ln_e_offset': (0.0, 0.419),
     'L1_gnn_msg_b1': (0.0, 0.1),
     'L1_gnn_msg_b2': (0.0, 0.1),
     'L1_gnn_upd_b': (0.0, 0.1),
     'L1_gnn_ln_scale': (1.0, 0.2),
     'L1_gnn_ln_offset': (0.0, 0.1),
     'L3_gnn_b1': (0.0, 0.283),
     'L3_gnn_b2': (0.0, 0.1)}
    factors = {}
    for name, (base, spread) in spreads.items():
        noise = np.random.default_rng([zlib.crc32(name.encode()), seed]).standard_normal(out[name].shape)
        drawn = base * np.exp(spread * noise) if base else spread * noise
        out[name] = jnp.asarray(drawn.astype(out[name].dtype))
    for name, factor in factors.items():
        out[name] = (out[name] * factor).astype(out[name].dtype)
    return out
```

```python
from contextlib import ExitStack

import concourse.bass as bass
from concourse import mybir

F32 = mybir.dt.float32
I32 = mybir.dt.int32
I16 = mybir.dt.int16
BF16 = mybir.dt.bfloat16
ALU = mybir.AluOpType
ACT = mybir.ActivationFunctionType
AX = mybir.AxisListType

N, E, D = 3125, 50000, 128
R = 125
W = N // R
T = E // R
G = 256
GROUPS = E // G + W
TILES = 2 * GROUPS
SLOTS = G * GROUPS
H = 2 * D
LN_EPS = 1e-5
CHUNK = 500
U = 5
NC = W // U


class Chain:

    def __init__(self, eng, sem):
        self.eng, self.sem, self.n, self.i, self.per, self.k = eng, sem, 0, None, 0, 0

    def loop(self, i, per):
        self.i, self.per, self.k = i, per, 0

    def end(self, trips):
        assert self.k == self.per, (self.k, self.per)
        self.n += self.per * trips
        self.i = None

    def __call__(self, ins):
        ins.then_inc(self.sem, 1)
        if self.i is None:
            self.n += 1
            self.eng.wait_ge(self.sem, self.n)
        else:
            self.k += 1
            self.eng.wait_ge(self.sem, self.i * self.per + (self.n + self.k))


class Scope:

    def __init__(self, nc):
        self.nc, self.sems = nc, []

    def __enter__(self):
        return self

    def semaphore(self, name):
        self.sems.append(self.nc.alloc_semaphore(name=name))
        return self.sems[-1]

    def __exit__(self, *_):
        self.nc.clear_and_free_semaphores(self.sems)
        self.nc.all_engine_barrier()


class Part:

    def __init__(self, nc, name, ctx):
        self.nc, self.name, self.ctx, self.own = nc, name, ctx, ExitStack()

    def __enter__(self):
        return self

    def __exit__(self, *_):
        self.own.close()

    def sb(self, name, shape, dt=F32):
        return self.own.enter_context(self.nc.sbuf_tensor(f"{self.name}_{name}", shape, dt))

    def ps(self, name, shape, dt=F32):
        return self.own.enter_context(self.nc.psum_tensor(f"{self.name}_{name}", shape, dt))

    def sem(self, name):
        return self.ctx.semaphore(f"{self.name}_{name}")

    def block(self):
        return self.own.enter_context(self.nc.Block())


def wide(ap, n):
    return ap.unsqueeze(2).to_broadcast([ap.shape[0], ap.shape[1], n])


def build_constants(nc, ctx, K):
    with Part(nc, "const", ctx) as p:
        made, link_p, link_v = p.sem("made"), p.sem("link_p"), p.sem("link_v")
        block = p.block()

        @block.gpsimd
        def _(pool):
            link = Chain(pool, link_p)
            link(nc.gpsimd.memset(K.ident[:, :], 0.0))
            link(nc.gpsimd.affine_select(out=K.ident[:, :], in_=K.ident[:, :], compare_op=ALU.not_equal,
                                         fill=1.0, base=0, pattern=[[-1, 128]], channel_multiplier=1))
            link(nc.gpsimd.memset(K.below[:, :], 1.0))
            link(nc.gpsimd.affine_select(out=K.below[:, :], in_=K.below[:, :], compare_op=ALU.is_gt,
                                         fill=0.0, base=0, pattern=[[1, 128]], channel_multiplier=-1))
            nc.gpsimd.iota(K.iota_i[:, :], pattern=[[1, N]], base=0, channel_multiplier=0).then_inc(made, 1)
            nc.gpsimd.iota(K.lane_i[:, :], pattern=[[0, 1]], base=0, channel_multiplier=1).then_inc(made, 1)

        @block.vector
        def _(dve):
            nc.vector.memset(K.ones[:, :], 1.0)
            nc.vector.memset(K.iota16[:, N:N + 1], -7)
            dve.wait_ge(made, 2)
            nc.vector.tensor_copy(K.iota16[:, 0:N], K.iota_i[:, :])
            nc.vector.tensor_copy(K.iota_f[:, :], K.iota_i[:, 0:128])
            nc.vector.tensor_copy(K.lane_f[:, :], K.lane_i[:, :])
            dve.wait_ge(link_p, 4)
            nc.vector.tensor_copy(K.ident16[:, :], K.ident[:, :])


def sort_edges(nc, ctx, K, src, dst, slot_meta, slot_raw):
    with Part(nc, "sort", ctx) as p:
        dst_i, src_i = p.sb("dst_i", [R, T], I32), p.sb("src_i", [R, T], I32)
        dst_f, quot_i = p.sb("dst_f", [R, T]), p.sb("quot_i", [R, T], I32)
        win, rel, low, high = (p.sb(n, [R, T]) for n in ("win", "rel", "low", "high"))
        mask, count, rank, term = (p.sb(n, [R, T]) for n in ("mask", "count", "rank", "term"))
        tot = p.sb("tot", [R, W])
        vid = p.sb("vid", [128, W])
        cnt_f, cnt_i, end_f = p.sb("cnt_f", [128, W]), p.sb("cnt_i", [128, W], I32), p.sb("end_f", [128, W])
        groups_f = p.sb("groups_f", [128, W])
        off = p.sb("off", [R, W])
        slot_i, tile_i, lane_i = (p.sb(n, [R, T], I32) for n in ("slot_i", "tile_i", "lane_i"))
        tile_f, lane_f = p.sb("tile_f", [R, T]), p.sb("lane_f", [R, T])
        zeros = p.sb("zeros", [128, 5120])
        pad = p.sb("pad", [128, TILES, 2], I32)
        ps_before, ps_cnt = p.ps("before", [128, 512]), p.ps("cnt", [128, 512])
        loaded, filled, zeroed, padded, pads_ready, zeros_ready, tots, summed, chain = (
            p.sem(n) for n in ("loaded", "filled", "zeroed", "padded", "pads_ready", "zeros_ready",
                               "tots", "summed", "chain"))
        block = p.block()
        raw = slot_raw.rearrange("(p a) d -> p (a d)", p=128)
        zero_cols = SLOTS * D // 128 // 11

        @block.sync
        def _(sp):
            sp.dma_start(dst_i[:, :], dst.rearrange("(p t) -> p t", p=R)).then_inc(loaded, 16)
            sp.dma_start(src_i[:, :], src.rearrange("(p t) -> p t", p=R)).then_inc(loaded, 16)
            sp.wait_ge(pads_ready, 2)
            sp.dma_start(slot_meta.rearrange("(p t) c -> p (t c)", p=128),
                         pad[:, :, :].rearrange("p t c -> p (t c)")).then_inc(padded, 16)
            sp.wait_ge(zeros_ready, 1)
            for c in range(11):
                sp.dma_start(raw[:, c * zero_cols:(c + 1) * zero_cols], zeros[:, 0:zero_cols]).then_inc(zeroed, 16)
            sp.wait_ge(padded, 16)
            sp.wait_ge(zeroed, 16 * 11)

        @block.gpsimd
        def _(pool):
            nc.gpsimd.memset(zeros[:, :], 0.0).then_inc(zeros_ready, 1)
            nc.gpsimd.memset(pad[:, :, 0:1], 0).then_inc(pads_ready, 1)
            nc.gpsimd.memset(pad[:, :, 1:2].bitcast(F32), -1.0).then_inc(pads_ready, 1)

        @block.tensor
        def _(pe):
            pe.wait_ge(tots, 1)
            nc.tensor.matmul(ps_before[0:R, 0:W], K.below[0:R, 0:R], tot[:, :], start=True, stop=True).then_inc(summed, 1)
            nc.tensor.matmul(ps_cnt[:, 0:W], K.ones[0:R, 0:128], tot[:, :], start=True, stop=True).then_inc(summed, 1)

        @block.vector
        def _(dve):
            link = Chain(dve, chain)
            link(nc.vector.tensor_copy(vid[:, :], K.iota_f[:, 0:W]))
            link(nc.vector.memset(rank[:, :], 0.0))
            dve.wait_ge(loaded, 32)
            link(nc.vector.tensor_copy(dst_f[:, :], dst_i[:, :]))
            link(nc.vector.tensor_scalar(quot_i[:, :], dst_f[:, :], 1.0 / R, None, ALU.mult))
            link(nc.vector.tensor_copy(win[:, :], quot_i[:, :]))
            link(nc.vector.scalar_tensor_tensor(out=rel[:, :], in0=win[:, :], scalar=-float(R), in1=dst_f[:, :],
                                                op0=ALU.mult, op1=ALU.add))
            link(nc.vector.tensor_scalar(low[:, :], rel[:, :], 0.0, None, ALU.is_lt))
            link(nc.vector.tensor_scalar(high[:, :], rel[:, :], float(R), None, ALU.is_ge))
            link(nc.vector.tensor_tensor(high[:, :], high[:, :], low[:, :], ALU.subtract))
            link(nc.vector.tensor_tensor(win[:, :], win[:, :], high[:, :], ALU.add))
            link(nc.vector.scalar_tensor_tensor(out=rel[:, :], in0=high[:, :], scalar=-float(R), in1=rel[:, :],
                                                op0=ALU.mult, op1=ALU.add))
            with dve.Fori(0, W) as v:
                link.loop(v, 4)
                link(nc.vector.tensor_scalar(mask[:, :], win[:, :], vid[0:R, bass.ds(v, 1)], None, ALU.is_equal))
                link(nc.vector.tensor_tensor_scan(count[:, :], K.ones_row[0:R, 0:T], mask[:, :], 0.0, ALU.mult, ALU.add))
                nc.vector.tensor_copy(tot[:, bass.ds(v, 1)], count[:, T - 1:T])
                link(nc.vector.tensor_tensor(term[:, :], mask[:, :], count[:, :], ALU.mult))
                link(nc.vector.tensor_tensor(rank[:, :], rank[:, :], term[:, :], ALU.add))
            link.end(W)
            nc.vector.tensor_copy(tot[:, W - 1:W], count[:, T - 1:T]).then_inc(tots, 1)
            dve.wait_ge(summed, 2)
            link(nc.vector.tensor_scalar(cnt_i[:, :], ps_cnt[:, 0:W], float(G - 1), None, ALU.add))
            link(nc.vector.tensor_scalar(cnt_i[:, :], cnt_i[:, :], 8, None, ALU.logical_shift_right))
            link(nc.vector.tensor_scalar(groups_f[:, :], cnt_i[:, :], 1.0, None, ALU.max))
            link(nc.vector.tensor_tensor_scan(end_f[:, :], K.ones_row[:, 0:W], groups_f[:, :], 0.0, ALU.mult, ALU.add))
            link(nc.vector.memset(K.bases[:, :], 0))
            link(nc.vector.tensor_copy(K.bases[:, 1:W + 1], end_f[:, :]))
            link(nc.vector.tensor_tensor(cnt_f[:, :], end_f[:, :], groups_f[:, :], ALU.subtract))
            link(nc.vector.tensor_scalar(cnt_f[:, :], cnt_f[:, :], float(G), -1.0, ALU.mult, ALU.add))
            link(nc.vector.tensor_tensor(off[:, :], cnt_f[0:R, :], ps_before[0:R, 0:W], ALU.add))
            with dve.Fori(0, W) as v:
                link.loop(v, 2)
                link(nc.vector.tensor_scalar(term[:, :], win[:, :], vid[0:R, bass.ds(v, 1)], off[:, bass.ds(v, 1)],
                                             ALU.is_equal, ALU.mult))
                link(nc.vector.tensor_tensor(rank[:, :], rank[:, :], term[:, :], ALU.add))
            link.end(W)
            link(nc.vector.tensor_copy(K.slot_of[:, :], rank[:, :]))
            link(nc.vector.tensor_scalar(tile_i[:, :], K.slot_of[:, :], 7, None, ALU.logical_shift_right))
            link(nc.vector.tensor_scalar(lane_i[:, :], K.slot_of[:, :], 127, None, ALU.bitwise_and))
            link(nc.vector.tensor_copy(tile_f[:, :], tile_i[:, :]))
            link(nc.vector.tensor_copy(lane_f[:, :], lane_i[:, :]))
            link(nc.vector.scalar_tensor_tensor(out=K.meta_row_of[:, :], in0=lane_f[:, :], scalar=float(TILES),
                                                in1=tile_f[:, :], op0=ALU.mult, op1=ALU.add))
            nc.vector.tensor_copy(K.meta[:, :, 0:1], src_i[:, :].unsqueeze(2))
            nc.vector.tensor_copy(K.meta[:, :, 1:2].bitcast(F32), rel[:, :].unsqueeze(2))


def scatter_meta(nc, ctx, K, slot_meta):
    B = 8
    with Part(nc, "meta", ctx) as p:
        rows = [p.sb(f"rows{h}", [R, B], I32) for h in range(2)]
        vals = [p.sb(f"vals{h}", [R, B, 2], I32) for h in range(2)]
        staged = [p.sem(f"staged{h}") for h in range(2)]
        done = [p.sem(f"done{h}") for h in range(2)]
        begun = p.sem("begun")
        block = p.block()

        @block.vector
        def _(dve):
            with dve.Fori(0, T // (2 * B)) as i:
                for h in range(2):
                    dve.wait_ge(done[h], i * (16 * B))
                    nc.vector.tensor_copy(rows[h][:, :], K.meta_row_of[:, bass.ds(i * (2 * B) + h * B, B)]).then_inc(staged[h], 1)
                    nc.vector.tensor_copy(vals[h][:, :, :], K.meta[:, bass.ds(i * (2 * B) + h * B, B), :]).then_inc(staged[h], 1)

        @block.gpsimd
        def _(pool):
            with pool.Fori(0, T // (2 * B)) as i:
                for h in range(2):
                    pool.wait_ge(staged[h], i * 2 + 2)
                    pool.sem_inc(begun, 1)
                    for b in range(B):
                        pool.indirect_dma_start(slot_meta, bass.IndirectOffsetOnAxis(ap=rows[h][:, b:b + 1], axis=0),
                                                vals[h][:, b, :], None).then_inc(done[h], 16)
            for h in range(2):
                pool.wait_ge(done[h], 16 * T // 2)


class Kept:

    def __init__(self, nc, ctx):
        def sb(name, shape, dt=F32):
            return ctx.enter_context(nc.sbuf_tensor(name, shape, dt))

        self.ident, self.ident16 = sb("ident", [128, 128]), sb("ident16", [128, 128], BF16)
        self.below, self.ones = sb("below", [128, 128]), sb("ones", [128, 512])
        self.ones_row = self.ones
        self.iota_i, self.iota16 = sb("iota_i", [128, N], I32), sb("iota16", [128, N + 1], I16)
        self.iota_f = sb("iota_f", [128, 128])
        self.lane_i, self.lane_f = sb("lane_i", [128, 1], I32), sb("lane_f", [128, 1])
        self.bases = sb("bases", [128, W + 1], I32)
        self.slot_of, self.meta_row_of = sb("slot_of", [R, T], I32), sb("meta_row_of", [R, T], I32)
        self.meta = sb("meta", [R, T, 2], I32)
        self.sender, self.sender_f, self.rel = sb("sender", [128, TILES + 2], I32), sb("sender_f", [128, TILES]), sb("rel", [128, TILES])
        self.deg, self.dinv = sb("deg", [R, W, 2]), sb("dinv", [R, W])
        self.x, self.mean, self.rstd = sb("x", [R, W, D]), sb("mean", [R, W]), sb("rstd", [R, W])


def read_slots(nc, ctx, K, slot_meta, rel_rows, x_in):
    C = TILES // 4
    with Part(nc, "slots", ctx) as p:
        both = p.sb("both", [128, TILES, 2], I32)
        rows = p.sb("rows", [C, 4, 128])
        ps = p.ps("ps", [128, 4, 128])
        loaded, split, turned, copied, stored, xin = (p.sem(n) for n in ("loaded", "split", "turned", "copied", "stored", "xin"))
        block = p.block()

        @block.sync
        def _(sp):
            sp.dma_start(both[:, :, :].rearrange("p t c -> p (t c)"),
                         slot_meta.rearrange("(p t) c -> p (t c)", p=128)).then_inc(loaded, 16)
            sp.dma_start(K.x[:, :, :], x_in.rearrange("(w p) d -> p w d", p=R)).then_inc(xin, 16)
            sp.wait_ge(copied, 1)
            sp.dma_start(rel_rows.rearrange("(a t) l -> t a l", a=4), rows[:, :, :]).then_inc(stored, 16)
            sp.wait_ge(xin, 16)
            sp.wait_ge(stored, 16)

        @block.vector
        def _(dve):
            dve.wait_ge(loaded, 16)
            nc.vector.tensor_copy(K.rel[:, :], both[:, :, 1:2].rearrange("p t c -> p (t c)").bitcast(F32)).then_inc(split, 1)
            nc.vector.memset(K.sender[:, TILES:TILES + 2], 0)
            nc.vector.tensor_copy(K.sender[:, 0:TILES], both[:, :, 0:1].rearrange("p t c -> p (t c)"))
            nc.vector.tensor_copy(K.sender_f[:, :], both[:, :, 0:1].rearrange("p t c -> p (t c)"))
            dve.wait_ge(turned, 1)
            nc.vector.tensor_copy(rows[:, :, :], ps[0:C, :, :]).then_inc(copied, 1)

        @block.tensor
        def _(pe):
            pe.wait_ge(split, 1)
            for a in range(4):
                last = nc.tensor.transpose(ps[0:C, a, :], K.rel[:, a * C:(a + 1) * C], K.ident[:, :])
            last.then_inc(turned, 1)


def count_edges(nc, ctx, K, edge_attr, slot_raw, a_dram):
    B = 8
    NB = (N + CHUNK - 1) // CHUNK
    full = (NB - 1) * CHUNK
    with Part(nc, "count", ctx) as p:
        oh_s = [p.sb(f"oh_s{h}", [128, N + 1], BF16) for h in range(2)]
        oh_r = [p.sb(f"oh_r{h}", [128, R], BF16) for h in range(2)]
        zrow = p.sb("zrow", [1, CHUNK], BF16)
        a_sb = p.sb("a_sb", [R, N], BF16)
        raws = [p.sb(f"raws{h}", [R, B, D]) for h in range(2)]
        rows = [p.sb(f"rows{h}", [R, B], I32) for h in range(2)]
        ps = p.ps("ps", [128, NB, 512])
        zeroed, ready, used, counted, taken_a, taken_d, a_stored = (
            p.sem(n) for n in ("zeroed", "ready", "used", "counted", "taken_a", "taken_d", "a_stored"))
        rows_in = [p.sem(f"rows_in{h}") for h in range(2)]
        staged = [p.sem(f"staged{h}") for h in range(2)]
        scattered = [p.sem(f"scattered{h}") for h in range(2)]
        begun = p.sem("begun")
        block = p.block()
        attr = edge_attr.rearrange("(p t) d -> p t d", p=R)

        @block.vector
        def _(dve):
            nc.vector.memset(zrow[:, :], 0.0).then_inc(zeroed, 1)
            with dve.Fori(0, W) as w:
                lo = dve.value_load(K.bases[0:1, bass.ds(w, 1)], min_val=0, max_val=GROUPS)
                hi = dve.value_load(K.bases[0:1, bass.ds(w + 1, 1)], min_val=1, max_val=GROUPS)
                with dve.Fori(lo, hi) as s:
                    for h in range(2):
                        dve.wait_ge(used, s * 2 + h)
                        nc.vector.tensor_scalar(oh_r[h][:, :], K.iota_f[:, 0:R], K.rel[:, bass.ds(s * 2 + h, 1)], None, ALU.is_equal)
                        nc.vector.tensor_scalar(oh_s[h][:, :], K.iota16[:, :], K.sender_f[:, bass.ds(s * 2 + h, 1)], None,
                                                ALU.is_equal).then_inc(ready, 1)
                dve.wait_ge(counted, w + 1)
                dve.wait_ge(a_stored, w * 16)
                nc.vector.tensor_scalar(a_sb[:, full:N], ps[0:R, NB - 1, 0:N - full], 1.0, 0.0, ALU.mult, ALU.add,
                                        accum_out=K.deg[:, bass.ds(w, 1), 1]).then_inc(taken_d, 1)

        @block.tensor
        def _(pe):
            pe.sem_inc(used, 1)
            pe.wait_ge(zeroed, 1)
            with pe.Fori(0, W) as w:
                lo = pe.value_load(K.bases[0:1, bass.ds(w, 1)], min_val=0, max_val=GROUPS)
                hi = pe.value_load(K.bases[0:1, bass.ds(w + 1, 1)], min_val=1, max_val=GROUPS)
                pe.wait_ge(taken_a, w)
                pe.wait_ge(taken_d, w)
                for c in range(NB):
                    n = min(CHUNK, N - c * CHUNK)
                    nc.tensor.matmul(ps[0:R, c, 0:n], zrow[0:1, 0:R], zrow[0:1, 0:n], start=True, stop=False, skip_group_check=True)
                with pe.Fori(lo, hi) as s:
                    for h in range(2):
                        pe.wait_ge(ready, s * 2 + (h + 1))
                        for c in range(NB):
                            n = min(CHUNK, N - c * CHUNK)
                            last = nc.tensor.matmul(ps[0:R, c, 0:n], oh_r[h][:, :], oh_s[h][:, c * CHUNK:c * CHUNK + n],
                                                    start=False, stop=False, skip_group_check=True)
                        last.then_inc(used, 1)
                for c in range(NB):
                    last = nc.tensor.matmul(ps[0:R, c, 0:1], zrow[0:1, 0:R], zrow[0:1, 0:1], start=False, stop=True, skip_group_check=True)
                last.then_inc(counted, 1)

        @block.scalar
        def _(act):
            with act.Fori(0, W) as w:
                for h in range(2):
                    act.wait_ge(scattered[h], w * (16 * B))
                    nc.scalar.copy(rows[h][:, :], K.slot_of[:, bass.ds(w * (2 * B) + h * B, B)]).then_inc(staged[h], 1)
                act.wait_ge(counted, w + 1)
                act.wait_ge(a_stored, w * 16)
                nc.scalar.activation(a_sb[:, 0:full].rearrange("p (c n) -> p c n", n=CHUNK), ps[0:R, 0:NB - 1, 0:CHUNK], ACT.Copy,
                                     accum_out=K.deg[:, bass.ds(w, 1), 0]).then_inc(taken_a, 1)
                act.wait_ge(taken_a, w + 1)
                act.wait_ge(taken_d, w + 1)
                act.dma_start(a_dram[bass.ds(w, 1), :, :].rearrange("a p n -> p (a n)"), a_sb[:, :]).then_inc(a_stored, 16)
            act.wait_ge(a_stored, 16 * W)

        @block.sync
        def _(sp):
            with sp.Fori(0, T // (2 * B)) as i:
                for h in range(2):
                    sp.wait_ge(scattered[h], i * (16 * B))
                    sp.dma_start(raws[h][:, :, :], attr[:, bass.ds(i * (2 * B) + h * B, B), :]).then_inc(rows_in[h], 16)

        @block.gpsimd
        def _(pool):
            with pool.Fori(0, T // (2 * B)) as i:
                for h in range(2):
                    pool.wait_ge(rows_in[h], i * 16 + 16)
                    pool.sem_inc(begun, 1)
                    pool.wait_ge(staged[h], i + 1)
                    pool.sem_inc(begun, 1)
                    for b in range(B):
                        pool.indirect_dma_start(slot_raw, bass.IndirectOffsetOnAxis(ap=rows[h][:, b:b + 1], axis=0),
                                                raws[h][:, b, :], None).then_inc(scattered[h], 16)
            for h in range(2):
                pool.wait_ge(scattered[h], 16 * T // 2)


def encode_edges(nc, ctx, K, slot_raw, w_edge, b_edge, et_dram):
    B = 4
    with Part(nc, "encode", ctx) as p:
        wt, bias = p.sb("wt", [D, D]), p.sb("bias", [128, D])
        raw = [p.sb(f"raw{h}", [128, B, D]) for h in range(2)]
        raw_t = [p.sb(f"raw_t{h}", [128, B, D]) for h in range(2)]
        act_in = [p.sb(f"act_in{h}", [128, B, D]) for h in range(2)]
        act_out = [p.sb(f"act_out{h}", [128, B, D]) for h in range(2)]
        normed = [p.sb(f"normed{h}", [128, B, D]) for h in range(2)]
        et = [p.sb(f"et{h}", [128, B, D]) for h in range(2)]
        stats, mv = [p.sb(f"stats{h}", [128, B, 6]) for h in range(2)], [p.sb(f"mv{h}", [128, B, 2]) for h in range(2)]
        var = [p.sb(f"var{h}", [128, B]) for h in range(2)]
        rstd = [p.sb(f"rstd{h}", [128, B]) for h in range(2)]
        power = p.sb("power", [128, B])
        ps_in = [p.ps(f"ps_in{h}", [128, B, D]) for h in range(2)]
        ps_lin = [p.ps(f"ps_lin{h}", [128, B, D]) for h in range(2)]
        ps_out = [p.ps(f"ps_out{h}", [128, B, D]) for h in range(2)]
        consts, powered, turned, copied, lin, biased, gelued, moments, rooted, norm_done, back, out_ready, chain = (
            p.sem(n) for n in ("consts", "powered", "turned", "copied", "lin", "biased", "gelued", "moments",
                               "rooted", "norm_done", "back", "out_ready", "chain"))
        begun = p.sem("begun")
        raw_in = [p.sem(f"raw_in{h}") for h in range(2)]
        stored = [p.sem(f"stored{h}") for h in range(2)]
        block = p.block()
        slots = slot_raw.rearrange("(t l) d -> l t d", l=128)
        STEPS = TILES // (2 * B)

        @block.sync
        def _(sp):
            sp.dma_start(wt[:, :], w_edge).then_inc(consts, 16)
            sp.dma_start(bias[:, :], b_edge.partition_broadcast(128)).then_inc(consts, 16)
            with sp.Fori(0, STEPS) as i:
                for h in range(2):
                    sp.wait_ge(turned, i * 2 + h)
                    sp.dma_start(raw[h][:, :, :], slots[:, bass.ds(i * (2 * B) + h * B, B), :]).then_inc(raw_in[h], 16)

        @block.tensor
        def _(pe):
            pe.sem_inc(turned, 1)
            pe.sem_inc(back, 1)
            pe.sem_inc(lin, 1)
            pe.wait_ge(consts, 32)
            with pe.Fori(0, STEPS) as i:
                for h in range(2):
                    pe.wait_ge(raw_in[h], i * 16 + 16)
                    pe.wait_ge(copied, i * 2 + h)
                    for b in range(B):
                        last = nc.tensor.transpose(ps_in[h][:, b, :], raw[h][:, b, :], K.ident[:, :])
                    last.then_inc(turned, 1)
                for h in range(2):
                    pe.wait_ge(copied, i * 2 + (h + 2))
                    pe.wait_ge(biased, i * 2 + h)
                    for b in range(B):
                        last = nc.tensor.matmul(ps_lin[h][:, b, :], raw_t[h][:, b, :], wt[:, :], start=True, stop=True)
                    last.then_inc(lin, 1)
                for h in range(2):
                    pe.wait_ge(norm_done, i * 2 + (h + 2))
                    pe.wait_ge(out_ready, i * 2 + h)
                    for b in range(B):
                        last = nc.tensor.transpose(ps_out[h][:, b, :], normed[h][:, b, :], K.ident[:, :])
                    last.then_inc(back, 1)

        @block.scalar
        def _(act):
            act.sem_inc(copied, 1)
            act.sem_inc(gelued, 1)
            act.sem_inc(out_ready, 1)
            with act.Fori(0, STEPS) as i:
                for h in range(2):
                    act.wait_ge(turned, i * 2 + (h + 2))
                    act.wait_ge(lin, i * 2 + h)
                    nc.scalar.copy(raw_t[h][:, :, :], ps_in[h][:, :, :]).then_inc(copied, 1)
                for h in range(2):
                    act.wait_ge(biased, i * 2 + (h + 2))
                    nc.scalar.activation(act_out[h][:, :, :], act_in[h][:, :, :], ACT.Gelu_apprx_tanh).then_inc(gelued, 1)
                for h in range(2):
                    act.wait_ge(back, i * 2 + (h + 2))
                    act.wait_ge(stored[h], i * 16)
                    nc.scalar.copy(et[h][:, :, :], ps_out[h][:, :, :]).then_inc(out_ready, 1)
                    act.wait_ge(out_ready, i * 2 + (h + 2))
                    act.dma_start(et_dram[:, bass.ds(i * (2 * B * 128) + h * (B * 128), B * 128)],
                                  et[h][:, :, :].rearrange("p b l -> p (b l)")).then_inc(stored[h], 16)
            for h in range(2):
                act.wait_ge(stored[h], 16 * STEPS)

        @block.gpsimd
        def _(pool):
            nc.gpsimd.memset(power[:, :], -0.5).then_inc(powered, 1)
            pool.wait_ge(powered, 1)
            with pool.Fori(0, STEPS) as i:
                for h in range(2):
                    pool.wait_ge(moments, i * 2 + (h + 1))
                    nc.gpsimd.tensor_tensor(rstd[h][:, :], var[h][:, :], power[:, :], ALU.pow).then_inc(rooted, 1)

        @block.vector
        def _(dve):
            link = Chain(dve, chain)
            dve.sem_inc(biased, 1)
            dve.sem_inc(norm_done, 1)
            dve.wait_ge(consts, 32)
            with dve.Fori(0, STEPS) as i:
                link.loop(i, 4)
                for h in range(2):
                    dve.wait_ge(lin, i * 2 + (h + 2))
                    dve.wait_ge(gelued, i * 2 + h)
                    nc.vector.tensor_tensor(act_in[h][:, :, :], ps_lin[h][:, :, :],
                                            bias[:, :].unsqueeze(1).to_broadcast([128, B, D]), ALU.add).then_inc(biased, 1)
                for h in range(2):
                    dve.wait_ge(gelued, i * 2 + (h + 2))
                    for b in range(B):
                        last = nc.vector.bn_stats(stats[h][:, b, :], act_out[h][:, b, :])
                    link(last)
                    dve.sem_inc(begun, 1)
                    for b in range(B):
                        last = nc.vector.bn_aggr(mv[h][:, b, :], stats[h][:, b, :])
                    link(last)
                    nc.vector.tensor_scalar(var[h][:, :], mv[h][:, :, 1:2].rearrange("p b c -> p (b c)"), LN_EPS, None,
                                            ALU.add).then_inc(moments, 1)
                for h in range(2):
                    dve.wait_ge(rooted, i * 2 + (h + 1))
                    dve.wait_ge(back, i * 2 + h)
                    for b in range(B):
                        last = nc.vector.tensor_scalar(normed[h][:, b, :], act_out[h][:, b, :], mv[h][:, b, 0:1],
                                                       rstd[h][:, b:b + 1], ALU.subtract, ALU.mult)
                    last.then_inc(norm_done, 1)
            link.end(STEPS)


def norm_moments(nc, ctx, K, name, x):
    with Part(nc, name, ctx) as p:
        stats, half, var, tmp = p.sb("stats", [R, W, 6]), p.sb("half", [R, W]), p.sb("var", [R, W]), p.sb("tmp", [R, W])
        ready, rooted, chain = p.sem("ready"), p.sem("rooted"), p.sem("chain")
        block = p.block()

        def col(c):
            return stats[:, :, c:c + 1].rearrange("p w c -> p (w c)")

        @block.vector
        def _(dve):
            link = Chain(dve, chain)
            with dve.Fori(0, NC) as i:
                link.loop(i, 1)
                for u in range(U):
                    last = nc.vector.bn_stats(stats[:, bass.ds(i * U + u, 1), :].rearrange("p a c -> p (a c)"),
                                              x[:, bass.ds(i * U + u, 1), :].rearrange("p a d -> p (a d)"))
                link(last)
            link.end(NC)
            link(nc.vector.tensor_tensor(half[:, :], col(1), col(4), ALU.subtract))
            link(nc.vector.tensor_scalar(half[:, :], half[:, :], 0.5, None, ALU.mult))
            link(nc.vector.tensor_tensor(K.mean[:, :], col(4), half[:, :], ALU.add))
            link(nc.vector.tensor_tensor(half[:, :], half[:, :], half[:, :], ALU.mult))
            link(nc.vector.tensor_tensor(var[:, :], col(2), col(5), ALU.add))
            link(nc.vector.scalar_tensor_tensor(out=var[:, :], in0=var[:, :], scalar=1.0 / D, in1=half[:, :],
                                                op0=ALU.mult, op1=ALU.add))
            nc.vector.tensor_scalar(var[:, :], var[:, :], LN_EPS, None, ALU.add).then_inc(ready, 1)
            dve.wait_ge(rooted, 1)
            link(nc.vector.reciprocal(K.rstd[:, :], tmp[:, :]))

        @block.scalar
        def _(act):
            act.wait_ge(ready, 1)
            nc.scalar.activation(tmp[:, :], var[:, :], ACT.Sqrt).then_inc(rooted, 1)


def project(nc, ctx, K, name, x, weights, width, finish, norm=False, relu=False, loads=(), extra=None, extra_sb=None):
    def banks(n):
        return [range(a, min(a + n, U)) for a in range(0, U, n)]

    with Part(nc, name, ctx) as p:
        tiles = [p.sb(f"rows{u}", [R, D]) for u in range(U)]
        turned_sb = p.sb("turned", [D, U, 128])
        more = [p.sb(f"more{u}", [D, R]) for u in range(U)] if extra is not None else None
        per_t, per_o = 4, 512 // width
        ps_t = p.ps("ps_t", [128, len(banks(per_t)) * per_t, 128])
        ps_o = p.ps("ps_o", [128, len(banks(per_o)) * per_o, width])
        loaded, staged, turned, copied, product, done = (p.sem(n) for n in ("loaded", "staged", "turned", "copied", "product", "done"))
        link_sem = p.sem("link")
        work = finish(p)
        block = p.block()

        @block.sync
        def _(sp):
            for dst, src in loads:
                sp.dma_start(dst, src).then_inc(loaded, 16)
            if loads:
                sp.wait_ge(loaded, 16 * len(loads))

        @block.vector
        def _(dve):
            if loads:
                dve.wait_ge(loaded, 16 * len(loads))
            dve.sem_inc(done, U)
            with dve.Fori(0, NC) as i:
                for u in range(U):
                    w = i * U + u
                    dve.wait_ge(turned, w + 1)
                    row = x[:, bass.ds(w, 1), :].rearrange("p a d -> p (a d)")
                    if norm:
                        ins = nc.vector.tensor_scalar(tiles[u][:, :], row, K.mean[:, bass.ds(w, 1)], K.rstd[:, bass.ds(w, 1)],
                                                      ALU.subtract, ALU.mult)
                    else:
                        ins = nc.vector.tensor_copy(tiles[u][:, :], row)
                    if extra is not None:
                        ins = nc.vector.tensor_copy(more[u][:, :], extra_sb[:, bass.ds(w * R, R)])
                    ins.then_inc(staged, 1)
                for bank in banks(per_o):
                    dve.wait_ge(product, i * U + (bank[-1] + U + 1))
                    for u in bank:
                        work(nc, None, i * U + u, ps_o[0:R, u, :]).then_inc(done, 1)

        @block.tensor
        def _(pe):
            pe.sem_inc(turned, U)
            pe.sem_inc(product, U)
            if loads:
                pe.wait_ge(loaded, 16 * len(loads))
            with pe.Fori(0, NC) as i:
                for bank in banks(per_t):
                    pe.wait_ge(staged, i * U + (bank[-1] + 1))
                    for u in bank:
                        ins = nc.tensor.transpose(ps_t[:, u, 0:R], tiles[u][:, :], K.ident[0:R, 0:R])
                    ins.then_inc(turned, len(bank))
                for bank in banks(per_o):
                    pe.wait_ge(copied, i * U + (bank[-1] + 1))
                    pe.wait_ge(done, i * U + (bank[-1] + 1))
                    for u in bank:
                        ins = nc.tensor.matmul(ps_o[0:R, u, :], turned_sb[:, u, 0:R], weights, start=True, stop=extra is None)
                        if extra is not None:
                            ins = nc.tensor.matmul(ps_o[0:R, u, :], more[u][:, :], extra, start=False, stop=True)
                    ins.then_inc(product, len(bank))

        @block.scalar
        def _(act):
            with act.Fori(0, NC) as i:
                for bank in banks(per_t):
                    act.wait_ge(turned, i * U + (bank[-1] + U + 1))
                    act.wait_ge(product, i * U + (bank[-1] + 1))
                    b = slice(bank[0], bank[-1] + 1)
                    nc.scalar.activation(turned_sb[:, b, 0:R], ps_t[:, b, 0:R], ACT.Relu if relu else ACT.Copy).then_inc(copied, len(bank))


class Finish:

    def __init__(self, links, f):
        self.links, self.f = links, f

    def __call__(self, nc, link, w, product):
        return self.f(nc, link, w, product)


def at(t, w):
    return t[:, bass.ds(w, 1), :].rearrange("p a d -> p (a d)")


def spread(nc, ctx, K, name, g, bias, out, at_dram, a_dram=None, relu=False, residual=None):
    make = a_dram is not None
    with Part(nc, name, ctx) as p:
        parts = p.sb("parts", [R, W, 3, D], BF16)
        rest = p.sb("rest", [R, W, D])
        at_sb = [p.sb(f"at{u}", [R, W, R], BF16) for u in range(2)]
        a_sb = [p.sb(f"a{u}", [R, N], BF16) for u in range(2)] if make else None
        total = p.sb("total", [R, D])
        bias_sb = p.sb("bias", [128, D])
        ps = [p.ps(f"ps{u}", [128, 512]) for u in range(2)]
        ps_t = [p.ps(f"ps_t{u}", [128, 8, 128], BF16) for u in range(4)] if make else None
        biased, split, product, done, chain, turned, copied = (
            p.sem(n) for n in ("biased", "split", "product", "done", "chain", "turned", "copied"))
        a_in = [p.sem(f"a_in{u}") for u in range(2)]
        at_out = [p.sem(f"at_out{u}") for u in range(2)]
        block = p.block()
        ROUNDS = [(r, min(8, W - 8 * r)) for r in range(4)]

        @block.vector
        def _(dve):
            link = Chain(dve, chain)
            link(nc.vector.tensor_copy(parts[:, :, 0, :], g[:, :, :]))
            link(nc.vector.tensor_tensor(rest[:, :, :], g[:, :, :], parts[:, :, 0, :], ALU.subtract))
            link(nc.vector.tensor_copy(parts[:, :, 1, :], rest[:, :, :]))
            link(nc.vector.tensor_tensor(rest[:, :, :], rest[:, :, :], parts[:, :, 1, :], ALU.subtract))
            nc.vector.tensor_copy(parts[:, :, 2, :], rest[:, :, :]).then_inc(split, 1)
            dve.wait_ge(biased, 16)
            dve.sem_inc(done, 1)

            def window(w, u):
                dve.wait_ge(product, w + 2)
                link(nc.vector.tensor_reduce(total[:, :], ps[u][0:R, 0:3 * D].rearrange("p (c d) -> p d c", c=3), AX.X, ALU.add))
                link(nc.vector.tensor_tensor(total[:, :], total[:, :], at(g, w), ALU.add))
                ins = nc.vector.scalar_tensor_tensor(out=total[:, :] if relu or residual is not None else at(out, w),
                                                     in0=total[:, :], scalar=K.dinv[:, bass.ds(w, 1)],
                                                     in1=bias_sb[0:R, :], op0=ALU.mult, op1=ALU.add)
                if relu:
                    link(ins)
                    ins = nc.vector.tensor_scalar(at(out, w), total[:, :], 0.0, None, ALU.max)
                if residual is not None:
                    link(ins)
                    ins = nc.vector.tensor_tensor(at(out, w), total[:, :], at(residual, w), ALU.add)
                ins.then_inc(done, 1)
                dve.wait_ge(done, w + 2)

            links = 2 + bool(relu) + (residual is not None)
            with dve.Fori(0, W // 2) as i:
                link.loop(i, 2 * links)
                for u in range(2):
                    window(i * 2 + u, u)
            link.end(W // 2)
            window(W - 1, 0)

        @block.tensor
        def _(pe):
            def window(w, u, i):
                if make:
                    pe.wait_ge(a_in[u], i * 16 + 16)
                    for r, n in ROUNDS:
                        pe.wait_ge(copied, w * 4 + (r + 1))
                        for k in range(n):
                            c = 8 * r + k
                            ins = nc.tensor.transpose(ps_t[r][0:R, k, 0:R], a_sb[u][:, c * R:(c + 1) * R], K.ident16[0:R, 0:R])
                        ins.then_inc(turned, 1)
                    pe.wait_ge(copied, w * 4 + 8)
                else:
                    pe.wait_ge(a_in[u], i * 16 + 16)
                pe.wait_ge(done, w)
                for k in range(W):
                    ins = nc.tensor.matmul(ps[u][0:R, 0:3 * D], at_sb[u][:, k, :], parts[:, k, :, :].rearrange("p c d -> p (c d)"),
                                           start=(k == 0), stop=(k == W - 1))
                ins.then_inc(product, 1)

            pe.sem_inc(product, 1)
            pe.sem_inc(turned, 4)
            pe.wait_ge(split, 1)
            with pe.Fori(0, W // 2) as i:
                for u in range(2):
                    window(i * 2 + u, u, i)
            window(W - 1, 0, W // 2)

        @block.sync
        def _(sp):
            sp.dma_start(bias_sb[:, :], bias.partition_broadcast(128)).then_inc(biased, 16)

            def load(w, u, i):
                if make:
                    sp.wait_ge(turned, w * 4)
                    sp.dma_start(a_sb[u][:, :], a_dram[bass.ds(w, 1), :, :].rearrange("a p n -> p (a n)")).then_inc(a_in[u], 16)
                else:
                    sp.wait_ge(product, w)
                    sp.dma_start(at_sb[u][:, :, :].rearrange("p k r -> p (k r)"),
                                 at_dram[bass.ds(w, 1), :, :].rearrange("a p n -> p (a n)")).then_inc(a_in[u], 16)
            with sp.Fori(0, W // 2) as i:
                for u in range(2):
                    load(i * 2 + u, u, i)
            load(W - 1, 0, W // 2)

        if make:
            @block.scalar
            def _(act):
                act.sem_inc(copied, 4)

                def window(w, u, i):
                    act.wait_ge(product, w)
                    act.wait_ge(at_out[u], i * 16)
                    for r, n in ROUNDS:
                        act.wait_ge(turned, w * 4 + (r + 5))
                        nc.scalar.copy(at_sb[u][:, 8 * r:8 * r + n, :], ps_t[r][0:R, 0:n, 0:R]).then_inc(copied, 1)
                    act.wait_ge(copied, w * 4 + 8)
                    act.dma_start(at_dram[bass.ds(w, 1), :, :].rearrange("a p n -> p (a n)"),
                                  at_sb[u][:, :, :].rearrange("p k r -> p (k r)")).then_inc(at_out[u], 16)
                with act.Fori(0, W // 2) as i:
                    for u in range(2):
                        window(i * 2 + u, u, i)
                window(W - 1, 0, W // 2)
                act.wait_ge(at_out[0], 16 * (W // 2 + 1))
                act.wait_ge(at_out[1], 16 * (W // 2))


def sums_to_degrees(nc, ctx, K):
    with Part(nc, "degree", ctx) as p:
        deg, root = p.sb("deg", [R, W]), p.sb("root", [R, W])
        ready, rooted, chain = p.sem("ready"), p.sem("rooted"), p.sem("chain")
        block = p.block()

        @block.vector
        def _(dve):
            link = Chain(dve, chain)
            link(nc.vector.tensor_reduce(deg[:, :], K.deg[:, :, :], AX.X, ALU.add))
            nc.vector.tensor_scalar(deg[:, :], deg[:, :], 1.0, None, ALU.add).then_inc(ready, 1)
            dve.wait_ge(rooted, 1)
            link(nc.vector.reciprocal(K.dinv[:, :], root[:, :]))

        @block.scalar
        def _(act):
            act.wait_ge(ready, 1)
            nc.scalar.activation(root[:, :], deg[:, :], ACT.Sqrt).then_inc(rooted, 1)


def norm_apply(nc, ctx, K, name, x, out, scale=None, offset=None, relu=False, add_to=None, gelu_first=False):
    with Part(nc, name, ctx) as p:
        if scale is not None:
            scale_sb, offset_sb = p.sb("scale", [128, D]), p.sb("offset", [128, D])
        loaded, chain = p.sem("loaded"), p.sem("chain")
        block = p.block()

        @block.sync
        def _(sp):
            if scale is not None:
                sp.dma_start(scale_sb[:, :], scale.partition_broadcast(128)).then_inc(loaded, 16)
                sp.dma_start(offset_sb[:, :], offset.partition_broadcast(128)).then_inc(loaded, 16)
                sp.wait_ge(loaded, 32)

        @block.vector
        def _(dve):
            link = Chain(dve, chain)
            with dve.Fori(0, NC) as i:
                link.loop(i, 1)
                for u in range(U):
                    w = i * U + u
                    last = nc.vector.tensor_scalar(at(out, w), at(x, w), K.mean[:, bass.ds(w, 1)], K.rstd[:, bass.ds(w, 1)],
                                                   ALU.subtract, ALU.mult)
                link(last)
            link.end(NC)
            if relu:
                link(nc.vector.tensor_scalar(out[:, :, :], out[:, :, :], 0.0, None, ALU.max))
            if scale is not None:
                dve.wait_ge(loaded, 32)
                link(nc.vector.tensor_tensor(out[:, :, :], out[:, :, :], scale_sb[0:R, :].unsqueeze(1).to_broadcast([R, W, D]), ALU.mult))
                link(nc.vector.tensor_tensor(out[:, :, :], out[:, :, :], offset_sb[0:R, :].unsqueeze(1).to_broadcast([R, W, D]), ALU.add))
            if add_to is not None:
                link(nc.vector.tensor_tensor(add_to[:, :, :], add_to[:, :, :], out[:, :, :], ALU.add))


def gelu_nodes(nc, ctx, K, t):
    with Part(nc, "gelu", ctx) as p:
        done = p.sem("done")
        block = p.block()

        @block.scalar
        def _(act):
            nc.scalar.activation(t[:, :, :], t[:, :, :], ACT.Gelu_apprx_tanh).then_inc(done, 1)
            act.wait_ge(done, 1)


def message_weights(nc, ctx, K, name, M, w1, b1, w2, b2, e_scale, e_offset):
    with Part(nc, name, ctx) as p:
        raw = p.sb("raw", [D, H])
        sc, of = p.sb("sc", [D, 1]), p.sb("of", [D, 1])
        of_b = p.sb("of_b", [D, R])
        b1_sb = p.sb("b1", [128, H])
        ps = p.ps("ps", [128, 512])
        loaded, ready, done, chain = (p.sem(n) for n in ("loaded", "ready", "done", "chain"))
        block = p.block()
        loads = [(M.w_sr[:, 0:H], w1[0:D, :]), (M.w_sr[:, H:2 * H], w1[D:2 * D, :]), (raw[:, :], w1[2 * D:3 * D, :]),
                 (M.w2[:, :, :], w2.rearrange("(c k) n -> k c n", k=128)), (M.b2[:, :], b2.partition_broadcast(128)),
                 (b1_sb[:, :], b1.partition_broadcast(128)),
                 (sc[:, :], e_scale.rearrange("(p a) -> p a", a=1)), (of[:, :], e_offset.rearrange("(p a) -> p a", a=1))]

        @block.sync
        def _(sp):
            for dst, src in loads:
                sp.dma_start(dst, src).then_inc(loaded, 16)
            sp.wait_ge(loaded, 16 * len(loads))

        @block.vector
        def _(dve):
            link = Chain(dve, chain)
            dve.wait_ge(loaded, 16 * len(loads))
            link(nc.vector.tensor_scalar(M.w_e[:, :], raw[:, :], sc[:, 0:1], None, ALU.mult))
            nc.vector.tensor_scalar(of_b[:, :], K.ones[:, 0:R], of[:, 0:1], None, ALU.mult).then_inc(ready, 1)
            dve.wait_ge(done, 1)
            link(nc.vector.tensor_tensor(M.b_r[:, :], b1_sb[0:R, :], ps[0:R, 0:H], ALU.add))

        @block.tensor
        def _(pe):
            pe.wait_ge(loaded, 16 * len(loads))
            pe.wait_ge(ready, 1)
            nc.tensor.matmul(ps[0:R, 0:H], of_b[:, :], raw[:, :], start=True, stop=True).then_inc(done, 1)


def store_senders(nc, ctx, K, name, M, p_dram):
    with Part(nc, name, ctx) as p:
        stored = p.sem("stored")
        block = p.block()

        @block.sync
        def _(sp):
            sp.dma_start(p_dram.rearrange("(w p) d -> p w d", p=R), M.send[:, :, :]).then_inc(stored, 16)
            sp.wait_ge(stored, 16)


def messages(nc, ctx, K, name, M, p_dram, et_dram, rel_rows):
    with Part(nc, name, ctx) as p:
        et = [p.sb(f"et{h}", [D, 128]) for h in range(2)]
        rel_b = p.sb("rel_b", [R, 256])
        oh_t = p.sb("oh_t", [R, 256])
        oh = [p.sb(f"oh{h}", [128, R]) for h in range(2)]
        idx = [p.sb(f"idx{q}", [128, 2], I32) for q in range(2)]
        got = p.sb("got", [128, 4, H])
        hid = [p.sb(f"hid{h}", [128, H]) for h in range(2)]
        hid_t = [p.sb(f"hid_t{h}", [128, 2, 128]) for h in range(2)]
        msg_b, msg = p.sb("msg_b", [128, 2, D]), p.sb("msg", [128, 2, D])
        zrow = p.sb("zrow", [1, 128])
        ps1 = [p.ps(f"ps1_{h}", [128, 512]) for h in range(2)]
        ps_t = p.ps("ps_t", [128, 2, 4, 128])
        ps2 = p.ps("ps2", [128, 2, 512])
        ps_a = p.ps("ps_a", [128, 512])
        rel_in, oht_ready, oh_ready, added, biased, zeroed = (p.sem(n) for n in ("rel_in", "oht_ready", "oh_ready", "added", "biased", "zeroed"))
        first, turned, second, summed, closed = (p.sem(n) for n in ("first", "turned", "second", "summed", "closed"))
        relu1, relu2, agg_out, idx_ready, begun = (p.sem(n) for n in ("relu1", "relu2", "agg_out", "idx_ready", "begun"))
        et_in = [p.sem(f"et_in{h}") for h in range(2)]
        gathered = [[p.sem(f"gathered{q}{h}") for h in range(2)] for q in range(2)]
        block = p.block()

        def bounds(eng, w):
            return (eng.value_load(K.bases[0:1, bass.ds(w, 1)], min_val=0, max_val=GROUPS),
                    eng.value_load(K.bases[0:1, bass.ds(w + 1, 1)], min_val=1, max_val=GROUPS))

        @block.sync
        def _(sp):
            total = sp.value_load(K.bases[0:1, W:W + 1], min_val=1, max_val=GROUPS)
            rows = rel_rows.rearrange("(g t) l -> g (t l)", t=2)
            with sp.Fori(0, total) as s:
                sp.wait_ge(oht_ready, s)
                sp.dma_start(rel_b[:, :], rows[bass.ds(s, 1), :].to_broadcast([R, 256])).then_inc(rel_in, 16)
                for h in range(2):
                    sp.wait_ge(first, s * 2 + h)
                    sp.dma_start(et[h][:, :], et_dram[:, bass.ds(s * 256 + h * 128, 128)]).then_inc(et_in[h], 16)

        @block.gpsimd
        def _(pool):
            total = pool.value_load(K.bases[0:1, W:W + 1], min_val=1, max_val=GROUPS)
            with pool.Fori(0, total, 2) as s:
                for q in range(2):
                    for h in range(2):
                        pool.wait_ge(gathered[q][h], s * 8)
                    nc.gpsimd.tensor_copy(idx[q][:, :], K.sender[:, bass.ds(s * 2 + q * 2, 2)]).then_inc(idx_ready, 1)
                    pool.wait_ge(idx_ready, s + (q + 1))
                    pool.sem_inc(begun, 1)
                    for h in range(2):
                        pool.wait_ge(added, s * 2 + (2 * q + h))
                        pool.sem_inc(begun, 1)
                        pool.indirect_dma_start(got[:, 2 * q + h, :], None, p_dram,
                                                bass.IndirectOffsetOnAxis(ap=idx[q][:, h:h + 1], axis=0)).then_inc(gathered[q][h], 16)
            for q in range(2):
                for h in range(2):
                    pool.wait_ge(gathered[q][h], ((total + 1) >> 1) * 16)
            pool.sem_inc(begun, 1)

        @block.vector
        def _(dve):
            dve.sem_inc(added, 3)
            nc.vector.memset(zrow[:, :], 0.0).then_inc(zeroed, 1)
            with dve.Fori(0, W) as w:
                lo, hi = bounds(dve, w)
                with dve.Fori(lo, hi) as s:
                    dve.wait_ge(rel_in, s * 16 + 16)
                    dve.wait_ge(first, s * 2 + 1)
                    nc.vector.tensor_scalar(oh_t[:, :], rel_b[:, :], K.lane_f[0:R, 0:1], None, ALU.is_equal).then_inc(oht_ready, 1)
                    for h in range(2):
                        dve.wait_ge(summed, s * 2 + h)
                        nc.vector.tensor_scalar(oh[h][:, :], K.iota_f[:, 0:R], K.rel[:, bass.ds(s * 2 + h, 1)], None,
                                                ALU.is_equal).then_inc(oh_ready, 1)
                    for h in range(2):
                        dve.wait_ge(gathered[0][h], ((s + 2) >> 1) * 16)
                        dve.wait_ge(gathered[1][h], ((s + 1) >> 1) * 16)
                        dve.wait_ge(first, s * 2 + (h + 2))
                        dve.wait_ge(turned, s * 2 + h)
                        nc.vector.tensor_tensor(hid[h][:, :], ps1[h][:, 0:H], at(got, (s & 1) * 2 + h), ALU.add).then_inc(added, 1)
                    dve.wait_ge(second, s * 2 + 3)
                    dve.wait_ge(relu2, s)
                    nc.vector.tensor_tensor(msg_b[:, :, :], ps2[:, :, 0:D], M.b2[:, :].unsqueeze(1).to_broadcast([128, 2, D]),
                                            ALU.add).then_inc(biased, 1)

        @block.tensor
        def _(pe):
            for sem in (first, turned, second, summed):
                pe.sem_inc(sem, 1)
            pe.wait_ge(zeroed, 1)
            with pe.Fori(0, W) as w:
                lo, hi = bounds(pe, w)
                pe.wait_ge(agg_out, w)
                nc.tensor.matmul(ps_a[:, 0:R], zrow[0:1, :], zrow[0:1, 0:R], start=True, stop=False, skip_group_check=True)
                with pe.Fori(lo, hi) as s:
                    for h in range(2):
                        pe.wait_ge(et_in[h], s * 16 + 16)
                        pe.wait_ge(oht_ready, s + 1)
                        pe.wait_ge(added, s * 2 + (h + 2))
                        nc.tensor.matmul(ps1[h][:, 0:H], et[h][:, :], M.w_e[:, :], start=True, stop=False)
                        nc.tensor.matmul(ps1[h][:, 0:H], oh_t[:, h * 128:(h + 1) * 128], at(M.recv, w), start=False, stop=True).then_inc(first, 1)
                    for h in range(2):
                        pe.wait_ge(added, s * 2 + (h + 4))
                        pe.wait_ge(relu1, s * 2 + h)
                        for c in range(2):
                            ins = nc.tensor.transpose(ps_t[:, h, c, :], hid[h][:, c * 128:(c + 1) * 128], K.ident[:, :])
                        ins.then_inc(turned, 1)
                    for h in range(2):
                        pe.wait_ge(relu1, s * 2 + (h + 2))
                        pe.wait_ge(biased, s)
                        for c in range(2):
                            ins = nc.tensor.matmul(ps2[:, h, 0:D], hid_t[h][:, c, :], M.w2[:, c, :], start=(c == 0), stop=(c == 1))
                        ins.then_inc(second, 1)
                    for h in range(2):
                        pe.wait_ge(relu2, s + 1)
                        pe.wait_ge(oh_ready, s * 2 + (h + 1))
                        nc.tensor.matmul(ps_a[:, 0:R], msg[:, h, :], oh[h][:, :], start=False, stop=False,
                                         skip_group_check=True).then_inc(summed, 1)
                nc.tensor.matmul(ps_a[:, 0:1], zrow[0:1, :], zrow[0:1, 0:1], start=False, stop=True, skip_group_check=True).then_inc(closed, 1)

        @block.scalar
        def _(act):
            act.sem_inc(relu1, 1)
            with act.Fori(0, W) as w:
                lo, hi = bounds(act, w)
                with act.Fori(lo, hi) as s:
                    for h in range(2):
                        act.wait_ge(turned, s * 2 + (h + 2))
                        act.wait_ge(second, s * 2 + h)
                        nc.scalar.activation(hid_t[h][:, :, :], ps_t[:, h, 0:2, :], ACT.Relu).then_inc(relu1, 1)
                    act.wait_ge(biased, s + 1)
                    act.wait_ge(summed, s * 2 + 1)
                    nc.scalar.activation(msg[:, :, :], msg_b[:, :, :], ACT.Relu).then_inc(relu2, 1)
                act.wait_ge(closed, w + 1)
                nc.scalar.copy(M.agg[:, bass.ds(w * R, R)], ps_a[:, 0:R]).then_inc(agg_out, 1)


def attend(nc, ctx, K, h, w_row, a_dram, s_dram):
    NB = (N + CHUNK - 1) // CHUNK
    with Part(nc, "attend", ctx) as p:
        w_sb = p.sb("w", [128, D])
        prod = p.sb("prod", [R, W, D])
        s_col, s_turned = p.sb("s_col", [R, W]), p.sb("s_turned", [W, R])
        low = p.sb("low", [R, 1])
        srel = p.sb("srel", [R, N])
        a_sb = [p.sb(f"a{u}", [R, N], BF16) for u in range(2)]
        member = p.sb("member", [R, N], BF16)
        masked = [p.sb(f"masked{u}", [R, N]) for u in range(2)]
        wt_t = p.sb("wt_t", [R, W, R])
        top, ntop, den, rden = ([p.sb(f"{n}{u}", [R, 1]) for u in range(2)] for n in ("top", "ntop", "den", "rden"))
        total = p.sb("total", [R, D])
        ps_s = p.ps("ps_s", [128, 512])
        ps_t = p.ps("ps_t", [128, 4, 512])
        ps_o = [p.ps(f"ps_o{u}", [128, 512]) for u in range(2)]
        w_in, scored, s_ready, s_out, s_stored, s_in, chain = (p.sem(n) for n in ("w_in", "scored", "s_ready", "s_out", "s_stored", "s_in", "chain"))
        topped, exped, weighted, turned, copied, product, done = (
            p.sem(n) for n in ("topped", "exped", "weighted", "turned", "copied", "product", "done"))
        a_in = [p.sem(f"a_in{u}") for u in range(2)]
        begun = p.sem("begun")
        block = p.block()
        GROUPS_K = [(g, min(4, W - 4 * g)) for g in range(NB)]

        def windows(eng, f):
            with eng.Fori(0, W // 2) as i:
                for u in range(2):
                    f(i * 2 + u, u, i)
            f(W - 1, 0, W // 2)

        @block.sync
        def _(sp):
            sp.dma_start(w_sb[:, :], w_row.to_broadcast([128, D])).then_inc(w_in, 16)
            sp.wait_ge(s_out, 1)
            sp.dma_start(s_dram.rearrange("(w p) -> w p", p=R), s_turned[:, :]).then_inc(s_stored, 16)
            sp.wait_ge(s_stored, 16)
            sp.dma_start(srel[:, :], s_dram.partition_broadcast(R)).then_inc(s_in, 16)

            def load(w, u, i):
                sp.wait_ge(weighted, w)
                sp.dma_start(a_sb[u][:, :], a_dram[bass.ds(w, 1), :, :].rearrange("a p n -> p (a n)")).then_inc(a_in[u], 16)
            windows(sp, load)

        @block.vector
        def _(dve):
            link = Chain(dve, chain)
            dve.wait_ge(w_in, 16)
            link(nc.vector.tensor_tensor(prod[:, :, :], h[:, :, :], w_sb[0:R, :].unsqueeze(1).to_broadcast([R, W, D]), ALU.mult))
            nc.vector.tensor_reduce(s_col[:, :], prod[:, :, :], AX.X, ALU.add).then_inc(scored, 1)
            dve.wait_ge(s_ready, 1)
            nc.vector.tensor_copy(s_turned[:, :], ps_s[0:W, 0:R]).then_inc(s_out, 1)
            dve.wait_ge(s_in, 16)
            link(nc.vector.tensor_reduce(low[:, :], srel[:, :], AX.X, ALU.min))
            link(nc.vector.tensor_scalar(srel[:, :], srel[:, :], low[:, 0:1], None, ALU.subtract))
            dve.sem_inc(weighted, 1)
            dve.sem_inc(done, 1)

            def window(w, u, i):
                dve.wait_ge(a_in[u], i * 16 + 16)
                link(nc.vector.tensor_scalar(member[:, :], a_sb[u][:, :], 1.0, None, ALU.min))
                dve.wait_ge(turned, w * NB)
                dve.sem_inc(begun, 1)
                link(nc.vector.tensor_tensor_reduce(out=masked[u][:, :], in0=member[:, :], in1=srel[:, :], scale=1.0, scalar=0.0,
                                                    op0=ALU.mult, op1=ALU.max, accum_out=top[u][:, 0:1]))
                nc.vector.tensor_scalar(ntop[u][:, :], top[u][:, :], -1.0, None, ALU.mult).then_inc(topped, 1)
                dve.wait_ge(exped, w + 1)
                ins = nc.vector.tensor_tensor_reduce(out=masked[u][:, :], in0=masked[u][:, :], in1=a_sb[u][:, :], scale=1.0, scalar=0.0,
                                                     op0=ALU.mult, op1=ALU.add, accum_out=den[u][:, 0:1])
                ins.then_inc(weighted, 1)
                dve.wait_ge(weighted, w + 2)
                link(nc.vector.tensor_scalar(den[u][:, :], den[u][:, :], 1e-20, None, ALU.max))
                link(nc.vector.reciprocal(rden[u][:, :], den[u][:, :]))
                dve.wait_ge(product, w + 1)
                nc.vector.scalar_tensor_tensor(out=at(K.x, w), in0=ps_o[u][0:R, 0:D], scalar=rden[u][:, 0:1], in1=at(K.x, w),
                                               op0=ALU.mult, op1=ALU.add).then_inc(done, 1)

            with dve.Fori(0, W // 2) as i:
                link.loop(i, 2 * 4)
                for u in range(2):
                    window(i * 2 + u, u, i)
            link.end(W // 2)
            window(W - 1, 0, W // 2)

        @block.scalar
        def _(act):
            act.sem_inc(copied, NB)

            def window(w, u, i):
                act.wait_ge(topped, w + 1)
                nc.scalar.activation(masked[u][:, :], masked[u][:, :], ACT.Exp, bias=ntop[u][:, 0:1]).then_inc(exped, 1)
                act.wait_ge(product, w)
                for g, n in GROUPS_K:
                    act.wait_ge(turned, w * NB + (NB + g + 1))
                    nc.scalar.copy(wt_t[:, 4 * g:4 * g + n, :], ps_t[0:R, g % 4, 0:n * R].rearrange("p (k r) -> p k r", r=R)).then_inc(copied, 1)
            windows(act, window)

        @block.tensor
        def _(pe):
            pe.wait_ge(scored, 1)
            nc.tensor.transpose(ps_s[0:W, 0:R], s_col[:, :], K.ident[0:R, 0:R]).then_inc(s_ready, 1)
            pe.sem_inc(turned, NB)

            def window(w, u, i):
                pe.wait_ge(weighted, w + 2)
                for g, n in GROUPS_K:
                    pe.wait_ge(copied, w * NB + (NB + g - 3))
                    for k in range(n):
                        c = 4 * g + k
                        ins = nc.tensor.transpose(ps_t[0:R, g % 4, k * R:(k + 1) * R], masked[u][:, c * R:(c + 1) * R], K.ident[0:R, 0:R])
                    ins.then_inc(turned, 1)
                pe.wait_ge(copied, w * NB + 2 * NB)
                pe.wait_ge(done, w)
                for k in range(W):
                    ins = nc.tensor.matmul(ps_o[u][0:R, 0:D], wt_t[:, k, :], h[:, k, :], start=(k == 0), stop=(k == W - 1))
                ins.then_inc(product, 1)
            windows(pe, window)


class Layer:

    def __init__(self, p):
        self.w_sr, self.w_e, self.w2 = p.sb("w_sr", [D, 2 * H]), p.sb("w_e", [D, H]), p.sb("w2", [128, 2, D])
        self.b2, self.b_r = p.sb("b2", [128, D]), p.sb("b_r", [R, H])
        self.send, self.recv = p.sb("send", [R, W, H]), p.sb("recv", [R, W, H])
        self.agg = p.sb("agg", [D, N])


def scaled_by_dinv(K, g):
    return lambda p: Finish(0, lambda nc, link, w, product: nc.vector.tensor_scalar(
        at(g, w), product, K.dinv[:, bass.ds(w, 1)], None, ALU.mult))


def plus_row(out, row):
    return lambda p: Finish(0, lambda nc, link, w, product: nc.vector.tensor_tensor(at(out, w), product, row[0:R, :], ALU.add))


def into_tables(M):
    def f(nc, link, w, product):
        nc.vector.tensor_copy(at(M.send, w), product[:, 0:H])
        return nc.vector.tensor_tensor(at(M.recv, w), product[:, H:2 * H], M.b_r[:, :], ALU.add)
    return lambda p: Finish(0, f)


def turn_weights(nc, ctx, K, name, w, out):
    with Part(nc, name, ctx) as p:
        raw, ps = p.sb("raw", [D, D]), p.ps("ps", [128, 512])
        loaded, turned, copied = p.sem("loaded"), p.sem("turned"), p.sem("copied")
        block = p.block()

        @block.sync
        def _(sp):
            sp.dma_start(raw[:, :], w).then_inc(loaded, 16)

        @block.tensor
        def _(pe):
            pe.wait_ge(loaded, 16)
            nc.tensor.transpose(ps[:, 0:D], raw[:, :], K.ident[:, :]).then_inc(turned, 1)

        @block.vector
        def _(dve):
            dve.wait_ge(turned, 1)
            nc.vector.tensor_copy(out[:, :], ps[:, 0:D]).then_inc(copied, 1)
            dve.wait_ge(copied, 1)


def store_result(nc, ctx, K, out):
    with Part(nc, "result", ctx) as p:
        stored = p.sem("stored")
        block = p.block()

        @block.sync
        def _(sp):
            sp.dma_start(out.rearrange("(w p) d -> p w d", p=R), K.x[:, :, :]).then_inc(stored, 16)
            sp.wait_ge(stored, 16)


def gcn(nc, ctx, K, name, at_dram, w1, b1, w2, b2, a_dram=None, turn=False):
    with Part(nc, name, ctx) as p:
        w_sb, g, hid = p.sb("w", [D, D]), p.sb("g", [R, W, D]), p.sb("hid", [R, W, D])
        norm_moments(nc, ctx, K, name + "_norm", K.x)
        for n, (w, b) in enumerate(((w1, b1), (w2, b2))):
            if turn:
                turn_weights(nc, ctx, K, f"{name}_turn{n}", w, w_sb)
            project(nc, ctx, K, f"{name}_lin{n}", hid if n else K.x, w_sb[:, :], D, scaled_by_dinv(K, g),
                    norm=not n, relu=not n, loads=() if turn else ((w_sb[:, :], w),))
            spread(nc, ctx, K, f"{name}_spread{n}", g, b, K.x if n else hid, at_dram, a_dram=None if n else a_dram,
                   relu=not n, residual=K.x if n else None)


def bass_graph_layers(nc, io, out):
    slot_meta = nc.dram_tensor("slot_meta", (SLOTS, 2), I32, kind="Internal").ap()
    slot_raw = nc.dram_tensor("slot_raw", (SLOTS, D), F32, kind="Internal").ap()
    rel_rows = nc.dram_tensor("rel_rows", (TILES, 128), F32, kind="Internal").ap()
    a_dram = nc.dram_tensor("a_rows", (W, R, N), BF16, kind="Internal").ap()
    at_dram = nc.dram_tensor("a_cols", (W, R, N), BF16, kind="Internal").ap()
    et_dram = nc.dram_tensor("edges_t", (D, SLOTS), F32, kind="Internal").ap()
    p_dram = nc.dram_tensor("send_rows", (N, H), F32, kind="Internal").ap()
    s_dram = nc.dram_tensor("scores", (N,), F32, kind="Internal").ap()
    with ExitStack() as kept:
        K = Kept(nc, kept)
        with Scope(nc) as ctx:
            build_constants(nc, ctx, K)
            sort_edges(nc, ctx, K, io["src"], io["dst"], slot_meta, slot_raw)
            scatter_meta(nc, ctx, K, slot_meta)
            read_slots(nc, ctx, K, slot_meta, rel_rows, io["x"])
            count_edges(nc, ctx, K, io["edge_attr_128"], slot_raw, a_dram)
            sums_to_degrees(nc, ctx, K)
        with Scope(nc) as ctx:
            gcn(nc, ctx, K, "l0", at_dram, io["L0_gnn_W1"], io["L0_gnn_b1"], io["L0_gnn_W2"], io["L0_gnn_b2"], a_dram=a_dram)
        with Scope(nc) as ctx:
            encode_edges(nc, ctx, K, slot_raw, io["L1_gnn_w_edge"], io["L1_gnn_b_edge"], et_dram)
        with Part(nc, "l1", None) as p:
            M = Layer(p)
            n_sb, t_sb = p.sb("n", [R, W, D]), p.sb("t", [R, W, D])
            w_sb, w2_sb, b_sb = p.sb("w", [D, D]), p.sb("w_upd", [D, D]), p.sb("b", [128, D])
            with Scope(nc) as ctx:
                norm_moments(nc, ctx, K, "l1_norm", K.x)
                project(nc, ctx, K, "l1_node", K.x, w_sb[:, :], D, plus_row(t_sb, b_sb), norm=True, relu=True,
                        loads=((w_sb[:, :], io["L1_gnn_w_node"]), (b_sb[:, :], io["L1_gnn_b_node"].partition_broadcast(128))))
                gelu_nodes(nc, ctx, K, t_sb)
                norm_moments(nc, ctx, K, "l1_norm_n", t_sb)
                norm_apply(nc, ctx, K, "l1_apply", t_sb, n_sb, scale=io["L1_gnn_ln_n_scale"], offset=io["L1_gnn_ln_n_offset"])
            for l in range(3):
                with Scope(nc) as ctx:
                    message_weights(nc, ctx, K, f"l1_w{l}", M, io["L1_gnn_msg_w1"][l], io["L1_gnn_msg_b1"][l], io["L1_gnn_msg_w2"][l],
                                    io["L1_gnn_msg_b2"][l], io["L1_gnn_ln_e_scale"], io["L1_gnn_ln_e_offset"])
                    project(nc, ctx, K, f"l1_tables{l}", n_sb, M.w_sr[:, :], 2 * H, into_tables(M))
                    store_senders(nc, ctx, K, f"l1_send{l}", M, p_dram)
                    messages(nc, ctx, K, f"l1_msg{l}", M, p_dram, et_dram, rel_rows)
                    upd = io["L1_gnn_upd_w"][l]
                    project(nc, ctx, K, f"l1_upd{l}", n_sb, w_sb[:, :], D, plus_row(t_sb, b_sb), extra=w2_sb[:, :], extra_sb=M.agg,
                            loads=((w_sb[:, :], upd[0:D, :]), (w2_sb[:, :], upd[D:2 * D, :]),
                                   (b_sb[:, :], io["L1_gnn_upd_b"][l].partition_broadcast(128))))
                    norm_moments(nc, ctx, K, f"l1_norm{l}", t_sb)
                    norm_apply(nc, ctx, K, f"l1_add{l}", t_sb, t_sb, scale=io["L1_gnn_ln_scale"][l], offset=io["L1_gnn_ln_offset"][l],
                               add_to=n_sb)
            with Scope(nc) as ctx:
                add_nodes(nc, ctx, K, n_sb)
        with Scope(nc) as ctx, Part(nc, "l2", None) as p:
            h_sb = p.sb("h", [R, W, D])
            norm_moments(nc, ctx, K, "l2_norm", K.x)
            norm_apply(nc, ctx, K, "l2_apply", K.x, h_sb, relu=True)
            attend(nc, ctx, K, h_sb, io["L2_gnn_W"], a_dram, s_dram)
        with Scope(nc) as ctx:
            gcn(nc, ctx, K, "l3", at_dram, io["L3_gnn_W1"], io["L3_gnn_b1"], io["L3_gnn_W2"], io["L3_gnn_b2"], turn=True)
            store_result(nc, ctx, K, out)


def add_nodes(nc, ctx, K, n_sb):
    with Part(nc, "l1_out", ctx) as p:
        done = p.sem("done")
        block = p.block()

        @block.vector
        def _(dve):
            nc.vector.tensor_tensor(K.x[:, :, :], K.x[:, :, :], n_sb[:, :, :], ALU.add).then_inc(done, 1)
            dve.wait_ge(done, 1)


_INS = ["x", "src", "dst", "edge_attr_128", "L0_gnn_W1", "L0_gnn_b1", "L0_gnn_W2", "L0_gnn_b2",
        "L1_gnn_w_node", "L1_gnn_b_node", "L1_gnn_w_edge", "L1_gnn_b_edge", "L1_gnn_ln_n_scale", "L1_gnn_ln_n_offset",
        "L1_gnn_ln_e_scale", "L1_gnn_ln_e_offset", "L1_gnn_msg_w1", "L1_gnn_msg_b1", "L1_gnn_msg_w2", "L1_gnn_msg_b2",
        "L1_gnn_upd_w", "L1_gnn_upd_b", "L1_gnn_ln_scale", "L1_gnn_ln_offset", "L2_gnn_W",
        "L3_gnn_W1", "L3_gnn_b1", "L3_gnn_W2", "L3_gnn_b2"]


def kernel(**inputs):
    import numpy as np
    import concourse.bacc as bacc
    from concourse.bass_utils import run_bass_kernel_spmd

    nc = bacc.Bacc("TRN2", target_bir_lowering=False, num_devices=1)
    arrays, io = {}, {}
    for name in _INS:
        a = np.ascontiguousarray(inputs[name])
        arrays[f"in_{name}"] = a
        io[name] = nc.dram_tensor(f"in_{name}", a.shape, mybir.dt.from_np(a.dtype), kind="ExternalInput").ap()
    out = nc.dram_tensor("out_0", (N, D), F32, kind="ExternalOutput").ap()
    bass_graph_layers(nc, io, out)
    r = run_bass_kernel_spmd(nc, [arrays], core_ids=[0])
    return r.results[0]["out_0"]
```

```python
from contextlib import ExitStack

import concourse.bass as bass
from concourse import mybir

F32 = mybir.dt.float32
I32 = mybir.dt.int32
I16 = mybir.dt.int16
F32R = mybir.dt.float32r
BF16 = mybir.dt.bfloat16
ALU = mybir.AluOpType
ACT = mybir.ActivationFunctionType
AX = mybir.AxisListType

N, E, D = 3125, 50000, 128
R = 125
W = N // R
T = E // R
G = 256
MAX_GROUPS = E // G + W
GROUPS = -(-(MAX_GROUPS + 8) // 4) * 4
TILES = 2 * GROUPS
SLOTS = G * GROUPS
ZERO_COLS = SLOTS // 12
assert SLOTS % (12 * 128) == 0 and D == 128
H = 2 * D
LN_EPS = 1e-5
CHUNK = 500
U = 5
NC = W // U


class Index:

    def __init__(self, x, scale=1, offset=0):
        self.x, self.scale, self.offset = x, scale, offset

    def __add__(self, n):
        return Index(self.x, self.scale, self.offset + n)

    def __sub__(self, n):
        return self + -n

    def __mul__(self, n):
        return Index(self.x, self.scale * n, self.offset * n)

    @property
    def value(self):
        if self.x is None:
            return self.offset
        v = self.x if self.scale == 1 else self.x * self.scale
        return v + self.offset if self.offset else v


ZERO = Index(None)


def at_least(eng, sem, index):
    if index.x is not None or index.offset > 0:
        eng.wait_ge(sem, index.value)


class Chain:

    def __init__(self, eng, sem):
        self.eng, self.sem, self.n, self.i, self.per, self.k = eng, sem, 0, None, 0, 0

    def loop(self, i, per):
        self.i, self.per, self.k = i, per, 0

    def end(self, trips):
        assert self.k == self.per, (self.k, self.per)
        self.n += self.per * trips
        self.i = None

    def __call__(self, ins):
        ins.then_inc(self.sem, 1)
        if self.i is None:
            self.n += 1
            self.eng.wait_ge(self.sem, self.n)
        else:
            self.k += 1
            self.eng.wait_ge(self.sem, self.i * self.per + (self.n + self.k))


class Scope:

    def __init__(self, nc):
        self.nc, self.sems = nc, []

    def __enter__(self):
        return self

    def semaphore(self, name):
        self.sems.append(self.nc.alloc_semaphore(name=name))
        return self.sems[-1]

    def __exit__(self, *_):
        self.nc.clear_and_free_semaphores(self.sems)
        self.nc.all_engine_barrier()


class Part:

    def __init__(self, nc, name, ctx):
        self.nc, self.name, self.ctx, self.own = nc, name, ctx, ExitStack()

    def __enter__(self):
        return self

    def __exit__(self, *_):
        self.own.close()

    def sb(self, name, shape, dt=F32):
        return self.own.enter_context(self.nc.sbuf_tensor(f"{self.name}_{name}", shape, dt))

    def ps(self, name, shape, dt=F32):
        return self.own.enter_context(self.nc.psum_tensor(f"{self.name}_{name}", shape, dt))

    def sem(self, name):
        return self.ctx.semaphore(f"{self.name}_{name}")

    def block(self):
        return self.own.enter_context(self.nc.Block())


def wide(ap, n):
    return ap.unsqueeze(2).to_broadcast([ap.shape[0], ap.shape[1], n])


def build_constants(nc, ctx, K):
    with Part(nc, "const", ctx) as p:
        made, link_p, link_v = p.sem("made"), p.sem("link_p"), p.sem("link_v")
        block = p.block()

        @block.gpsimd
        def _(pool):
            link = Chain(pool, link_p)
            link(nc.gpsimd.memset(K.ident[:, :], 0.0))
            link(nc.gpsimd.affine_select(out=K.ident[:, :], in_=K.ident[:, :], compare_op=ALU.not_equal,
                                         fill=1.0, base=0, pattern=[[-1, 128]], channel_multiplier=1))
            link(nc.gpsimd.memset(K.below[:, :], 1.0))
            link(nc.gpsimd.affine_select(out=K.below[:, :], in_=K.below[:, :], compare_op=ALU.is_gt,
                                         fill=0.0, base=0, pattern=[[1, 128]], channel_multiplier=-1))
            nc.gpsimd.iota(K.iota_i[:, :], pattern=[[1, N]], base=0, channel_multiplier=0).then_inc(made, 1)
            nc.gpsimd.iota(K.lane_i[:, :], pattern=[[0, 1]], base=0, channel_multiplier=1).then_inc(made, 1)

        @block.vector
        def _(dve):
            nc.vector.memset(K.ones[:, :], 1.0)
            nc.vector.memset(K.iota16[:, N:N + 1], -7)
            dve.wait_ge(made, 2)
            nc.vector.tensor_copy(K.iota16[:, 0:N], K.iota_i[:, :])
            nc.vector.tensor_copy(K.iota_f[:, :], K.iota_i[:, 0:128])
            nc.vector.tensor_copy(K.lane_f[:, :], K.lane_i[:, :])
            dve.wait_ge(link_p, 4)
            nc.vector.tensor_copy(K.ident16[:, :], K.ident[:, :])


def sort_edges(nc, ctx, K, src, dst, slot_meta, slot_raw):
    with Part(nc, "sort", ctx) as p:
        dst_i, src_i = p.sb("dst_i", [R, T], I32), p.sb("src_i", [R, T], I32)
        dst_f, quot_i = p.sb("dst_f", [R, T]), p.sb("quot_i", [R, T], I32)
        win, rel, low, high = (p.sb(n, [R, T]) for n in ("win", "rel", "low", "high"))
        mask, count, rank, term = (p.sb(n, [R, T]) for n in ("mask", "count", "rank", "term"))
        tot = p.sb("tot", [R, W])
        vid = p.sb("vid", [128, W])
        cnt_f, cnt_i, end_f = p.sb("cnt_f", [128, W]), p.sb("cnt_i", [128, W], I32), p.sb("end_f", [128, W])
        groups_f = p.sb("groups_f", [128, W])
        off = p.sb("off", [R, W])
        slot_i, tile_i, lane_i = (p.sb(n, [R, T], I32) for n in ("slot_i", "tile_i", "lane_i"))
        tile_f, lane_f = p.sb("tile_f", [R, T]), p.sb("lane_f", [R, T])
        zeros = p.sb("zeros", [128, ZERO_COLS])
        pad = p.sb("pad", [128, TILES, 2], I32)
        ps_before, ps_cnt = p.ps("before", [128, 512]), p.ps("cnt", [128, 512])
        loaded, filled, zeroed, padded, pads_ready, zeros_ready, tots, summed, chain = (
            p.sem(n) for n in ("loaded", "filled", "zeroed", "padded", "pads_ready", "zeros_ready",
                               "tots", "summed", "chain"))
        block = p.block()
        raw = slot_raw.rearrange("(p a) d -> p (a d)", p=128)

        @block.sync
        def _(sp):
            sp.dma_start(dst_i[:, :], dst.rearrange("(p t) -> p t", p=R)).then_inc(loaded, 16)
            sp.dma_start(src_i[:, :], src.rearrange("(p t) -> p t", p=R)).then_inc(loaded, 16)
            sp.wait_ge(pads_ready, 2)
            sp.dma_start(slot_meta.rearrange("(p t) c -> p (t c)", p=128),
                         pad[:, :, :].rearrange("p t c -> p (t c)")).then_inc(padded, 16)
            sp.wait_ge(zeros_ready, 1)
            for c in range(SLOTS // ZERO_COLS):
                sp.dma_start(raw[:, c * ZERO_COLS:(c + 1) * ZERO_COLS], zeros[:, :]).then_inc(zeroed, 16)
            sp.wait_ge(padded, 16)
            sp.wait_ge(zeroed, 16 * (SLOTS // ZERO_COLS))

        @block.gpsimd
        def _(pool):
            nc.gpsimd.memset(zeros[:, :], 0.0).then_inc(zeros_ready, 1)
            nc.gpsimd.memset(pad[:, :, 0:1], 0).then_inc(pads_ready, 1)
            nc.gpsimd.memset(pad[:, :, 1:2].bitcast(F32), -1.0).then_inc(pads_ready, 1)

        @block.tensor
        def _(pe):
            pe.wait_ge(tots, 1)
            nc.tensor.matmul(ps_before[0:R, 0:W], K.below[0:R, 0:R], tot[:, :], start=True, stop=True).then_inc(summed, 1)
            nc.tensor.matmul(ps_cnt[:, 0:W], K.ones[0:R, 0:128], tot[:, :], start=True, stop=True).then_inc(summed, 1)

        @block.vector
        def _(dve):
            link = Chain(dve, chain)
            link(nc.vector.tensor_copy(vid[:, :], K.iota_f[:, 0:W]))
            link(nc.vector.memset(rank[:, :], 0.0))
            dve.wait_ge(loaded, 32)
            link(nc.vector.tensor_copy(dst_f[:, :], dst_i[:, :]))
            link(nc.vector.tensor_scalar(quot_i[:, :], dst_f[:, :], 1.0 / R, None, ALU.mult))
            link(nc.vector.tensor_copy(win[:, :], quot_i[:, :]))
            link(nc.vector.scalar_tensor_tensor(out=rel[:, :], in0=win[:, :], scalar=-float(R), in1=dst_f[:, :],
                                                op0=ALU.mult, op1=ALU.add))
            link(nc.vector.tensor_scalar(low[:, :], rel[:, :], 0.0, None, ALU.is_lt))
            link(nc.vector.tensor_scalar(high[:, :], rel[:, :], float(R), None, ALU.is_ge))
            link(nc.vector.tensor_tensor(high[:, :], high[:, :], low[:, :], ALU.subtract))
            link(nc.vector.tensor_tensor(win[:, :], win[:, :], high[:, :], ALU.add))
            link(nc.vector.scalar_tensor_tensor(out=rel[:, :], in0=high[:, :], scalar=-float(R), in1=rel[:, :],
                                                op0=ALU.mult, op1=ALU.add))
            with dve.Fori(0, W) as v:
                link.loop(v, 4)
                link(nc.vector.tensor_scalar(mask[:, :], win[:, :], vid[0:R, bass.ds(v, 1)], None, ALU.is_equal))
                link(nc.vector.tensor_tensor_scan(count[:, :], K.ones_row[0:R, 0:T], mask[:, :], 0.0, ALU.mult, ALU.add))
                nc.vector.tensor_copy(tot[:, bass.ds(v, 1)], count[:, T - 1:T])
                link(nc.vector.tensor_tensor(term[:, :], mask[:, :], count[:, :], ALU.mult))
                link(nc.vector.tensor_tensor(rank[:, :], rank[:, :], term[:, :], ALU.add))
            link.end(W)
            nc.vector.tensor_copy(tot[:, W - 1:W], count[:, T - 1:T]).then_inc(tots, 1)
            dve.wait_ge(summed, 2)
            link(nc.vector.tensor_scalar(cnt_i[:, :], ps_cnt[:, 0:W], float(G - 1), None, ALU.add))
            link(nc.vector.tensor_scalar(cnt_i[:, :], cnt_i[:, :], 8, None, ALU.logical_shift_right))
            link(nc.vector.tensor_scalar(groups_f[:, :], cnt_i[:, :], 1.0, None, ALU.max))
            link(nc.vector.tensor_tensor_scan(end_f[:, :], K.ones_row[:, 0:W], groups_f[:, :], 0.0, ALU.mult, ALU.add))
            link(nc.vector.memset(K.bases[:, :], 0))
            link(nc.vector.tensor_copy(K.bases[:, 1:W + 1], end_f[:, :]))
            link(nc.vector.tensor_tensor(cnt_f[:, :], end_f[:, :], groups_f[:, :], ALU.subtract))
            link(nc.vector.tensor_scalar(cnt_f[:, :], cnt_f[:, :], float(G), -1.0, ALU.mult, ALU.add))
            link(nc.vector.tensor_tensor(off[:, :], cnt_f[0:R, :], ps_before[0:R, 0:W], ALU.add))
            with dve.Fori(0, W) as v:
                link.loop(v, 2)
                link(nc.vector.tensor_scalar(term[:, :], win[:, :], vid[0:R, bass.ds(v, 1)], off[:, bass.ds(v, 1)],
                                             ALU.is_equal, ALU.mult))
                link(nc.vector.tensor_tensor(rank[:, :], rank[:, :], term[:, :], ALU.add))
            link.end(W)
            link(nc.vector.tensor_copy(K.slot_of[:, :], rank[:, :]))
            link(nc.vector.tensor_scalar(tile_i[:, :], K.slot_of[:, :], 7, None, ALU.logical_shift_right))
            link(nc.vector.tensor_scalar(lane_i[:, :], K.slot_of[:, :], 127, None, ALU.bitwise_and))
            link(nc.vector.tensor_copy(tile_f[:, :], tile_i[:, :]))
            link(nc.vector.tensor_copy(lane_f[:, :], lane_i[:, :]))
            link(nc.vector.scalar_tensor_tensor(out=K.meta_row_of[:, :], in0=lane_f[:, :], scalar=float(TILES),
                                                in1=tile_f[:, :], op0=ALU.mult, op1=ALU.add))
            nc.vector.tensor_copy(K.meta[:, :, 0:1], src_i[:, :].unsqueeze(2))
            nc.vector.tensor_copy(K.meta[:, :, 1:2].bitcast(F32), rel[:, :].unsqueeze(2))


def scatter_meta(nc, ctx, K, slot_meta):
    B = 8
    with Part(nc, "meta", ctx) as p:
        rows = [p.sb(f"rows{h}", [R, B], I32) for h in range(2)]
        vals = [p.sb(f"vals{h}", [R, B, 2], I32) for h in range(2)]
        staged = [p.sem(f"staged{h}") for h in range(2)]
        done = [p.sem(f"done{h}") for h in range(2)]
        begun = p.sem("begun")
        block = p.block()

        @block.vector
        def _(dve):
            with dve.Fori(0, T // (2 * B)) as i:
                for h in range(2):
                    dve.wait_ge(done[h], i * (16 * B))
                    nc.vector.tensor_copy(rows[h][:, :], K.meta_row_of[:, bass.ds(i * (2 * B) + h * B, B)]).then_inc(staged[h], 1)
                    nc.vector.tensor_copy(vals[h][:, :, :], K.meta[:, bass.ds(i * (2 * B) + h * B, B), :]).then_inc(staged[h], 1)

        @block.gpsimd
        def _(pool):
            with pool.Fori(0, T // (2 * B)) as i:
                for h in range(2):
                    pool.wait_ge(staged[h], i * 2 + 2)
                    pool.sem_inc(begun, 1)
                    for b in range(B):
                        pool.indirect_dma_start(slot_meta, bass.IndirectOffsetOnAxis(ap=rows[h][:, b:b + 1], axis=0),
                                                vals[h][:, b, :], None).then_inc(done[h], 16)
            for h in range(2):
                pool.wait_ge(done[h], 16 * T // 2)


class Kept:

    def __init__(self, nc, ctx, sorting):
        def sb(name, shape, dt=F32, ctx=ctx):
            return ctx.enter_context(nc.sbuf_tensor(name, shape, dt))

        self.ident, self.ident16 = sb("ident", [128, 128]), sb("ident16", [128, 128], BF16)
        self.below, self.ones = sb("below", [128, 128]), sb("ones", [128, 512])
        self.ones_row = self.ones
        self.iota_f = sb("iota_f", [128, 128])
        self.lane_i, self.lane_f = sb("lane_i", [128, 1], I32), sb("lane_f", [128, 1])
        self.bases = sb("bases", [128, W + 1], I32)
        self.sender, self.rel = sb("sender", [128, TILES], I32), sb("rel", [128, TILES])
        self.win_of = sb("win_of", [128, 1 + GROUPS], I32)
        self.deg, self.dinv = sb("deg", [R, W, 2]), sb("dinv", [R, W])
        self.x, self.mean, self.rstd = sb("x", [R, W, D]), sb("mean", [R, W]), sb("rstd", [R, W])
        self.iota_i, self.iota16 = sb("iota_i", [128, N], I32, sorting), sb("iota16", [128, N + 1], I16, sorting)
        self.slot_of, self.meta_row_of = sb("slot_of", [R, T], I32, sorting), sb("meta_row_of", [R, T], I32, sorting)
        self.meta, self.sender_f = sb("meta", [R, T, 2], I32, sorting), sb("sender_f", [128, TILES], F32, sorting)


def read_slots(nc, ctx, K, slot_meta, rel_rows, x_in):
    C = TILES // 4
    with Part(nc, "slots", ctx) as p:
        both = p.sb("both", [128, TILES, 2], I32)
        rows = p.sb("rows", [C, 4, 128])
        ps = p.ps("ps", [128, 4, 128])
        past, ends = p.sb("past", [1, GROUPS, W]), p.sb("ends", [1, GROUPS])
        chain = p.sem("chain")
        loaded, split, turned, copied, stored, xin = (p.sem(n) for n in ("loaded", "split", "turned", "copied", "stored", "xin"))
        block = p.block()

        @block.sync
        def _(sp):
            sp.dma_start(both[:, :, :].rearrange("p t c -> p (t c)"),
                         slot_meta.rearrange("(p t) c -> p (t c)", p=128)).then_inc(loaded, 16)
            sp.dma_start(K.x[:, :, :], x_in.rearrange("(w p) d -> p w d", p=R)).then_inc(xin, 16)
            sp.wait_ge(copied, 1)
            sp.dma_start(rel_rows.rearrange("(a t) l -> t a l", a=4), rows[:, :, :]).then_inc(stored, 16)
            sp.wait_ge(xin, 16)
            sp.wait_ge(stored, 16)

        @block.vector
        def _(dve):
            dve.wait_ge(loaded, 16)
            nc.vector.tensor_copy(K.rel[:, :], both[:, :, 1:2].rearrange("p t c -> p (t c)").bitcast(F32)).then_inc(split, 1)
            nc.vector.tensor_copy(K.sender[:, :], both[:, :, 0:1].rearrange("p t c -> p (t c)"))
            nc.vector.tensor_copy(K.sender_f[:, :], both[:, :, 0:1].rearrange("p t c -> p (t c)"))
            dve.wait_ge(turned, 1)
            nc.vector.tensor_copy(rows[:, :, :], ps[0:C, :, :]).then_inc(copied, 1)
            link = Chain(dve, chain)
            link(nc.vector.tensor_tensor(past[:, :, :], K.iota_i[0:1, 0:GROUPS].unsqueeze(2).to_broadcast([1, GROUPS, W]),
                                         K.bases[0:1, 1:W + 1].unsqueeze(1).to_broadcast([1, GROUPS, W]), ALU.is_ge))
            link(nc.vector.tensor_reduce(ends[:, :], past[:, :, :], AX.X, ALU.add))
            link(nc.vector.memset(K.win_of[0:1, 0:1], 0))
            link(nc.vector.tensor_scalar(K.win_of[0:1, 1:1 + GROUPS], ends[:, :], float(W - 1), None, ALU.min))

        @block.tensor
        def _(pe):
            pe.wait_ge(split, 1)
            for a in range(4):
                last = nc.tensor.transpose(ps[0:C, a, :], K.rel[:, a * C:(a + 1) * C], K.ident[:, :])
            last.then_inc(turned, 1)


def count_edges(nc, ctx, K, edge_attr, slot_raw, a_dram):
    B = 8
    NB = (N + CHUNK - 1) // CHUNK
    full = (NB - 1) * CHUNK
    with Part(nc, "count", ctx) as p:
        oh_s = [p.sb(f"oh_s{h}", [128, N + 1], BF16) for h in range(2)]
        oh_r = [p.sb(f"oh_r{h}", [128, R], BF16) for h in range(2)]
        zrow = p.sb("zrow", [1, CHUNK], BF16)
        a_sb = p.sb("a_sb", [R, N], BF16)
        raws = [p.sb(f"raws{h}", [R, B, D]) for h in range(2)]
        rows = [p.sb(f"rows{h}", [R, B], I32) for h in range(2)]
        ps = p.ps("ps", [128, NB, 512])
        zeroed, ready, used, counted, taken_a, taken_d, a_stored = (
            p.sem(n) for n in ("zeroed", "ready", "used", "counted", "taken_a", "taken_d", "a_stored"))
        rows_in = [p.sem(f"rows_in{h}") for h in range(2)]
        staged = [p.sem(f"staged{h}") for h in range(2)]
        scattered = [p.sem(f"scattered{h}") for h in range(2)]
        begun = p.sem("begun")
        block = p.block()
        attr = edge_attr.rearrange("(p t) d -> p t d", p=R)

        @block.vector
        def _(dve):
            nc.vector.memset(zrow[:, :], 0.0).then_inc(zeroed, 1)
            with dve.Fori(0, W) as w:
                lo = dve.value_load(K.bases[0:1, bass.ds(w, 1)], min_val=0, max_val=MAX_GROUPS)
                hi = dve.value_load(K.bases[0:1, bass.ds(w + 1, 1)], min_val=1, max_val=MAX_GROUPS)
                with dve.Fori(lo, hi) as s:
                    for h in range(2):
                        dve.wait_ge(used, s * 2 + h)
                        nc.vector.tensor_scalar(oh_r[h][:, :], K.iota_f[:, 0:R], K.rel[:, bass.ds(s * 2 + h, 1)], None, ALU.is_equal)
                        nc.vector.tensor_scalar(oh_s[h][:, :], K.iota16[:, :], K.sender_f[:, bass.ds(s * 2 + h, 1)], None,
                                                ALU.is_equal).then_inc(ready, 1)
                dve.wait_ge(counted, w + 1)
                dve.wait_ge(a_stored, w * 16)
                nc.vector.tensor_scalar(a_sb[:, full:N], ps[0:R, NB - 1, 0:N - full], 1.0, 0.0, ALU.mult, ALU.add,
                                        accum_out=K.deg[:, bass.ds(w, 1), 1]).then_inc(taken_d, 1)

        @block.tensor
        def _(pe):
            pe.sem_inc(used, 1)
            pe.wait_ge(zeroed, 1)
            with pe.Fori(0, W) as w:
                lo = pe.value_load(K.bases[0:1, bass.ds(w, 1)], min_val=0, max_val=MAX_GROUPS)
                hi = pe.value_load(K.bases[0:1, bass.ds(w + 1, 1)], min_val=1, max_val=MAX_GROUPS)
                pe.wait_ge(taken_a, w)
                pe.wait_ge(taken_d, w)
                for c in range(NB):
                    n = min(CHUNK, N - c * CHUNK)
                    nc.tensor.matmul(ps[0:R, c, 0:n], zrow[0:1, 0:R], zrow[0:1, 0:n], start=True, stop=False, skip_group_check=True)
                with pe.Fori(lo, hi) as s:
                    for h in range(2):
                        pe.wait_ge(ready, s * 2 + (h + 1))
                        for c in range(NB):
                            n = min(CHUNK, N - c * CHUNK)
                            last = nc.tensor.matmul(ps[0:R, c, 0:n], oh_r[h][:, :], oh_s[h][:, c * CHUNK:c * CHUNK + n],
                                                    start=False, stop=False, skip_group_check=True)
                        last.then_inc(used, 1)
                for c in range(NB):
                    last = nc.tensor.matmul(ps[0:R, c, 0:1], zrow[0:1, 0:R], zrow[0:1, 0:1], start=False, stop=True, skip_group_check=True)
                last.then_inc(counted, 1)

        @block.scalar
        def _(act):
            with act.Fori(0, W) as w:
                for h in range(2):
                    act.wait_ge(scattered[h], w * (16 * B))
                    nc.scalar.copy(rows[h][:, :], K.slot_of[:, bass.ds(w * (2 * B) + h * B, B)]).then_inc(staged[h], 1)
                act.wait_ge(counted, w + 1)
                act.wait_ge(a_stored, w * 16)
                nc.scalar.activation(a_sb[:, 0:full].rearrange("p (c n) -> p c n", n=CHUNK), ps[0:R, 0:NB - 1, 0:CHUNK], ACT.Copy,
                                     accum_out=K.deg[:, bass.ds(w, 1), 0]).then_inc(taken_a, 1)
                act.wait_ge(taken_a, w + 1)
                act.wait_ge(taken_d, w + 1)
                act.dma_start(a_dram[bass.ds(w, 1), :, :].rearrange("a p n -> p (a n)"), a_sb[:, :]).then_inc(a_stored, 16)
            act.wait_ge(a_stored, 16 * W)

        @block.sync
        def _(sp):
            with sp.Fori(0, T // (2 * B)) as i:
                for h in range(2):
                    sp.wait_ge(scattered[h], i * (16 * B))
                    sp.dma_start(raws[h][:, :, :], attr[:, bass.ds(i * (2 * B) + h * B, B), :]).then_inc(rows_in[h], 16)

        @block.gpsimd
        def _(pool):
            with pool.Fori(0, T // (2 * B)) as i:
                for h in range(2):
                    pool.wait_ge(rows_in[h], i * 16 + 16)
                    pool.sem_inc(begun, 1)
                    pool.wait_ge(staged[h], i + 1)
                    pool.sem_inc(begun, 1)
                    for b in range(B):
                        pool.indirect_dma_start(slot_raw, bass.IndirectOffsetOnAxis(ap=rows[h][:, b:b + 1], axis=0),
                                                raws[h][:, b, :], None).then_inc(scattered[h], 16)
            for h in range(2):
                pool.wait_ge(scattered[h], 16 * T // 2)


def pipeline(eng, count, stages):
    leads = [lead for lead, _ in stages]
    begin, end = 2 - min(leads), count - max(leads)
    pairs = (end - begin) // 2

    def peeled(c):
        for lead, f in stages:
            if 0 <= c + lead < count:
                f(Index(None, offset=c + lead), (c + lead) % 2, Index(None, offset=(c + lead) // 2))

    for c in range(-max(leads), begin):
        peeled(c)
    with eng.Fori(0, pairs) as i:
        for j in range(2):
            for lead, f in stages:
                first = begin + j + lead
                f(Index(i, 2, first), first % 2, Index(i, 1, first // 2))
    for c in range(begin + 2 * pairs, count - min(leads)):
        peeled(c)


def encode_edges(nc, ctx, K, slot_raw, w_edge, b_edge, edges):
    B = 4
    CHUNKS = TILES // B
    with Part(nc, "encode", ctx) as p:
        wt, bias = p.sb("wt", [D, D]), p.sb("bias", [1, B, D])
        two = range(2)
        raw = [p.sb(f"raw{b}", [128, B, D]) for b in two]
        raw_t = [p.sb(f"raw_t{b}", [128, B, D]) for b in two]
        act_out = [p.sb(f"act_out{b}", [128, B, D]) for b in two]
        normed = [p.sb(f"normed{b}", [128, B, D]) for b in two]
        both = [p.sb(f"both{b}", [128, B, 2, D], F32R) for b in two]
        stats, mv = [p.sb(f"stats{b}", [128, B, 6]) for b in two], [p.sb(f"mv{b}", [128, B, 2]) for b in two]
        var, rstd = [p.sb(f"var{b}", [128, B]) for b in two], [p.sb(f"rstd{b}", [128, B]) for b in two]
        power = p.sb("power", [128, B])
        ps_in = [p.ps(f"ps_in{b}", [128, B, D]) for b in two]
        ps_lin = [p.ps(f"ps_lin{b}", [128, B, D]) for b in two]
        ps_out = [p.ps(f"ps_out{b}", [128, B, D]) for b in two]
        consts, powered, turned, copied, lin, gelued, moments, rooted, norm_done, back, high_ready, low_ready = (
            p.sem(n) for n in ("consts", "powered", "turned", "copied", "lin", "gelued", "moments",
                               "rooted", "norm_done", "back", "high_ready", "low_ready"))
        begun, chain = p.sem("begun"), p.sem("chain")
        raw_in = [p.sem(f"raw_in{b}") for b in two]
        stored = [p.sem(f"stored{b}") for b in two]
        block = p.block()
        slots = slot_raw.rearrange("(t l) d -> l t d", l=128)

        @block.sync
        def _(sp):
            sp.dma_start(wt[:, :], w_edge).then_inc(consts, 16)
            for b in range(B):
                sp.dma_start(bias[:, b, :], b_edge.rearrange("(a n) -> a n", a=1)).then_inc(consts, 16)

            def load(c, b, n):
                at_least(sp, turned, c - 1)
                sp.dma_start(raw[b][:, :, :], slots[:, bass.ds((c * B).value, B), :]).then_inc(raw_in[b], 16)

            def store(c, b, n):
                at_least(sp, low_ready, c + 1)
                sp.dma_start(edges[:, bass.ds((c * B).value, B), :, :].rearrange("p b c d -> p (b c d)"),
                             both[b][:, :, :, :].rearrange("p b c d -> p (b c d)").bitcast(F32)).then_inc(stored[b], 16)
            pipeline(sp, CHUNKS, [(2, load), (-3, store)])
            for b in two:
                sp.wait_ge(stored[b], 8 * CHUNKS)

        @block.tensor
        def _(pe):
            def transpose_in(c, b, n):
                at_least(pe, raw_in[b], n * 16 + 16)
                at_least(pe, copied, c - 1)
                for k in range(B):
                    ins = nc.tensor.transpose(ps_in[b][:, k, :], raw[b][:, k, :], K.ident[:, :])
                ins.then_inc(turned, 1)

            def linear(c, b, n):
                at_least(pe, copied, c + 1)
                at_least(pe, gelued, c - 1)
                nc.tensor.matmul(ps_lin[b][:, :, :].rearrange("p k d -> p (k d)"), K.ones[0:1, 0:128],
                                 bias[:, :, :].rearrange("p k d -> p (k d)"), start=True, stop=False, skip_group_check=True)
                for k in range(B):
                    ins = nc.tensor.matmul(ps_lin[b][:, k, :], raw_t[b][:, k, :], wt[:, :], start=False, stop=k == B - 1,
                                           skip_group_check=True)
                ins.then_inc(lin, 1)

            def transpose_back(c, b, n):
                at_least(pe, norm_done, c + 1)
                at_least(pe, low_ready, c - 1)
                for k in range(B):
                    ins = nc.tensor.transpose(ps_out[b][:, k, :], normed[b][:, k, :], K.ident[:, :])
                ins.then_inc(back, 1)

            pe.wait_ge(consts, 16 * (B + 1))
            pipeline(pe, CHUNKS, [(1, transpose_in), (0, linear), (-2, transpose_back)])

        @block.scalar
        def _(act):
            def copy_in(c, b, n):
                at_least(act, turned, c + 1)
                at_least(act, lin, c - 1)
                nc.scalar.copy(raw_t[b][:, :, :], ps_in[b][:, :, :]).then_inc(copied, 1)

            def gelu(c, b, n):
                at_least(act, lin, c + 1)
                at_least(act, norm_done, c - 1)
                nc.scalar.activation(act_out[b][:, :, :], ps_lin[b][:, :, :], ACT.Gelu_apprx_tanh).then_inc(gelued, 1)

            def copy_high(c, b, n):
                at_least(act, back, c + 1)
                at_least(act, stored[b], n * 16)
                nc.scalar.copy(both[b][:, :, 0, :], ps_out[b][:, :, :]).then_inc(high_ready, 1)
            pipeline(act, CHUNKS, [(1, copy_in), (0, gelu), (-3, copy_high)])

        @block.gpsimd
        def _(pool):
            nc.gpsimd.memset(power[:, :], -0.5).then_inc(powered, 1)
            pool.wait_ge(powered, 1)

            def root(c, b, n):
                at_least(pool, moments, c + 1)
                nc.gpsimd.tensor_tensor(rstd[b][:, :], var[b][:, :], power[:, :], ALU.pow).then_inc(rooted, 1)
            pipeline(pool, CHUNKS, [(0, root)])

        @block.vector
        def _(dve):
            def take_moments(c, b, n):
                at_least(dve, gelued, c + 1)
                for k in range(B):
                    ins = nc.vector.bn_stats(stats[b][:, k, :], act_out[b][:, k, :])
                ins.then_inc(chain, 1)
                at_least(dve, chain, c * 2 + 1)
                dve.sem_inc(begun, 1)
                for k in range(B):
                    ins = nc.vector.bn_aggr(mv[b][:, k, :], stats[b][:, k, :])
                ins.then_inc(chain, 1)
                at_least(dve, chain, c * 2 + 2)
                nc.vector.tensor_scalar(var[b][:, :], mv[b][:, :, 1:2].rearrange("p b c -> p (b c)"), LN_EPS, None,
                                        ALU.add).then_inc(moments, 1)

            def normalise(c, b, n):
                at_least(dve, rooted, c + 1)
                at_least(dve, back, c - 1)
                for k in range(B):
                    ins = nc.vector.tensor_scalar(normed[b][:, k, :], act_out[b][:, k, :], mv[b][:, k, 0:1],
                                                  rstd[b][:, k:k + 1], ALU.subtract, ALU.mult)
                ins.then_inc(norm_done, 1)

            def take_low(c, b, n):
                at_least(dve, high_ready, c + 1)
                nc.vector.tensor_tensor(both[b][:, :, 1, :], ps_out[b][:, :, :], both[b][:, :, 0, :].bitcast(F32), ALU.subtract).then_inc(low_ready, 1)
            pipeline(dve, CHUNKS, [(0, take_moments), (-1, normalise), (-3, take_low)])


def norm_moments(nc, ctx, K, name, x):
    with Part(nc, name, ctx) as p:
        stats, half, var, tmp = p.sb("stats", [R, W, 6]), p.sb("half", [R, W]), p.sb("var", [R, W]), p.sb("tmp", [R, W])
        ready, rooted, chain = p.sem("ready"), p.sem("rooted"), p.sem("chain")
        block = p.block()

        def col(c):
            return stats[:, :, c:c + 1].rearrange("p w c -> p (w c)")

        @block.vector
        def _(dve):
            link = Chain(dve, chain)
            with dve.Fori(0, NC) as i:
                link.loop(i, 1)
                for u in range(U):
                    last = nc.vector.bn_stats(stats[:, bass.ds(i * U + u, 1), :].rearrange("p a c -> p (a c)"),
                                              x[:, bass.ds(i * U + u, 1), :].rearrange("p a d -> p (a d)"))
                link(last)
            link.end(NC)
            link(nc.vector.tensor_tensor(half[:, :], col(1), col(4), ALU.subtract))
            link(nc.vector.tensor_scalar(half[:, :], half[:, :], 0.5, None, ALU.mult))
            link(nc.vector.tensor_tensor(K.mean[:, :], col(4), half[:, :], ALU.add))
            link(nc.vector.tensor_tensor(half[:, :], half[:, :], half[:, :], ALU.mult))
            link(nc.vector.tensor_tensor(var[:, :], col(2), col(5), ALU.add))
            link(nc.vector.scalar_tensor_tensor(out=var[:, :], in0=var[:, :], scalar=1.0 / D, in1=half[:, :],
                                                op0=ALU.mult, op1=ALU.add))
            nc.vector.tensor_scalar(var[:, :], var[:, :], LN_EPS, None, ALU.add).then_inc(ready, 1)
            dve.wait_ge(rooted, 1)
            link(nc.vector.reciprocal(K.rstd[:, :], tmp[:, :]))

        @block.scalar
        def _(act):
            act.wait_ge(ready, 1)
            nc.scalar.activation(tmp[:, :], var[:, :], ACT.Sqrt).then_inc(rooted, 1)


def project(nc, ctx, K, name, x, weights, width, finish, norm=False, relu=False, loads=(), extra=None, extra_sb=None):
    def banks(n):
        return [range(a, min(a + n, U)) for a in range(0, U, n)]

    with Part(nc, name, ctx) as p:
        tiles = [p.sb(f"rows{u}", [R, D]) for u in range(U)]
        turned_sb = p.sb("turned", [D, U, 128])
        more = [p.sb(f"more{u}", [D, R]) for u in range(U)] if extra is not None else None
        per_t, per_o = 4, 512 // width
        ps_t = p.ps("ps_t", [128, len(banks(per_t)) * per_t, 128])
        ps_o = p.ps("ps_o", [128, len(banks(per_o)) * per_o, width])
        loaded, staged, turned, copied, product, done = (p.sem(n) for n in ("loaded", "staged", "turned", "copied", "product", "done"))
        link_sem = p.sem("link")
        work = finish(p)
        block = p.block()

        @block.sync
        def _(sp):
            for dst, src in loads:
                sp.dma_start(dst, src).then_inc(loaded, 16)
            if loads:
                sp.wait_ge(loaded, 16 * len(loads))

        @block.vector
        def _(dve):
            if loads:
                dve.wait_ge(loaded, 16 * len(loads))
            link = Chain(dve, link_sem)
            dve.sem_inc(done, U)
            with dve.Fori(0, NC) as i:
                link.loop(i, U * work.links)
                for u in range(U):
                    w = i * U + u
                    dve.wait_ge(turned, w + 1)
                    row = x[:, bass.ds(w, 1), :].rearrange("p a d -> p (a d)")
                    if norm:
                        ins = nc.vector.tensor_scalar(tiles[u][:, :], row, K.mean[:, bass.ds(w, 1)], K.rstd[:, bass.ds(w, 1)],
                                                      ALU.subtract, ALU.mult)
                    else:
                        ins = nc.vector.tensor_copy(tiles[u][:, :], row)
                    if extra is not None:
                        ins = nc.vector.tensor_copy(more[u][:, :], extra_sb[:, bass.ds(w * R, R)])
                    ins.then_inc(staged, 1)
                for bank in banks(per_o):
                    dve.wait_ge(product, i * U + (bank[-1] + U + 1))
                    for u in bank:
                        work(nc, link, i * U + u, ps_o[0:R, u, :]).then_inc(done, 1)
            link.end(NC)

        @block.tensor
        def _(pe):
            pe.sem_inc(turned, U)
            pe.sem_inc(product, U)
            if loads:
                pe.wait_ge(loaded, 16 * len(loads))
            with pe.Fori(0, NC) as i:
                for bank in banks(per_t):
                    pe.wait_ge(staged, i * U + (bank[-1] + 1))
                    for u in bank:
                        ins = nc.tensor.transpose(ps_t[:, u, 0:R], tiles[u][:, :], K.ident[0:R, 0:R])
                    ins.then_inc(turned, len(bank))
                for bank in banks(per_o):
                    pe.wait_ge(copied, i * U + (bank[-1] + 1))
                    pe.wait_ge(done, i * U + (bank[-1] + 1))
                    for u in bank:
                        ins = nc.tensor.matmul(ps_o[0:R, u, :], turned_sb[:, u, 0:R], weights, start=True, stop=extra is None)
                        if extra is not None:
                            ins = nc.tensor.matmul(ps_o[0:R, u, :], more[u][:, :], extra, start=False, stop=True)
                    ins.then_inc(product, len(bank))

        @block.scalar
        def _(act):
            with act.Fori(0, NC) as i:
                for bank in banks(per_t):
                    act.wait_ge(turned, i * U + (bank[-1] + U + 1))
                    act.wait_ge(product, i * U + (bank[-1] + 1))
                    b = slice(bank[0], bank[-1] + 1)
                    nc.scalar.activation(turned_sb[:, b, 0:R], ps_t[:, b, 0:R], ACT.Relu if relu else ACT.Copy).then_inc(copied, len(bank))


class Finish:

    def __init__(self, links, f):
        self.links, self.f = links, f

    def __call__(self, nc, link, w, product):
        return self.f(nc, link, w, product)


def at(t, w):
    return t[:, bass.ds(w, 1), :].rearrange("p a d -> p (a d)")


def spread(nc, ctx, K, name, g, bias, out, at_dram, a_dram=None, relu=False, residual=None):
    make = a_dram is not None
    with Part(nc, name, ctx) as p:
        parts = p.sb("parts", [R, W, 3, D], BF16)
        rest = p.sb("rest", [R, W, D])
        at_sb = [p.sb(f"at{u}", [R, W, R], BF16) for u in range(2)]
        a_sb = [p.sb(f"a{u}", [R, N], BF16) for u in range(2)] if make else None
        total = p.sb("total", [R, D])
        bias_sb = p.sb("bias", [128, D])
        ps = [p.ps(f"ps{u}", [128, 512]) for u in range(2)]
        ps_t = [p.ps(f"ps_t{u}", [128, 8, 128], BF16) for u in range(4)] if make else None
        biased, split, product, done, chain, turned, copied = (
            p.sem(n) for n in ("biased", "split", "product", "done", "chain", "turned", "copied"))
        a_in = [p.sem(f"a_in{u}") for u in range(2)]
        at_out = [p.sem(f"at_out{u}") for u in range(2)]
        block = p.block()
        ROUNDS = [(r, min(8, W - 8 * r)) for r in range(4)]

        @block.vector
        def _(dve):
            link = Chain(dve, chain)
            link(nc.vector.tensor_copy(parts[:, :, 0, :], g[:, :, :]))
            link(nc.vector.tensor_tensor(rest[:, :, :], g[:, :, :], parts[:, :, 0, :], ALU.subtract))
            link(nc.vector.tensor_copy(parts[:, :, 1, :], rest[:, :, :]))
            link(nc.vector.tensor_tensor(rest[:, :, :], rest[:, :, :], parts[:, :, 1, :], ALU.subtract))
            nc.vector.tensor_copy(parts[:, :, 2, :], rest[:, :, :]).then_inc(split, 1)
            dve.wait_ge(biased, 16)
            dve.sem_inc(done, 1)

            def window(w, u):
                dve.wait_ge(product, w + 2)
                link(nc.vector.tensor_reduce(total[:, :], ps[u][0:R, 0:3 * D].rearrange("p (c d) -> p d c", c=3), AX.X, ALU.add))
                link(nc.vector.tensor_tensor(total[:, :], total[:, :], at(g, w), ALU.add))
                ins = nc.vector.scalar_tensor_tensor(out=total[:, :] if relu or residual is not None else at(out, w),
                                                     in0=total[:, :], scalar=K.dinv[:, bass.ds(w, 1)],
                                                     in1=bias_sb[0:R, :], op0=ALU.mult, op1=ALU.add)
                if relu:
                    link(ins)
                    ins = nc.vector.tensor_scalar(at(out, w), total[:, :], 0.0, None, ALU.max)
                if residual is not None:
                    link(ins)
                    ins = nc.vector.tensor_tensor(at(out, w), total[:, :], at(residual, w), ALU.add)
                ins.then_inc(done, 1)
                dve.wait_ge(done, w + 2)

            links = 2 + bool(relu) + (residual is not None)
            with dve.Fori(0, W // 2) as i:
                link.loop(i, 2 * links)
                for u in range(2):
                    window(i * 2 + u, u)
            link.end(W // 2)
            window(W - 1, 0)

        @block.tensor
        def _(pe):
            def window(w, u, i):
                if make:
                    pe.wait_ge(a_in[u], i * 16 + 16)
                    for r, n in ROUNDS:
                        pe.wait_ge(copied, w * 4 + (r + 1))
                        for k in range(n):
                            c = 8 * r + k
                            ins = nc.tensor.transpose(ps_t[r][0:R, k, 0:R], a_sb[u][:, c * R:(c + 1) * R], K.ident16[0:R, 0:R])
                        ins.then_inc(turned, 1)
                    pe.wait_ge(copied, w * 4 + 8)
                else:
                    pe.wait_ge(a_in[u], i * 16 + 16)
                pe.wait_ge(done, w)
                for k in range(W):
                    ins = nc.tensor.matmul(ps[u][0:R, 0:3 * D], at_sb[u][:, k, :], parts[:, k, :, :].rearrange("p c d -> p (c d)"),
                                           start=(k == 0), stop=(k == W - 1))
                ins.then_inc(product, 1)

            pe.sem_inc(product, 1)
            pe.sem_inc(turned, 4)
            pe.wait_ge(split, 1)
            with pe.Fori(0, W // 2) as i:
                for u in range(2):
                    window(i * 2 + u, u, i)
            window(W - 1, 0, W // 2)

        @block.sync
        def _(sp):
            sp.dma_start(bias_sb[:, :], bias.partition_broadcast(128)).then_inc(biased, 16)

            def load(w, u, i):
                if make:
                    sp.wait_ge(turned, w * 4)
                    sp.dma_start(a_sb[u][:, :], a_dram[bass.ds(w, 1), :, :].rearrange("a p n -> p (a n)")).then_inc(a_in[u], 16)
                else:
                    sp.wait_ge(product, w)
                    sp.dma_start(at_sb[u][:, :, :].rearrange("p k r -> p (k r)"),
                                 at_dram[bass.ds(w, 1), :, :].rearrange("a p n -> p (a n)")).then_inc(a_in[u], 16)
            with sp.Fori(0, W // 2) as i:
                for u in range(2):
                    load(i * 2 + u, u, i)
            load(W - 1, 0, W // 2)

        if make:
            @block.scalar
            def _(act):
                act.sem_inc(copied, 4)

                def window(w, u, i):
                    act.wait_ge(product, w)
                    act.wait_ge(at_out[u], i * 16)
                    for r, n in ROUNDS:
                        act.wait_ge(turned, w * 4 + (r + 5))
                        nc.scalar.copy(at_sb[u][:, 8 * r:8 * r + n, :], ps_t[r][0:R, 0:n, 0:R]).then_inc(copied, 1)
                    act.wait_ge(copied, w * 4 + 8)
                    act.dma_start(at_dram[bass.ds(w, 1), :, :].rearrange("a p n -> p (a n)"),
                                  at_sb[u][:, :, :].rearrange("p k r -> p (k r)")).then_inc(at_out[u], 16)
                with act.Fori(0, W // 2) as i:
                    for u in range(2):
                        window(i * 2 + u, u, i)
                window(W - 1, 0, W // 2)
                act.wait_ge(at_out[0], 16 * (W // 2 + 1))
                act.wait_ge(at_out[1], 16 * (W // 2))


def sums_to_degrees(nc, ctx, K):
    with Part(nc, "degree", ctx) as p:
        deg, root = p.sb("deg", [R, W]), p.sb("root", [R, W])
        ready, rooted, chain = p.sem("ready"), p.sem("rooted"), p.sem("chain")
        block = p.block()

        @block.vector
        def _(dve):
            link = Chain(dve, chain)
            link(nc.vector.tensor_reduce(deg[:, :], K.deg[:, :, :], AX.X, ALU.add))
            nc.vector.tensor_scalar(deg[:, :], deg[:, :], 1.0, None, ALU.add).then_inc(ready, 1)
            dve.wait_ge(rooted, 1)
            link(nc.vector.reciprocal(K.dinv[:, :], root[:, :]))

        @block.scalar
        def _(act):
            act.wait_ge(ready, 1)
            nc.scalar.activation(root[:, :], deg[:, :], ACT.Sqrt).then_inc(rooted, 1)


def norm_apply(nc, ctx, K, name, x, out, scale=None, offset=None, relu=False, add_to=None, gelu_first=False):
    with Part(nc, name, ctx) as p:
        if scale is not None:
            scale_sb, offset_sb = p.sb("scale", [128, D]), p.sb("offset", [128, D])
        loaded, chain = p.sem("loaded"), p.sem("chain")
        block = p.block()

        @block.sync
        def _(sp):
            if scale is not None:
                sp.dma_start(scale_sb[:, :], scale.partition_broadcast(128)).then_inc(loaded, 16)
                sp.dma_start(offset_sb[:, :], offset.partition_broadcast(128)).then_inc(loaded, 16)
                sp.wait_ge(loaded, 32)

        @block.vector
        def _(dve):
            link = Chain(dve, chain)
            with dve.Fori(0, NC) as i:
                link.loop(i, 1)
                for u in range(U):
                    w = i * U + u
                    last = nc.vector.tensor_scalar(at(out, w), at(x, w), K.mean[:, bass.ds(w, 1)], K.rstd[:, bass.ds(w, 1)],
                                                   ALU.subtract, ALU.mult)
                link(last)
            link.end(NC)
            if relu:
                link(nc.vector.tensor_scalar(out[:, :, :], out[:, :, :], 0.0, None, ALU.max))
            if scale is not None:
                dve.wait_ge(loaded, 32)
                link(nc.vector.tensor_tensor(out[:, :, :], out[:, :, :], scale_sb[0:R, :].unsqueeze(1).to_broadcast([R, W, D]), ALU.mult))
                link(nc.vector.tensor_tensor(out[:, :, :], out[:, :, :], offset_sb[0:R, :].unsqueeze(1).to_broadcast([R, W, D]), ALU.add))
            if add_to is not None:
                link(nc.vector.tensor_tensor(add_to[:, :, :], add_to[:, :, :], out[:, :, :], ALU.add))


def gelu_nodes(nc, ctx, K, t):
    with Part(nc, "gelu", ctx) as p:
        done = p.sem("done")
        block = p.block()

        @block.scalar
        def _(act):
            nc.scalar.activation(t[:, :, :], t[:, :, :], ACT.Gelu_apprx_tanh).then_inc(done, 1)
            act.wait_ge(done, 1)


def message_weights(nc, ctx, K, name, M, w1, b1, w2, b2, e_scale, e_offset):
    with Part(nc, name, ctx) as p:
        raw = p.sb("raw", [D, H])
        sc, of = p.sb("sc", [D, 1]), p.sb("of", [D, 1])
        of_b = p.sb("of_b", [D, R])
        b1_sb = p.sb("b1", [128, H])
        ps = p.ps("ps", [128, 512])
        loaded, ready, done, chain = (p.sem(n) for n in ("loaded", "ready", "done", "chain"))
        block = p.block()
        loads = [(M.w_sr[:, 0:H], w1[0:D, :]), (M.w_sr[:, H:2 * H], w1[D:2 * D, :]), (raw[:, :], w1[2 * D:3 * D, :]),
                 (M.w2[:, :, :], w2.rearrange("(c k) n -> k c n", k=128)), (M.b2[:, :], b2.partition_broadcast(128)),
                 (b1_sb[:, :], b1.partition_broadcast(128)),
                 (sc[:, :], e_scale.rearrange("(p a) -> p a", a=1)), (of[:, :], e_offset.rearrange("(p a) -> p a", a=1))]

        @block.sync
        def _(sp):
            for dst, src in loads:
                sp.dma_start(dst, src).then_inc(loaded, 16)
            sp.wait_ge(loaded, 16 * len(loads))

        @block.vector
        def _(dve):
            link = Chain(dve, chain)
            dve.wait_ge(loaded, 16 * len(loads))
            link(nc.vector.tensor_scalar(M.w_e[:, :], raw[:, :], sc[:, 0:1], None, ALU.mult))
            link(nc.vector.tensor_copy(M.we_h[:, :], M.w_e[:, :]))
            link(nc.vector.tensor_tensor(M.we_l[:, :], M.w_e[:, :], M.we_h[:, :].bitcast(F32), ALU.subtract))
            nc.vector.tensor_scalar(of_b[:, :], K.ones[:, 0:R], of[:, 0:1], None, ALU.mult).then_inc(ready, 1)
            dve.wait_ge(done, 1)
            link(nc.vector.tensor_tensor(M.b_r[:, :], b1_sb[0:R, :], ps[0:R, 0:H], ALU.add))

        @block.tensor
        def _(pe):
            pe.wait_ge(loaded, 16 * len(loads))
            pe.wait_ge(ready, 1)
            nc.tensor.matmul(ps[0:R, 0:H], of_b[:, :], raw[:, :], start=True, stop=True).then_inc(done, 1)


def store_senders(nc, ctx, K, name, M, p_dram):
    with Part(nc, name, ctx) as p:
        stored = p.sem("stored")
        block = p.block()

        @block.sync
        def _(sp):
            sp.dma_start(p_dram.rearrange("(w p) d -> p w d", p=R), M.send[:, :, :]).then_inc(stored, 16)
            sp.wait_ge(stored, 16)


def messages(nc, ctx, K, name, M, p_dram, edges, rel_rows):
    with Part(nc, name, ctx) as p:
        four, two = range(4), range(2)
        edge = [p.sb(f"edge{m}", [D, 2, 2, 128], F32R) for m in four]
        rel_b = [p.sb(f"rel_b{m}", [R, 256]) for m in four]
        got = [p.sb(f"got{m}", [128, 2, H]) for m in four]
        idx = [p.sb(f"idx{m}", [128, 2], I32) for m in four]
        oh = [p.sb(f"oh{m}", [128, 2, R + 1], F32R) for m in four]
        oh_t = [p.sb(f"oh_t{q}", [R, 256], F32R) for q in two]
        hid = [p.sb(f"hid{h}", [128, H]) for h in two]
        hid_t = [p.sb(f"hid_t{h}", [128, 2, 128]) for h in two]
        msg_b = p.sb("msg_b", [128, 2, D])
        msg_h, msg_l = ([p.sb(f"{n}{q}", [128, 2, D], F32R) for q in two] for n in ("msg_h", "msg_l"))
        ps1 = [p.ps(f"ps1_{h}", [128, 512]) for h in two]
        ps_t = [p.ps(f"ps_t{h}", [128, 4, 128]) for h in two]
        ps2 = p.ps("ps2", [128, 2, 512])
        ps_a = [p.ps(f"ps_a{q}", [128, 512]) for q in two]
        oht_ready, oh_ready, added, biased, rest_ready, cleared = (
            p.sem(n) for n in ("oht_ready", "oh_ready", "added", "biased", "rest_ready", "cleared"))
        first, turned, second, summed, banked = (p.sem(n) for n in ("first", "turned", "second", "summed", "banked"))
        relu1, relu2, idx_ready = (p.sem(n) for n in ("relu1", "relu2", "idx_ready"))
        begun, ended = p.sem("begun"), p.sem("ended")
        rel_in = [p.sem(f"rel_in{m}") for m in four]
        e_in = [p.sem(f"e_in{m}") for m in four]
        gathered = [[p.sem(f"gathered{m}{h}") for h in two] for m in four]
        block = p.block()

        def steps(eng):
            total = eng.value_load(K.bases[0:1, W:W + 1], min_val=1, max_val=MAX_GROUPS)
            return ((total + 3) >> 2) << 2, (total + 3) >> 2

        def groups(eng, step):
            total = eng.value_load(K.bases[0:1, W:W + 1], min_val=1, max_val=MAX_GROUPS)
            with eng.Fori(0, (total + 3) >> 2) as turn:
                for k in four:
                    step(Index(turn, 4, k), k, turn)

        def nth(turn, k, lead):
            return (k + lead) % 4, Index(turn, offset=(k + lead) // 4)


        @block.sync
        def _(sp):
            rows = rel_rows.rearrange("(g t) l -> g (t l)", t=2)

            def load(g, m, waits):
                if waits:
                    at_least(sp, oht_ready, g - 3)
                sp.dma_start(rel_b[m][:, :], rows[bass.ds(g.value, 1), :].to_broadcast([R, 256])).then_inc(rel_in[m], 16)
                if waits:
                    at_least(sp, first, g * 2 - 6)
                sp.dma_start(edge[m][:, :, :, :].rearrange("p t c l -> p (t c l)").bitcast(F32),
                             edges[:, bass.ds((g * 2).value, 2), :, :].rearrange("p t c l -> p (t c l)")).then_inc(e_in[m], 16)

            for m in four:
                load(ZERO + m, m, False)
            groups(sp, lambda g, k, turn: load(g + 4, k, True))
            _, rounds = steps(sp)
            for m in four:
                sp.wait_ge(rel_in[m], rounds * 16 + 16)
                sp.wait_ge(e_in[m], rounds * 16 + 16)
            sp.sem_inc(ended, 1)

        @block.gpsimd
        def _(pool):
            def gather(g, m, waits):
                nc.gpsimd.tensor_copy(idx[m][:, :], K.sender[:, bass.ds((g * 2).value, 2)]).then_inc(idx_ready, 1)
                at_least(pool, idx_ready, g + 1)
                if waits:
                    pool.sem_inc(begun, 1)
                for h in two:
                    pool.indirect_dma_start(got[m][:, h, :], None, p_dram,
                                            bass.IndirectOffsetOnAxis(ap=idx[m][:, h:h + 1], axis=0)).then_inc(gathered[m][h], 16)

            def step(g, k, turn):
                at_least(pool, added, g * 2 + 2)
                pool.sem_inc(begun, 1)
                gather(g + 4, k, True)

            for m in four:
                gather(ZERO + m, m, False)
            groups(pool, step)
            _, rounds = steps(pool)
            for m in four:
                for h in two:
                    pool.wait_ge(gathered[m][h], rounds * 16 + 16)
            pool.sem_inc(begun, 1)

        @block.vector
        def _(dve):
            def columns(g, q, m, n, waits):
                at_least(dve, rel_in[m], n * 16 + 16)
                if waits:
                    at_least(dve, first, g * 2 - 2)
                nc.vector.tensor_scalar(oh_t[q][:, :], rel_b[m][:, :], K.lane_f[0:R, 0:1], None, ALU.is_equal).then_inc(oht_ready, 1)

            def rows(g, m):
                for h in two:
                    nc.vector.tensor_scalar(oh[m][:, h, :], K.iota_f[:, 0:R + 1], K.rel[:, bass.ds((g * 2 + h).value, 1)], None,
                                            ALU.is_equal).then_inc(oh_ready, 1)

            def add(g, m, n, h, waits):
                at_least(dve, gathered[m][h], n * 16 + 16)
                at_least(dve, first, g * 2 + (h + 1))
                if waits:
                    at_least(dve, turned, g * 2 - 1 + h)
                nc.vector.tensor_tensor(hid[h][:, :], ps1[h][:, 0:H], got[m][:, h, :], ALU.add).then_inc(added, 1)

            def bank(g, q, w):
                at_least(dve, summed, g + 3)
                at_least(dve, banked, g + 3)
                nc.vector.tensor_tensor(M.agg[:, bass.ds(w * R, R)], M.agg[:, bass.ds(w * R, R)], ps_a[q][:, 0:R],
                                        ALU.add).then_inc(banked, 1)

            def step(g, k, turn):
                q = k % 2
                w = dve.value_load(K.win_of[0:1, bass.ds(g.value, 1)], min_val=0, max_val=W - 1)
                add(g + 1, *nth(turn, k, 1), 0, True)
                columns(g + 2, q, *nth(turn, k, 2), True)
                rows(g + 2, (k + 2) % 4)
                add(g + 1, *nth(turn, k, 1), 1, True)
                at_least(dve, second, g * 2 + 3)
                nc.vector.tensor_tensor(msg_b[:, :, :], ps2[:, :, 0:D], M.b2[:, :].unsqueeze(1).to_broadcast([128, 2, D]),
                                        ALU.add).then_inc(biased, 1)
                bank(g - 1, 1 - q, w)
                at_least(dve, relu2, g + 1)
                nc.vector.scalar_tensor_tensor(out=msg_l[q][:, :, :].rearrange("p h d -> p (h d)"),
                                               in0=msg_b[:, :, :].rearrange("p h d -> p (h d)"), scalar=0.0,
                                               in1=msg_h[q][:, :, :].bitcast(F32).rearrange("p h d -> p (h d)"),
                                               op0=ALU.max, op1=ALU.subtract).then_inc(rest_ready, 1)

            nc.vector.memset(M.agg[:, :], 0.0).then_inc(cleared, 1)
            for t in (msg_l[1], msg_h[1], oh[3]):
                nc.vector.memset(t[:, :, :].bitcast(F32), 0.0).then_inc(cleared, 1)
            dve.wait_ge(cleared, 4)
            dve.sem_inc(oh_ready, 2)
            dve.sem_inc(rest_ready, 1)
            dve.sem_inc(banked, 2)
            dve.sem_inc(biased, 1)
            for g in two:
                columns(ZERO + g, g, g, ZERO, False)
                rows(ZERO + g, g)
            for h in two:
                add(ZERO, 0, ZERO, h, False)
            groups(dve, step)
            total, _ = steps(dve)
            w = dve.value_load(K.win_of[0:1, bass.ds(total, 1)], min_val=0, max_val=W - 1)
            dve.wait_ge(summed, total + 2)
            dve.wait_ge(banked, total + 2)
            nc.vector.tensor_tensor(M.agg[:, bass.ds(w * R, R)], M.agg[:, bass.ds(w * R, R)], ps_a[1][:, 0:R], ALU.add).then_inc(banked, 1)

        @block.tensor
        def _(pe):
            def products(g, q, m, n, h, w, waits):
                if h == 0:
                    at_least(pe, e_in[m], n * 16 + 16)
                    at_least(pe, oht_ready, g + 1)
                if waits:
                    at_least(pe, added, g * 2 - 1 + h)
                out = ps1[h][:, 0:H]
                nc.tensor.matmul(out, edge[m][:, h, 1, :], M.we_h[:, :], start=True, stop=False)
                nc.tensor.matmul(out, edge[m][:, h, 0, :], M.we_l[:, :], start=False, stop=False)
                nc.tensor.matmul(out, edge[m][:, h, 0, :], M.we_h[:, :], start=False, stop=False)
                nc.tensor.matmul(out, oh_t[q][:, h * 128:(h + 1) * 128], at(M.recv_l, w), start=False, stop=False)
                nc.tensor.matmul(out, oh_t[q][:, h * 128:(h + 1) * 128], at(M.recv_h, w), start=False, stop=True).then_inc(first, 1)

            def turn_hidden(g, h, waits):
                at_least(pe, added, g * 2 + (h + 1))
                if waits:
                    at_least(pe, relu1, g * 2 - 1 + 2 * h)
                for c in two:
                    ins = nc.tensor.transpose(ps_t[h][:, c, :], hid[h][:, c * 128:(c + 1) * 128], K.ident[:, :])
                ins.then_inc(turned, 1)

            def message(g, h):
                at_least(pe, relu1, g * 2 + (h + 1))
                if h == 0:
                    at_least(pe, biased, g + 1)
                for c in two:
                    ins = nc.tensor.matmul(ps2[:, h, 0:D], hid_t[h][:, c, :], M.w2[:, c, :], start=(c == 0), stop=(c == 1))
                ins.then_inc(second, 1)

            def sums(q, m):
                for h in two:
                    for part in (msg_l[q], msg_h[q]):
                        ins = nc.tensor.matmul(ps_a[q][:, 0:R + 1], part[:, h, :], oh[m][:, h, :],
                                               start=(h == 0 and part is msg_l[q]), stop=(h == 1 and part is msg_h[q]))
                ins.then_inc(summed, 1)

            def step(g, k, turn):
                q = k % 2
                w = pe.value_load(K.win_of[0:1, bass.ds((g + 2).value, 1)], min_val=0, max_val=W - 1)
                products(g + 1, 1 - q, *nth(turn, k, 1), 0, w, True)
                turn_hidden(g, 1, True)
                message(g, 0)
                products(g + 1, 1 - q, *nth(turn, k, 1), 1, w, True)
                turn_hidden(g + 1, 0, True)
                message(g, 1)
                at_least(pe, banked, g + 1)
                at_least(pe, rest_ready, g + 1)
                at_least(pe, oh_ready, g * 2 + 2)
                sums(1 - q, (k + 3) % 4)

            pe.sem_inc(summed, 1)
            pe.sem_inc(second, 1)
            w = pe.value_load(K.win_of[0:1, 1:2], min_val=0, max_val=W - 1)
            for h in two:
                products(ZERO, 0, 0, ZERO, h, w, False)
            turn_hidden(ZERO, 0, False)
            groups(pe, step)
            total, _ = steps(pe)
            pe.wait_ge(banked, total + 1)
            pe.wait_ge(rest_ready, total + 1)
            pe.wait_ge(oh_ready, total * 2 + 2)
            sums(1, 3)

        @block.scalar
        def _(act):
            def relu_turned(g, h, waits):
                at_least(act, turned, g * 2 + (h + 1))
                if waits:
                    at_least(act, second, g * 2 + h)
                nc.scalar.activation(hid_t[h][:, :, :], ps_t[h][:, 0:2, :], ACT.Relu).then_inc(relu1, 1)

            def step(g, k, turn):
                q = k % 2
                relu_turned(g, 1, True)
                relu_turned(g + 1, 0, True)
                at_least(act, biased, g + 2)
                at_least(act, summed, g + 1)
                nc.scalar.activation(msg_h[q][:, :, :], msg_b[:, :, :], ACT.Relu).then_inc(relu2, 1)

            relu_turned(ZERO, 0, False)
            groups(act, step)


def attend(nc, ctx, K, h, w_row, a_dram, s_dram):
    NB = (N + CHUNK - 1) // CHUNK
    with Part(nc, "attend", ctx) as p:
        w_sb = p.sb("w", [128, D])
        prod = p.sb("prod", [R, W, D])
        s_col, s_turned = p.sb("s_col", [R, W]), p.sb("s_turned", [W, R])
        low = p.sb("low", [R, 1])
        srel = p.sb("srel", [R, N])
        a_sb = [p.sb(f"a{u}", [R, N], BF16) for u in range(2)]
        member = p.sb("member", [R, N], BF16)
        masked = [p.sb(f"masked{u}", [R, N]) for u in range(2)]
        wt_t = p.sb("wt_t", [R, W, R])
        top, ntop, den, rden = ([p.sb(f"{n}{u}", [R, 1]) for u in range(2)] for n in ("top", "ntop", "den", "rden"))
        total = p.sb("total", [R, D])
        ps_s = p.ps("ps_s", [128, 512])
        ps_t = p.ps("ps_t", [128, 4, 512])
        ps_o = [p.ps(f"ps_o{u}", [128, 512]) for u in range(2)]
        w_in, scored, s_ready, s_out, s_stored, s_in, chain = (p.sem(n) for n in ("w_in", "scored", "s_ready", "s_out", "s_stored", "s_in", "chain"))
        topped, exped, weighted, turned, copied, product, done = (
            p.sem(n) for n in ("topped", "exped", "weighted", "turned", "copied", "product", "done"))
        a_in = [p.sem(f"a_in{u}") for u in range(2)]
        begun = p.sem("begun")
        block = p.block()
        GROUPS_K = [(g, min(4, W - 4 * g)) for g in range(NB)]

        def windows(eng, f):
            with eng.Fori(0, W // 2) as i:
                for u in range(2):
                    f(i * 2 + u, u, i)
            f(W - 1, 0, W // 2)

        @block.sync
        def _(sp):
            sp.dma_start(w_sb[:, :], w_row.to_broadcast([128, D])).then_inc(w_in, 16)
            sp.wait_ge(s_out, 1)
            sp.dma_start(s_dram.rearrange("(w p) -> w p", p=R), s_turned[:, :]).then_inc(s_stored, 16)
            sp.wait_ge(s_stored, 16)
            sp.dma_start(srel[:, :], s_dram.partition_broadcast(R)).then_inc(s_in, 16)

            def load(w, u, i):
                sp.wait_ge(weighted, w)
                sp.dma_start(a_sb[u][:, :], a_dram[bass.ds(w, 1), :, :].rearrange("a p n -> p (a n)")).then_inc(a_in[u], 16)
            windows(sp, load)

        @block.vector
        def _(dve):
            link = Chain(dve, chain)
            dve.wait_ge(w_in, 16)
            link(nc.vector.tensor_tensor(prod[:, :, :], h[:, :, :], w_sb[0:R, :].unsqueeze(1).to_broadcast([R, W, D]), ALU.mult))
            nc.vector.tensor_reduce(s_col[:, :], prod[:, :, :], AX.X, ALU.add).then_inc(scored, 1)
            dve.wait_ge(s_ready, 1)
            nc.vector.tensor_copy(s_turned[:, :], ps_s[0:W, 0:R]).then_inc(s_out, 1)
            dve.wait_ge(s_in, 16)
            link(nc.vector.tensor_reduce(low[:, :], srel[:, :], AX.X, ALU.min))
            link(nc.vector.tensor_scalar(srel[:, :], srel[:, :], low[:, 0:1], None, ALU.subtract))
            dve.sem_inc(weighted, 1)
            dve.sem_inc(done, 1)

            def window(w, u, i):
                dve.wait_ge(a_in[u], i * 16 + 16)
                link(nc.vector.tensor_scalar(member[:, :], a_sb[u][:, :], 1.0, None, ALU.min))
                dve.wait_ge(turned, w * NB)
                dve.sem_inc(begun, 1)
                link(nc.vector.tensor_tensor_reduce(out=masked[u][:, :], in0=member[:, :], in1=srel[:, :], scale=1.0, scalar=0.0,
                                                    op0=ALU.mult, op1=ALU.max, accum_out=top[u][:, 0:1]))
                nc.vector.tensor_scalar(ntop[u][:, :], top[u][:, :], -1.0, None, ALU.mult).then_inc(topped, 1)
                dve.wait_ge(exped, w + 1)
                ins = nc.vector.tensor_tensor_reduce(out=masked[u][:, :], in0=masked[u][:, :], in1=a_sb[u][:, :], scale=1.0, scalar=0.0,
                                                     op0=ALU.mult, op1=ALU.add, accum_out=den[u][:, 0:1])
                ins.then_inc(weighted, 1)
                dve.wait_ge(weighted, w + 2)
                link(nc.vector.tensor_scalar(den[u][:, :], den[u][:, :], 1e-20, None, ALU.max))
                link(nc.vector.reciprocal(rden[u][:, :], den[u][:, :]))
                dve.wait_ge(product, w + 1)
                nc.vector.scalar_tensor_tensor(out=at(K.x, w), in0=ps_o[u][0:R, 0:D], scalar=rden[u][:, 0:1], in1=at(K.x, w),
                                               op0=ALU.mult, op1=ALU.add).then_inc(done, 1)

            with dve.Fori(0, W // 2) as i:
                link.loop(i, 2 * 4)
                for u in range(2):
                    window(i * 2 + u, u, i)
            link.end(W // 2)
            window(W - 1, 0, W // 2)

        @block.scalar
        def _(act):
            act.sem_inc(copied, NB)

            def window(w, u, i):
                act.wait_ge(topped, w + 1)
                nc.scalar.activation(masked[u][:, :], masked[u][:, :], ACT.Exp, bias=ntop[u][:, 0:1]).then_inc(exped, 1)
                act.wait_ge(product, w)
                for g, n in GROUPS_K:
                    act.wait_ge(turned, w * NB + (NB + g + 1))
                    nc.scalar.copy(wt_t[:, 4 * g:4 * g + n, :], ps_t[0:R, g % 4, 0:n * R].rearrange("p (k r) -> p k r", r=R)).then_inc(copied, 1)
            windows(act, window)

        @block.tensor
        def _(pe):
            pe.wait_ge(scored, 1)
            nc.tensor.transpose(ps_s[0:W, 0:R], s_col[:, :], K.ident[0:R, 0:R]).then_inc(s_ready, 1)
            pe.sem_inc(turned, NB)

            def window(w, u, i):
                pe.wait_ge(weighted, w + 2)
                for g, n in GROUPS_K:
                    pe.wait_ge(copied, w * NB + (NB + g - 3))
                    for k in range(n):
                        c = 4 * g + k
                        ins = nc.tensor.transpose(ps_t[0:R, g % 4, k * R:(k + 1) * R], masked[u][:, c * R:(c + 1) * R], K.ident[0:R, 0:R])
                    ins.then_inc(turned, 1)
                pe.wait_ge(copied, w * NB + 2 * NB)
                pe.wait_ge(done, w)
                for k in range(W):
                    ins = nc.tensor.matmul(ps_o[u][0:R, 0:D], wt_t[:, k, :], h[:, k, :], start=(k == 0), stop=(k == W - 1))
                ins.then_inc(product, 1)
            windows(pe, window)


class Layer:

    def __init__(self, p):
        self.w_sr, self.w_e, self.w2 = p.sb("w_sr", [D, 2 * H]), p.sb("w_e", [D, H]), p.sb("w2", [128, 2, D])
        self.we_h, self.we_l = p.sb("we_h", [D, H], F32R), p.sb("we_l", [D, H], F32R)
        self.b2, self.b_r = p.sb("b2", [128, D]), p.sb("b_r", [R, H])
        self.send, self.recv = p.sb("send", [R, W, H]), [p.sb("recv", [R, H])]
        self.recv_h, self.recv_l = p.sb("recv_h", [R, W, H], F32R), p.sb("recv_l", [R, W, H], F32R)
        self.agg = p.sb("agg", [D, N])


def scaled_by_dinv(K, g):
    return lambda p: Finish(0, lambda nc, link, w, product: nc.vector.tensor_scalar(
        at(g, w), product, K.dinv[:, bass.ds(w, 1)], None, ALU.mult))


def plus_row(out, row):
    return lambda p: Finish(0, lambda nc, link, w, product: nc.vector.tensor_tensor(at(out, w), product, row[0:R, :], ALU.add))


def into_tables(M):
    def f(nc, link, w, product):
        link(nc.vector.tensor_tensor(M.recv[0][:, :], product[:, H:2 * H], M.b_r[:, :], ALU.add))
        link(nc.vector.tensor_copy(at(M.recv_h, w), M.recv[0][:, :]))
        link(nc.vector.tensor_tensor(at(M.recv_l, w), M.recv[0][:, :], at(M.recv_h, w).bitcast(F32), ALU.subtract))
        return nc.vector.tensor_copy(at(M.send, w), product[:, 0:H])
    return lambda p: Finish(3, f)


def turn_weights(nc, ctx, K, name, w, out):
    with Part(nc, name, ctx) as p:
        raw, ps = p.sb("raw", [D, D]), p.ps("ps", [128, 512])
        loaded, turned, copied = p.sem("loaded"), p.sem("turned"), p.sem("copied")
        block = p.block()

        @block.sync
        def _(sp):
            sp.dma_start(raw[:, :], w).then_inc(loaded, 16)

        @block.tensor
        def _(pe):
            pe.wait_ge(loaded, 16)
            nc.tensor.transpose(ps[:, 0:D], raw[:, :], K.ident[:, :]).then_inc(turned, 1)

        @block.vector
        def _(dve):
            dve.wait_ge(turned, 1)
            nc.vector.tensor_copy(out[:, :], ps[:, 0:D]).then_inc(copied, 1)
            dve.wait_ge(copied, 1)


def store_result(nc, ctx, K, out):
    with Part(nc, "result", ctx) as p:
        stored = p.sem("stored")
        block = p.block()

        @block.sync
        def _(sp):
            sp.dma_start(out.rearrange("(w p) d -> p w d", p=R), K.x[:, :, :]).then_inc(stored, 16)
            sp.wait_ge(stored, 16)


def gcn(nc, ctx, K, name, at_dram, w1, b1, w2, b2, a_dram=None, turn=False):
    with Part(nc, name, ctx) as p:
        w_sb, g, hid = p.sb("w", [D, D]), p.sb("g", [R, W, D]), p.sb("hid", [R, W, D])
        norm_moments(nc, ctx, K, name + "_norm", K.x)
        for n, (w, b) in enumerate(((w1, b1), (w2, b2))):
            if turn:
                turn_weights(nc, ctx, K, f"{name}_turn{n}", w, w_sb)
            project(nc, ctx, K, f"{name}_lin{n}", hid if n else K.x, w_sb[:, :], D, scaled_by_dinv(K, g),
                    norm=not n, relu=not n, loads=() if turn else ((w_sb[:, :], w),))
            spread(nc, ctx, K, f"{name}_spread{n}", g, b, K.x if n else hid, at_dram, a_dram=None if n else a_dram,
                   relu=not n, residual=K.x if n else None)


def bass_graph_layers(nc, io, out):
    slot_meta = nc.dram_tensor("slot_meta", (SLOTS, 2), I32, kind="Internal").ap()
    slot_raw = nc.dram_tensor("slot_raw", (SLOTS, D), F32, kind="Internal").ap()
    rel_rows = nc.dram_tensor("rel_rows", (TILES, 128), F32, kind="Internal").ap()
    a_dram = nc.dram_tensor("a_rows", (W, R, N), BF16, kind="Internal").ap()
    at_dram = nc.dram_tensor("a_cols", (W, R, N), BF16, kind="Internal").ap()
    edges = nc.dram_tensor("edges", (D, TILES, 2, 128), F32, kind="Internal").ap()
    p_dram = nc.dram_tensor("send_rows", (N, H), F32, kind="Internal").ap()
    s_dram = nc.dram_tensor("scores", (N,), F32, kind="Internal").ap()
    with ExitStack() as kept:
        sorting = ExitStack()
        K = Kept(nc, kept, sorting)
        with sorting, Scope(nc) as ctx:
            build_constants(nc, ctx, K)
            sort_edges(nc, ctx, K, io["src"], io["dst"], slot_meta, slot_raw)
            scatter_meta(nc, ctx, K, slot_meta)
            read_slots(nc, ctx, K, slot_meta, rel_rows, io["x"])
            count_edges(nc, ctx, K, io["edge_attr_128"], slot_raw, a_dram)
            sums_to_degrees(nc, ctx, K)
        with Scope(nc) as ctx:
            gcn(nc, ctx, K, "l0", at_dram, io["L0_gnn_W1"], io["L0_gnn_b1"], io["L0_gnn_W2"], io["L0_gnn_b2"], a_dram=a_dram)
        with Scope(nc) as ctx:
            encode_edges(nc, ctx, K, slot_raw, io["L1_gnn_w_edge"], io["L1_gnn_b_edge"], edges)
        with Part(nc, "l1", None) as p:
            M = Layer(p)
            n_sb, t_sb = p.sb("n", [R, W, D]), p.sb("t", [R, W, D])
            w_sb, w2_sb, b_sb = p.sb("w", [D, D]), p.sb("w_upd", [D, D]), p.sb("b", [128, D])
            with Scope(nc) as ctx:
                norm_moments(nc, ctx, K, "l1_norm", K.x)
                project(nc, ctx, K, "l1_node", K.x, w_sb[:, :], D, plus_row(t_sb, b_sb), norm=True, relu=True,
                        loads=((w_sb[:, :], io["L1_gnn_w_node"]), (b_sb[:, :], io["L1_gnn_b_node"].partition_broadcast(128))))
                gelu_nodes(nc, ctx, K, t_sb)
                norm_moments(nc, ctx, K, "l1_norm_n", t_sb)
                norm_apply(nc, ctx, K, "l1_apply", t_sb, n_sb, scale=io["L1_gnn_ln_n_scale"], offset=io["L1_gnn_ln_n_offset"])
            for l in range(3):
                with Scope(nc) as ctx:
                    message_weights(nc, ctx, K, f"l1_w{l}", M, io["L1_gnn_msg_w1"][l], io["L1_gnn_msg_b1"][l], io["L1_gnn_msg_w2"][l],
                                    io["L1_gnn_msg_b2"][l], io["L1_gnn_ln_e_scale"], io["L1_gnn_ln_e_offset"])
                    project(nc, ctx, K, f"l1_tables{l}", n_sb, M.w_sr[:, :], 2 * H, into_tables(M))
                    store_senders(nc, ctx, K, f"l1_send{l}", M, p_dram)
                    messages(nc, ctx, K, f"l1_msg{l}", M, p_dram, edges, rel_rows)
                    upd = io["L1_gnn_upd_w"][l]
                    project(nc, ctx, K, f"l1_upd{l}", n_sb, w_sb[:, :], D, plus_row(t_sb, b_sb), extra=w2_sb[:, :], extra_sb=M.agg,
                            loads=((w_sb[:, :], upd[0:D, :]), (w2_sb[:, :], upd[D:2 * D, :]),
                                   (b_sb[:, :], io["L1_gnn_upd_b"][l].partition_broadcast(128))))
                    norm_moments(nc, ctx, K, f"l1_norm{l}", t_sb)
                    norm_apply(nc, ctx, K, f"l1_add{l}", t_sb, t_sb, scale=io["L1_gnn_ln_scale"][l], offset=io["L1_gnn_ln_offset"][l],
                               add_to=n_sb)
            with Scope(nc) as ctx:
                add_nodes(nc, ctx, K, n_sb)
        with Scope(nc) as ctx, Part(nc, "l2", None) as p:
            h_sb = p.sb("h", [R, W, D])
            norm_moments(nc, ctx, K, "l2_norm", K.x)
            norm_apply(nc, ctx, K, "l2_apply", K.x, h_sb, relu=True)
            attend(nc, ctx, K, h_sb, io["L2_gnn_W"], a_dram, s_dram)
        with Scope(nc) as ctx:
            gcn(nc, ctx, K, "l3", at_dram, io["L3_gnn_W1"], io["L3_gnn_b1"], io["L3_gnn_W2"], io["L3_gnn_b2"], turn=True)
            store_result(nc, ctx, K, out)


def add_nodes(nc, ctx, K, n_sb):
    with Part(nc, "l1_out", ctx) as p:
        done = p.sem("done")
        block = p.block()

        @block.vector
        def _(dve):
            nc.vector.tensor_tensor(K.x[:, :, :], K.x[:, :, :], n_sb[:, :, :], ALU.add).then_inc(done, 1)
            dve.wait_ge(done, 1)


_INS = ["x", "src", "dst", "edge_attr_128", "L0_gnn_W1", "L0_gnn_b1", "L0_gnn_W2", "L0_gnn_b2",
        "L1_gnn_w_node", "L1_gnn_b_node", "L1_gnn_w_edge", "L1_gnn_b_edge", "L1_gnn_ln_n_scale", "L1_gnn_ln_n_offset",
        "L1_gnn_ln_e_scale", "L1_gnn_ln_e_offset", "L1_gnn_msg_w1", "L1_gnn_msg_b1", "L1_gnn_msg_w2", "L1_gnn_msg_b2",
        "L1_gnn_upd_w", "L1_gnn_upd_b", "L1_gnn_ln_scale", "L1_gnn_ln_offset", "L2_gnn_W",
        "L3_gnn_W1", "L3_gnn_b1", "L3_gnn_W2", "L3_gnn_b2"]


def kernel(**inputs):
    import numpy as np
    import concourse.bacc as bacc
    from concourse.bass_utils import run_bass_kernel_spmd

    nc = bacc.Bacc("TRN2", target_bir_lowering=False, num_devices=1)
    arrays, io = {}, {}
    for name in _INS:
        a = np.ascontiguousarray(inputs[name])
        arrays[f"in_{name}"] = a
        io[name] = nc.dram_tensor(f"in_{name}", a.shape, mybir.dt.from_np(a.dtype), kind="ExternalInput").ap()
    out = nc.dram_tensor("out_0", (N, D), F32, kind="ExternalOutput").ap()
    bass_graph_layers(nc, io, out)
    r = run_bass_kernel_spmd(nc, [arrays], core_ids=[0])
    return r.results[0]["out_0"]
```

```python
from contextlib import ExitStack

import concourse.bass as bass
from concourse import mybir

F32 = mybir.dt.float32
I32 = mybir.dt.int32
I16 = mybir.dt.int16
F32R = mybir.dt.float32r
BF16 = mybir.dt.bfloat16
ALU = mybir.AluOpType
ACT = mybir.ActivationFunctionType
AX = mybir.AxisListType

N, E, D = 3125, 50000, 128
R = 125
W = N // R
NP = N + 128 - R
T = E // R
G = 256
MAX_GROUPS = E // G + W
GROUPS = -(-(MAX_GROUPS + 8) // 4) * 4
TILES = 2 * GROUPS
assert T % 16 == 0 and D == 128
H = 2 * D
LN_EPS = 1e-5
CHUNK = 500
U = 5
NC = W // U


class Index:

    def __init__(self, x, scale=1, offset=0):
        self.x, self.scale, self.offset = x, scale, offset

    def __add__(self, n):
        return Index(self.x, self.scale, self.offset + n)

    def __sub__(self, n):
        return self + -n

    def __mul__(self, n):
        return Index(self.x, self.scale * n, self.offset * n)

    @property
    def value(self):
        if self.x is None:
            return self.offset
        v = self.x if self.scale == 1 else self.x * self.scale
        return v + self.offset if self.offset else v


ZERO = Index(None)


def at_least(eng, sem, index):
    if index.x is not None or index.offset > 0:
        eng.wait_ge(sem, index.value)


class Chain:

    def __init__(self, eng, sem):
        self.eng, self.sem, self.n, self.i, self.per, self.k = eng, sem, 0, None, 0, 0

    def loop(self, i, per):
        self.i, self.per, self.k = i, per, 0

    def end(self, trips):
        assert self.k == self.per, (self.k, self.per)
        self.n += self.per * trips
        self.i = None

    def __call__(self, ins):
        ins.then_inc(self.sem, 1)
        if self.i is None:
            self.n += 1
            self.eng.wait_ge(self.sem, self.n)
        else:
            self.k += 1
            self.eng.wait_ge(self.sem, self.i * self.per + (self.n + self.k))


class Scope:

    def __init__(self, nc):
        self.nc, self.sems = nc, []

    def __enter__(self):
        return self

    def semaphore(self, name):
        self.sems.append(self.nc.alloc_semaphore(name=name))
        return self.sems[-1]

    def __exit__(self, *_):
        self.nc.clear_and_free_semaphores(self.sems)
        self.nc.all_engine_barrier()


class Part:

    def __init__(self, nc, name, ctx):
        self.nc, self.name, self.ctx, self.own = nc, name, ctx, ExitStack()

    def __enter__(self):
        return self

    def __exit__(self, *_):
        self.own.close()

    def sb(self, name, shape, dt=F32):
        return self.own.enter_context(self.nc.sbuf_tensor(f"{self.name}_{name}", shape, dt))

    def ps(self, name, shape, dt=F32):
        return self.own.enter_context(self.nc.psum_tensor(f"{self.name}_{name}", shape, dt))

    def sem(self, name):
        return self.ctx.semaphore(f"{self.name}_{name}")

    def block(self):
        return self.own.enter_context(self.nc.Block())


def wide(ap, n):
    return ap.unsqueeze(2).to_broadcast([ap.shape[0], ap.shape[1], n])


def build_constants(nc, ctx, K):
    with Part(nc, "const", ctx) as p:
        made, link_p, link_v = p.sem("made"), p.sem("link_p"), p.sem("link_v")
        block = p.block()

        @block.gpsimd
        def _(pool):
            link = Chain(pool, link_p)
            link(nc.gpsimd.memset(K.ident[:, :], 0.0))
            link(nc.gpsimd.affine_select(out=K.ident[:, :], in_=K.ident[:, :], compare_op=ALU.not_equal,
                                         fill=1.0, base=0, pattern=[[-1, 128]], channel_multiplier=1))
            link(nc.gpsimd.memset(K.below[:, :], 1.0))
            link(nc.gpsimd.affine_select(out=K.below[:, :], in_=K.below[:, :], compare_op=ALU.is_gt,
                                         fill=0.0, base=0, pattern=[[1, 128]], channel_multiplier=-1))
            nc.gpsimd.iota(K.iota_i[:, :], pattern=[[1, NP]], base=0, channel_multiplier=0).then_inc(made, 1)
            nc.gpsimd.iota(K.lane_i[:, :], pattern=[[0, 1]], base=0, channel_multiplier=1).then_inc(made, 1)

        @block.vector
        def _(dve):
            nc.vector.memset(K.ones[:, :], 1.0)
            dve.wait_ge(made, 2)
            nc.vector.tensor_copy(K.iota16[:, :], K.iota_i[:, :])
            nc.vector.tensor_copy(K.iota_f[:, :], K.iota_i[:, 0:128])
            nc.vector.tensor_copy(K.lane_f[:, :], K.lane_i[:, :])
            dve.wait_ge(link_p, 4)
            nc.vector.tensor_copy(K.ident16[:, :], K.ident[:, :])


class Kept:

    def __init__(self, nc, ctx, sorting):
        def sb(name, shape, dt=F32, ctx=ctx):
            return ctx.enter_context(nc.sbuf_tensor(name, shape, dt))

        self.ident, self.ident16 = sb("ident", [128, 128]), sb("ident16", [128, 128], BF16)
        self.below, self.ones = sb("below", [128, 128]), sb("ones", [128, 512])
        self.iota_f = sb("iota_f", [128, 128])
        self.lane_i, self.lane_f = sb("lane_i", [128, 1], I32), sb("lane_f", [128, 1])
        self.bases = sb("bases", [128, W + 1], I32)
        self.unsorted, self.first_of = sb("unsorted", [128, 1], I32), sb("first_of", [128, GROUPS], I32)
        self.sender, self.rel = sb("sender", [128, TILES], I32), sb("rel", [128, TILES])
        self.win_of = sb("win_of", [128, 1 + GROUPS], I32)
        self.deg, self.dinv = sb("deg", [128, W, -(-NP // CHUNK)]), sb("dinv", [R, W])
        self.x, self.mean, self.rstd = sb("x", [R, W, D]), sb("mean", [R, W]), sb("rstd", [R, W])
        self.iota_i, self.iota16 = sb("iota_i", [128, NP], I32, sorting), sb("iota16", [128, NP], I16, sorting)
        self.sender_f, self.win = sb("sender_f", [128, TILES], F32, sorting), sb("win", [R, T], F32, sorting)
        self.tot, self.before = sb("tot", [R, W], F32, sorting), sb("before", [R, W], F32, sorting)
        self.node0, self.clamped, self.early = (sb(n, [128, 2], F32, sorting) for n in ("node0", "clamped", "early"))
        self.row_idx = sb("row_idx", [128, 2], I32, sorting)


def sort_edges(nc, ctx, K, src, dst):
    with Part(nc, "sort", ctx) as p:
        dst_i, next_i = p.sb("dst_i", [R, T], I32), p.sb("next_i", [R, T], I32)
        dst_f, quot_i = p.sb("dst_f", [R, T]), p.sb("quot_i", [R, T], I32)
        rel, low, high, falls, mask = (p.sb(n, [R, T]) for n in ("rel", "low", "high", "falls", "mask"))
        fallen = p.sb("fallen", [R, 1])
        cnt, cnt_i, end, groups, begin = (p.sb("cnt", [128, W]), p.sb("cnt_i", [128, W], I32), p.sb("end", [128, W]),
                                          p.sb("groups", [128, W]), p.sb("begin", [128, W]))
        shift, rise = p.sb("shift", [128, W + 1]), p.sb("rise", [128, W])
        base_f = p.sb("base_f", [128, W])
        past, part = p.sb("past", [128, W]), p.sb("part", [128, W])
        g_col, wins, jump, begins = (p.sb(n, [128, 2]) for n in ("g_col", "wins", "jump", "begins"))
        ps_before, ps_cnt, ps_flag, ps_row = (p.ps(n, [128, 512]) for n in ("ps_before", "ps_cnt", "ps_flag", "ps_row"))
        loaded, summed, tots, flagged, placed, rowed, chain = (
            p.sem(n) for n in ("loaded", "summed", "tots", "flagged", "placed", "rowed", "chain"))
        nexts = p.sem("nexts")
        block = p.block()

        @block.sync
        def _(sp):
            sp.wait_ge(nexts, 1)
            sp.dma_start(dst_i[:, :], dst.rearrange("(p t) -> p t", p=R)).then_inc(loaded, 16)
            sp.dma_start(next_i[0:R - 1, :], dst[1:1 + (R - 1) * T].rearrange("(p t) -> p t", t=T)).then_inc(loaded, 16)
            sp.dma_start(next_i[R - 1:R, 0:T - 1], dst[1 + (R - 1) * T:E].rearrange("(p t) -> p t", p=1)).then_inc(loaded, 16)

        @block.tensor
        def _(pe):
            pe.wait_ge(flagged, 1)
            nc.tensor.matmul(ps_flag[:, 0:1], K.ones[0:R, 0:128], fallen[:, :], start=True, stop=True).then_inc(summed, 1)
            pe.wait_ge(tots, 1)
            nc.tensor.matmul(ps_before[0:R, 0:W], K.below[0:R, 0:R], K.tot[:, :], start=True, stop=True).then_inc(summed, 1)
            nc.tensor.matmul(ps_cnt[:, 0:W], K.ones[0:R, 0:128], K.tot[:, :], start=True, stop=True).then_inc(summed, 1)
            pe.wait_ge(placed, 1)
            for k, t in enumerate((wins, K.clamped)):
                for a in range(2):
                    ins = nc.tensor.transpose(ps_row[0:1, (2 * k + a) * 128:(2 * k + a + 1) * 128], t[:, a:a + 1], K.ident[:, :])
            ins.then_inc(rowed, 1)

        @block.vector
        def _(dve):
            link = Chain(dve, chain)
            nc.vector.memset(next_i[:, :], N).then_inc(nexts, 1)
            link(nc.vector.tensor_scalar(g_col[:, 0:1], K.lane_f[:, :], 0.0, None, ALU.add))
            link(nc.vector.tensor_scalar(g_col[:, 1:2], K.lane_f[:, :], 128.0, None, ALU.add))
            dve.wait_ge(loaded, 48)
            link(nc.vector.tensor_tensor(falls[:, :], dst_i[:, :], next_i[:, :], ALU.is_gt))
            nc.vector.tensor_reduce(fallen[:, :], falls[:, :], AX.X, ALU.add).then_inc(flagged, 1)
            link(nc.vector.tensor_copy(dst_f[:, :], dst_i[:, :]))
            link(nc.vector.tensor_scalar(quot_i[:, :], dst_f[:, :], 1.0 / R, None, ALU.mult))
            link(nc.vector.tensor_copy(K.win[:, :], quot_i[:, :]))
            link(nc.vector.scalar_tensor_tensor(out=rel[:, :], in0=K.win[:, :], scalar=-float(R), in1=dst_f[:, :],
                                                op0=ALU.mult, op1=ALU.add))
            link(nc.vector.tensor_scalar(low[:, :], rel[:, :], 0.0, None, ALU.is_lt))
            link(nc.vector.tensor_scalar(high[:, :], rel[:, :], float(R), None, ALU.is_ge))
            link(nc.vector.tensor_tensor(high[:, :], high[:, :], low[:, :], ALU.subtract))
            link(nc.vector.tensor_tensor(K.win[:, :], K.win[:, :], high[:, :], ALU.add))
            with dve.Fori(0, W) as v:
                link.loop(v, 1)
                link(nc.vector.tensor_scalar(mask[:, :], K.win[:, :], K.iota_f[0:R, bass.ds(v, 1)], 0.0, ALU.is_equal, ALU.add,
                                             accum_out=K.tot[:, bass.ds(v, 1)]))
            link.end(W)
            dve.sem_inc(tots, 1)
            dve.wait_ge(summed, 3)
            link(nc.vector.tensor_copy(K.unsorted[:, :], ps_flag[:, 0:1]))
            link(nc.vector.tensor_copy(cnt[:, :], ps_cnt[:, 0:W]))
            link(nc.vector.tensor_scalar(cnt_i[:, :], cnt[:, :], float(G - 1), None, ALU.add))
            link(nc.vector.tensor_scalar(cnt_i[:, :], cnt_i[:, :], 8, None, ALU.logical_shift_right))
            link(nc.vector.tensor_scalar(groups[:, :], cnt_i[:, :], 1.0, None, ALU.max))
            link(nc.vector.tensor_tensor_scan(end[:, :], K.ones[:, 0:W], groups[:, :], 0.0, ALU.mult, ALU.add))
            link(nc.vector.memset(K.bases[:, :], 0))
            link(nc.vector.tensor_copy(K.bases[:, 1:W + 1], end[:, :]))
            link(nc.vector.tensor_tensor(base_f[:, :], end[:, :], groups[:, :], ALU.subtract))
            link(nc.vector.tensor_tensor_scan(begin[:, :], K.ones[:, 0:W], cnt[:, :], 0.0, ALU.mult, ALU.add))
            link(nc.vector.tensor_tensor(begin[:, :], begin[:, :], cnt[:, :], ALU.subtract))
            link(nc.vector.tensor_tensor(K.before[:, :], begin[0:R, :], ps_before[0:R, 0:W], ALU.add))
            link(nc.vector.memset(shift[:, :], 0.0))
            link(nc.vector.scalar_tensor_tensor(out=shift[:, 0:W], in0=base_f[:, :], scalar=-float(G), in1=begin[:, :],
                                                op0=ALU.mult, op1=ALU.add))
            link(nc.vector.memset(rise[:, :], 0.0))
            link(nc.vector.tensor_tensor(rise[:, 0:W - 1], shift[:, 1:W], shift[:, 0:W - 1], ALU.subtract))
            for a in range(2):
                link(nc.vector.tensor_scalar(past[:, :], end[:, :], g_col[:, a:a + 1], 0.0, ALU.is_le, ALU.add, accum_out=wins[:, a:a + 1]))
                link(nc.vector.tensor_tensor(part[:, :], past[:, :], rise[:, :], ALU.mult))
                link(nc.vector.tensor_reduce(jump[:, a:a + 1], part[:, :], AX.X, ALU.add))
            link(nc.vector.tensor_scalar(wins[:, :], wins[:, :], float(W - 1), None, ALU.min))
            link(nc.vector.tensor_scalar(K.node0[:, :], wins[:, :], float(R), None, ALU.mult))
            link(nc.vector.scalar_tensor_tensor(out=begins[:, :], in0=g_col[:, :], scalar=float(G), in1=jump[:, :],
                                                op0=ALU.mult, op1=ALU.add))
            link(nc.vector.tensor_scalar(K.clamped[:, :], begins[:, :], float(E - G), None, ALU.min))
            link(nc.vector.tensor_copy(K.row_idx[:, :], K.clamped[:, :]))
            nc.vector.tensor_tensor(K.early[:, :], begins[:, :], K.clamped[:, :], ALU.subtract).then_inc(placed, 1)
            dve.wait_ge(rowed, 1)
            link(nc.vector.memset(K.win_of[0:1, 0:1], 0))
            link(nc.vector.tensor_copy(K.win_of[0:1, 1:1 + GROUPS], ps_row[0:1, 0:GROUPS]))
            link(nc.vector.tensor_copy(K.first_of[0:1, :], ps_row[0:1, 256:256 + GROUPS]))


def reorder_edges(nc, ctx, K, src, dst, attr, by_window):
    B = 8
    s_src, s_dst, s_attr = by_window
    with Part(nc, "reorder", ctx) as p:
        src_i, dst_i = p.sb("src_i", [R, T], I32), p.sb("dst_i", [R, T], I32)
        mask, count, rank, term = (p.sb(n, [R, T]) for n in ("mask", "count", "rank", "term"))
        place = p.sb("place", [R, T], I32)
        rows, ends = ([p.sb(f"{n}{h}", [R, B], I32) for h in range(2)] for n in ("rows", "ends"))
        senders = [p.sb(f"senders{h}", [R, B], I32) for h in range(2)]
        raws = [p.sb(f"raws{h}", [R, B, D]) for h in range(2)]
        loaded, chain, begun = p.sem("loaded"), p.sem("chain"), p.sem("begun")
        rows_in = [p.sem(f"rows_in{h}") for h in range(2)]
        staged = [p.sem(f"staged{h}") for h in range(2)]
        scattered = [p.sem(f"scattered{h}") for h in range(2)]
        block = p.block()
        raw = attr.rearrange("(p t) d -> p t d", p=R)

        def unsorted(eng):
            return eng.value_load(K.unsorted[0:1, 0:1], min_val=0, max_val=E) > 0

        @block.sync
        def _(sp):
            with sp.If(unsorted(sp)):
                sp.dma_start(src_i[:, :], src.rearrange("(p t) -> p t", p=R)).then_inc(loaded, 16)
                sp.dma_start(dst_i[:, :], dst.rearrange("(p t) -> p t", p=R)).then_inc(loaded, 16)
                for h in range(2):
                    sp.dma_start(raws[h][:, :, :], raw[:, h * B:(h + 1) * B, :]).then_inc(rows_in[h], 16)
                with sp.Fori(1, T // (2 * B)) as i:
                    for h in range(2):
                        sp.wait_ge(scattered[h], i * (48 * B))
                        sp.dma_start(raws[h][:, :, :], raw[:, bass.ds(i * (2 * B) + h * B, B), :]).then_inc(rows_in[h], 16)

        @block.vector
        def _(dve):
            with dve.If(unsorted(dve)):
                link = Chain(dve, chain)
                link(nc.vector.memset(rank[:, :], -1.0))
                with dve.Fori(0, W) as v:
                    link.loop(v, 6)
                    link(nc.vector.tensor_scalar(mask[:, :], K.win[:, :], K.iota_f[0:R, bass.ds(v, 1)], None, ALU.is_equal))
                    link(nc.vector.tensor_tensor_scan(count[:, :], K.ones[0:R, 0:T], mask[:, :], 0.0, ALU.mult, ALU.add))
                    link(nc.vector.tensor_tensor(term[:, :], mask[:, :], count[:, :], ALU.mult))
                    link(nc.vector.tensor_tensor(rank[:, :], rank[:, :], term[:, :], ALU.add))
                    link(nc.vector.tensor_scalar(term[:, :], mask[:, :], K.before[:, bass.ds(v, 1)], None, ALU.mult))
                    link(nc.vector.tensor_tensor(rank[:, :], rank[:, :], term[:, :], ALU.add))
                link.end(W)
                link(nc.vector.tensor_copy(place[:, :], rank[:, :]))
                dve.wait_ge(loaded, 32)

                def stage(h, columns):
                    for out, table in ((rows, place), (senders, src_i), (ends, dst_i)):
                        nc.vector.tensor_copy(out[h][:, :], table[:, columns]).then_inc(staged[h], 1)

                for h in range(2):
                    stage(h, slice(h * B, (h + 1) * B))
                with dve.Fori(1, T // (2 * B)) as i:
                    for h in range(2):
                        dve.wait_ge(scattered[h], i * (48 * B))
                        stage(h, bass.ds(i * (2 * B) + h * B, B))

        @block.gpsimd
        def _(pool):
            with pool.If(unsorted(pool)):
                with pool.Fori(0, T // (2 * B)) as i:
                    for h in range(2):
                        pool.wait_ge(rows_in[h], i * 16 + 16)
                        pool.sem_inc(begun, 1)
                        pool.wait_ge(staged[h], i * 3 + 3)
                        pool.sem_inc(begun, 1)
                        for b in range(B):
                            for out, vals in ((s_attr, raws[h][:, b, :]), (s_src, senders[h][:, b:b + 1]), (s_dst, ends[h][:, b:b + 1])):
                                pool.indirect_dma_start(out, bass.IndirectOffsetOnAxis(ap=rows[h][:, b:b + 1], axis=0),
                                                        vals, None).then_inc(scattered[h], 16)
                for h in range(2):
                    pool.wait_ge(scattered[h], 48 * T // 2)


def read_slots(nc, ctx, K, given, by_window, rel_rows, x_in):
    A = (128, GROUPS - 128)
    with Part(nc, "slots", ctx) as p:
        both = [p.sb(f"both{a}", [128, 2, G], I32) for a in range(2)]
        vals = [p.sb(f"vals{a}", [128, 2, G]) for a in range(2)]
        here, far = ([p.sb(f"{n}{a}", [128, G]) for a in range(2)] for n in ("here", "far"))
        iota = p.sb("iota", [128, G])
        ps = p.ps("ps", [128, 4, 512])
        chain = p.sem("chain")
        gathered, ready, turned, stored, xin = (p.sem(n) for n in ("gathered", "ready", "turned", "stored", "xin"))
        block = p.block()

        @block.gpsimd
        def _(pool):
            def gather(src, dst):
                for a, n in enumerate(A):
                    for k, table in enumerate((src, dst)):
                        pool.indirect_dma_start(both[a][0:n, k, :], None, table.rearrange("(e a) -> e a", a=1),
                                                bass.IndirectOffsetOnAxis(ap=K.row_idx[0:n, a:a + 1], axis=0)).then_inc(gathered, 16)

            unsorted = pool.value_load(K.unsorted[0:1, 0:1], min_val=0, max_val=E)
            with pool.If(unsorted > 0):
                gather(by_window[0], by_window[1])
            with pool.Else():
                gather(given[0], given[1])
            pool.wait_ge(gathered, 64)

        @block.sync
        def _(sp):
            sp.dma_start(K.x[:, :, :], x_in.rearrange("(w p) d -> p w d", p=R)).then_inc(xin, 16)
            for a, n in enumerate(A):
                sp.wait_ge(ready, a + 1)
                sp.dma_start(rel_rows[a * 128:a * 128 + n, :], vals[a][0:n, 1, :]).then_inc(stored, 16)
            sp.wait_ge(xin, 16)
            sp.wait_ge(stored, 32)

        @block.vector
        def _(dve):
            link = Chain(dve, chain)
            link(nc.vector.tensor_copy(iota[:, :], K.iota_i[:, 0:G]))
            dve.wait_ge(gathered, 64)
            for a, n in enumerate(A):
                link(nc.vector.tensor_copy(vals[a][0:n, :, :], both[a][0:n, :, :]))
                rel = vals[a][0:n, 1, :]
                link(nc.vector.tensor_scalar(rel, rel, K.node0[0:n, a:a + 1], 1.0, ALU.subtract, ALU.add))
                link(nc.vector.tensor_scalar(here[a][0:n, :], iota[0:n, :], K.early[0:n, a:a + 1], None, ALU.is_ge))
                link(nc.vector.tensor_tensor(rel, rel, here[a][0:n, :], ALU.mult))
                link(nc.vector.tensor_scalar(far[a][0:n, :], rel, float(R), None, ALU.is_le))
                link(nc.vector.tensor_tensor(rel, rel, far[a][0:n, :], ALU.mult))
                nc.vector.tensor_scalar(rel, rel, 1.0, None, ALU.subtract).then_inc(ready, 1)
            dve.wait_ge(turned, 1)
            for k, out in enumerate((K.sender_f, K.rel)):
                view = out[:, :].rearrange("p (g h) -> p h g", h=2)
                for h in range(2):
                    last = nc.vector.tensor_copy(view[:, h, :], ps[:, 2 * k + h, 0:GROUPS])
            link(last)
            link(nc.vector.tensor_copy(K.sender[:, :], K.sender_f[:, :]))

        @block.tensor
        def _(pe):
            pe.wait_ge(ready, 2)
            for k in range(2):
                for h in range(2):
                    for a, n in enumerate(A):
                        last = nc.tensor.transpose(ps[:, 2 * k + h, a * 128:a * 128 + n], vals[a][0:n, k, h * 128:(h + 1) * 128],
                                                   K.ident[0:n, 0:n])
            last.then_inc(turned, 1)


def count_edges(nc, ctx, K, a_dram):
    NB = -(-NP // CHUNK)
    with Part(nc, "count", ctx) as p:
        oh_s, oh_r = p.sb("oh_s", [128, 4, NP], BF16), p.sb("oh_r", [128, 4, 128], BF16)
        a_sb = [p.sb(f"a_sb{u}", [128, NP], BF16) for u in range(2)]
        ps = p.ps("ps", [128, NB, 512])
        ready, used, counted = (p.sem(n) for n in ("ready", "used", "counted"))
        stored = [p.sem(f"stored{u}") for u in range(2)]
        taken = [p.sem(f"taken{c}") for c in range(NB)]
        block = p.block()

        def bounds(eng, w):
            return (eng.value_load(K.bases[0:1, bass.ds(w, 1)], min_val=0, max_val=MAX_GROUPS),
                    eng.value_load(K.bases[0:1, bass.ds(w + 1, 1)], min_val=1, max_val=MAX_GROUPS))

        ACT_BANKS, DVE_BANKS = [c for c in range(NB) if c not in (3, 5)], (3, 5)

        def take(eng, w, u, n, banks):
            eng.wait_ge(stored[u], n * 16 + 16)
            for c in banks:
                cols = slice(c * CHUNK, min(c * CHUNK + CHUNK, NP))
                rows, bank, total = a_sb[u][:, cols], ps[:, c, 0:cols.stop - cols.start], K.deg[:, bass.ds(w, 1), c]
                eng.wait_ge(counted, w * NB + (c + 1))
                if banks is DVE_BANKS:
                    ins = nc.vector.tensor_scalar(rows, bank, 1.0, 0.0, ALU.mult, ALU.add, accum_out=total)
                else:
                    ins = nc.scalar.activation(rows, bank, ACT.Copy, accum_out=total)
                ins.then_inc(taken[c], 1)

        @block.vector
        def _(dve):
            def one_hots(s):
                for h in range(2):
                    t = s * 2 + h
                    dve.wait_ge(used, t + 1)
                    nc.vector.tensor_scalar(at(oh_r, t & 3), K.iota_f[:, :], K.rel[:, bass.ds(t, 1)], None, ALU.is_equal)
                    nc.vector.tensor_scalar(at(oh_s, t & 3), K.iota16[:, :], K.sender_f[:, bass.ds(t, 1)], None,
                                            ALU.is_equal).then_inc(ready, 1)

            def window(w, u, n):
                lo, hi = bounds(dve, w)
                with dve.If(hi > lo + 1):
                    with dve.Fori(lo + 1, hi) as s:
                        one_hots(s)
                one_hots(hi)
                take(dve, w, u, n, DVE_BANKS)

            for c in DVE_BANKS:
                dve.sem_inc(taken[c], 1)
            for h in range(2):
                nc.vector.tensor_scalar(oh_r[:, h, :], K.iota_f[:, :], K.rel[:, h:h + 1], None, ALU.is_equal)
                nc.vector.tensor_scalar(oh_s[:, h, :], K.iota16[:, :], K.sender_f[:, h:h + 1], None, ALU.is_equal).then_inc(ready, 1)
            with dve.Fori(0, W // 2) as i:
                for u in range(2):
                    window(i * 2 + u, u, i)
            window(W - 1, 0, W // 2)

        @block.tensor
        def _(pe):
            def tile(t, first, last, w):
                pe.wait_ge(ready, t + 1)
                for c in range(NB):
                    n = min(CHUNK, NP - c * CHUNK)
                    if first:
                        pe.wait_ge(taken[c], w + 1)
                    ins = nc.tensor.matmul(ps[:, c, 0:n], at(oh_r, t & 3), at(oh_s, t & 3)[:, c * CHUNK:c * CHUNK + n],
                                           start=first, stop=last, skip_group_check=True)
                    if last:
                        ins.then_inc(counted, 1)
                if last:
                    pe.wait_ge(counted, w * NB + NB)
                    pe.sem_inc(used, 1)
                else:
                    ins.then_inc(used, 1)

            pe.sem_inc(used, 4)
            with pe.Fori(0, W) as w:
                lo, hi = bounds(pe, w)
                tile(lo * 2, True, False, w)
                with pe.If(hi > lo + 1):
                    with pe.Fori(lo + 1, hi) as s:
                        tile(s * 2 - 1, False, False, w)
                        tile(s * 2, False, False, w)
                tile(hi * 2 - 1, False, True, w)

        @block.scalar
        def _(act):
            def window(w, u, n):
                take(act, w, u, n, ACT_BANKS)
                for c in range(NB):
                    act.wait_ge(taken[c], w + 2)
                act.dma_start(a_dram[bass.ds(w, 1), :, :].rearrange("a p n -> p (a n)"), a_sb[u][:, :]).then_inc(stored[u], 16)

            for u in range(2):
                act.sem_inc(stored[u], 16)
            for c in ACT_BANKS:
                act.sem_inc(taken[c], 1)
            with act.Fori(0, W // 2) as i:
                for u in range(2):
                    window(i * 2 + u, u, i)
            window(W - 1, 0, W // 2)
            act.wait_ge(stored[0], 16 * (W // 2 + 1) + 16)
            act.wait_ge(stored[1], 16 * (W // 2) + 16)


def pipeline(eng, count, stages):
    leads = [lead for lead, _ in stages]
    begin, end = 4 - min(leads), count - max(leads)
    rounds = (end - begin) // 4

    def peeled(c):
        for lead, f in stages:
            if 0 <= c + lead < count:
                f(Index(None, offset=c + lead), (c + lead) % 4, Index(None, offset=(c + lead) // 4))

    for c in range(-max(leads), begin):
        peeled(c)
    with eng.Fori(0, rounds) as i:
        for j in range(4):
            for lead, f in stages:
                first = begin + j + lead
                f(Index(i, 4, first), first % 4, Index(i, 1, first // 4))
    for c in range(begin + 4 * rounds, count - min(leads)):
        peeled(c)


def encode_edges(nc, ctx, K, attr, attr_by_window, w_edge, b_edge, edges):
    B = 4
    CHUNKS = TILES // B
    with Part(nc, "encode", ctx) as p:
        wt, bias = p.sb("wt", [D, D]), p.sb("bias", [1, B, D])
        bias_h, bias_l, ones = p.sb("bias_h", [1, B * D], F32R), p.sb("bias_l", [1, B * D], F32R), p.sb("ones", [1, 128], F32R)
        two, four = range(2), range(4)
        raw = [p.sb(f"raw{m}", [128, B, D]) for m in four]
        raw_t = [p.sb(f"raw_t{b}", [128, B, D]) for b in two]
        act_out = [p.sb(f"act_out{m}", [128, B, D]) for m in four]
        normed = [p.sb(f"normed{b}", [128, B, D]) for b in two]
        both = [p.sb(f"both{m}", [128, B, 2, D], F32R) for m in four]
        stats, mv = [p.sb(f"stats{b}", [128, B, 6]) for b in two], [p.sb(f"mv{m}", [128, B, 2]) for m in four]
        var, rstd = [p.sb(f"var{b}", [128, B]) for b in two], [p.sb(f"rstd{b}", [128, B]) for b in two]
        power = p.sb("power", [128, B])
        ps_in = [p.ps(f"ps_in{b}", [128, B, D]) for b in two]
        ps_lin = [p.ps(f"ps_lin{b}", [128, B, D]) for b in two]
        ps_out = [p.ps(f"ps_out{b}", [128, B, D]) for b in two]
        consts, powered, turned, copied, lin, gelued, moments, rooted, norm_done, back, high_ready, low_ready = (
            p.sem(n) for n in ("consts", "powered", "turned", "copied", "lin", "gelued", "moments",
                               "rooted", "norm_done", "back", "high_ready", "low_ready"))
        begun, chain, bias_split = p.sem("begun"), p.sem("chain"), p.sem("bias_split")
        raw_in = [p.sem(f"raw_in{m}") for m in four]
        stored = [p.sem(f"stored{m}") for m in four]
        block = p.block()

        @block.sync
        def _(sp):
            sp.dma_start(wt[:, :], w_edge).then_inc(consts, 16)
            for b in range(B):
                sp.dma_start(bias[:, b, :], b_edge.rearrange("(a n) -> a n", a=1)).then_inc(consts, 16)

            def loads(table):
                def load(c, m, n):
                    at_least(sp, turned, c - 3)
                    for k in range(B // 2):
                        first = sp.value_load(K.first_of[0:1, bass.ds((c * (B // 2) + k).value, 1)], min_val=0, max_val=E - G)
                        sp.dma_start(raw[m][:, 2 * k:2 * k + 2, :],
                                     table[bass.ds(first, G), :].rearrange("(t l) d -> l t d", l=128)).then_inc(raw_in[m], 16)
                return load

            def store(c, m, n):
                at_least(sp, low_ready, c + 1)
                sp.dma_start(edges[:, bass.ds((c * B).value, B), :, :].rearrange("p b c d -> p (b c d)"),
                             both[m][:, :, :, :].rearrange("p b c d -> p (b c d)").bitcast(F32)).then_inc(stored[m], 16)

            unsorted = sp.value_load(K.unsorted[0:1, 0:1], min_val=0, max_val=E)
            with sp.If(unsorted > 0):
                pipeline(sp, CHUNKS, [(4, loads(attr_by_window)), (-3, store)])
            with sp.Else():
                pipeline(sp, CHUNKS, [(4, loads(attr)), (-3, store)])
            for m in four:
                sp.wait_ge(stored[m], 16 * len(range(m, CHUNKS, 4)))

        @block.tensor
        def _(pe):
            def transpose_in(c, m, n):
                b = m % 2
                at_least(pe, raw_in[m], n * (8 * B) + 8 * B)
                at_least(pe, copied, c - 1)
                for k in range(B):
                    ins = nc.tensor.transpose(ps_in[b][:, k, :], raw[m][:, k, :], K.ident[:, :])
                ins.then_inc(turned, 1)

            def linear(c, m, n):
                b = m % 2
                at_least(pe, copied, c + 1)
                at_least(pe, gelued, c - 1)
                for part in (bias_l, bias_h):
                    nc.tensor.matmul(ps_lin[b][:, :, :].rearrange("p k d -> p (k d)"), ones[:, :], part[:, :],
                                     start=part is bias_l, stop=False, skip_group_check=True)
                for k in range(B):
                    ins = nc.tensor.matmul(ps_lin[b][:, k, :], raw_t[b][:, k, :], wt[:, :], start=False, stop=k == B - 1,
                                           skip_group_check=True)
                ins.then_inc(lin, 1)

            def transpose_back(c, m, n):
                b = m % 2
                at_least(pe, norm_done, c + 1)
                at_least(pe, low_ready, c - 1)
                for k in range(B):
                    ins = nc.tensor.transpose(ps_out[b][:, k, :], normed[b][:, k, :], K.ident[:, :])
                ins.then_inc(back, 1)

            pe.wait_ge(consts, 16 * (B + 1))
            pe.wait_ge(bias_split, 3)
            pipeline(pe, CHUNKS, [(1, transpose_in), (0, linear), (-2, transpose_back)])

        @block.scalar
        def _(act):
            def copy_in(c, m, n):
                b = m % 2
                at_least(act, turned, c + 1)
                at_least(act, lin, c - 1)
                nc.scalar.copy(raw_t[b][:, :, :], ps_in[b][:, :, :]).then_inc(copied, 1)

            def gelu(c, m, n):
                b = m % 2
                at_least(act, lin, c + 1)
                at_least(act, norm_done, c - 3)
                nc.scalar.activation(act_out[m][:, :, :], ps_lin[b][:, :, :], ACT.Gelu_apprx_tanh).then_inc(gelued, 1)

            def copy_high(c, m, n):
                b = m % 2
                at_least(act, back, c + 1)
                at_least(act, stored[m], n * 16)
                nc.scalar.copy(both[m][:, :, 0, :], ps_out[b][:, :, :]).then_inc(high_ready, 1)
            pipeline(act, CHUNKS, [(1, copy_in), (0, gelu), (-3, copy_high)])

        @block.gpsimd
        def _(pool):
            nc.gpsimd.memset(power[:, :], -0.5).then_inc(powered, 1)
            pool.wait_ge(powered, 1)

            def root(c, m, n):
                b = m % 2
                at_least(pool, moments, c + 1)
                nc.gpsimd.tensor_tensor(rstd[b][:, :], var[b][:, :], power[:, :], ALU.pow).then_inc(rooted, 1)
            pipeline(pool, CHUNKS, [(0, root)])

        @block.vector
        def _(dve):
            def take_stats(c, m, n):
                b = m % 2
                at_least(dve, gelued, c + 1)
                for k in range(B):
                    ins = nc.vector.bn_stats(stats[b][:, k, :], act_out[m][:, k, :])
                ins.then_inc(chain, 1)

            def take_moments(c, m, n):
                b = m % 2
                at_least(dve, chain, c * 2 + 1)
                dve.sem_inc(begun, 1)
                for k in range(B):
                    ins = nc.vector.bn_aggr(mv[m][:, k, :], stats[b][:, k, :])
                ins.then_inc(chain, 1)

            def take_variance(c, m, n):
                b = m % 2
                at_least(dve, chain, c * 2 + 2)
                nc.vector.tensor_scalar(var[b][:, :], mv[m][:, :, 1:2].rearrange("p b c -> p (b c)"), LN_EPS, None,
                                        ALU.add).then_inc(moments, 1)

            def normalise(half):
                def f(c, m, n):
                    b = m % 2
                    if half == 0:
                        at_least(dve, rooted, c + 1)
                        at_least(dve, back, c - 1)
                    for k in range(half * B // 2, (half + 1) * B // 2):
                        ins = nc.vector.tensor_scalar(normed[b][:, k, :], act_out[m][:, k, :], mv[m][:, k, 0:1],
                                                      rstd[b][:, k:k + 1], ALU.subtract, ALU.mult)
                    if half:
                        ins.then_inc(norm_done, 1)
                return f

            def take_low(c, m, n):
                b = m % 2
                at_least(dve, high_ready, c + 1)
                nc.vector.tensor_tensor(both[m][:, :, 1, :], ps_out[b][:, :, :], both[m][:, :, 0, :].bitcast(F32), ALU.subtract).then_inc(low_ready, 1)
            flat = bias[:, :, :].rearrange("p k d -> p (k d)")
            dve.wait_ge(consts, 16 * (B + 1))
            nc.vector.tensor_copy(ones[:, :], K.ones[0:1, 0:128]).then_inc(bias_split, 1)
            nc.vector.tensor_copy(bias_h[:, :], flat).then_inc(bias_split, 1)
            dve.wait_ge(bias_split, 2)
            nc.vector.tensor_tensor(bias_l[:, :], flat, bias_h[:, :].bitcast(F32), ALU.subtract).then_inc(bias_split, 1)
            pipeline(dve, CHUNKS, [(0, take_stats), (-3, take_low), (0, take_moments), (-1, normalise(0)), (0, take_variance),
                                   (-1, normalise(1))])


def norm_moments(nc, ctx, K, name, x):
    with Part(nc, name, ctx) as p:
        stats, half, var, power = p.sb("stats", [R, W, 6]), p.sb("half", [R, W]), p.sb("var", [R, W]), p.sb("power", [R, W])
        ready, powered, rooted, chain = p.sem("ready"), p.sem("powered"), p.sem("rooted"), p.sem("chain")
        block = p.block()

        def col(c):
            return stats[:, :, c:c + 1].rearrange("p w c -> p (w c)")

        @block.vector
        def _(dve):
            link = Chain(dve, chain)
            for w in range(W):
                last = nc.vector.bn_stats(stats[:, w, :], x[:, w, :])
            link(last)
            nc.vector.tensor_tensor(var[:, :], col(2), col(5), ALU.add)
            link(nc.vector.tensor_tensor(half[:, :], col(1), col(4), ALU.subtract))
            link(nc.vector.tensor_scalar(half[:, :], half[:, :], 0.5, None, ALU.mult))
            nc.vector.tensor_tensor(K.mean[:, :], col(4), half[:, :], ALU.add)
            link(nc.vector.tensor_tensor(half[:, :], half[:, :], half[:, :], ALU.mult))
            link(nc.vector.scalar_tensor_tensor(out=var[:, :], in0=var[:, :], scalar=1.0 / D, in1=half[:, :],
                                                op0=ALU.mult, op1=ALU.add))
            nc.vector.tensor_scalar(var[:, :], var[:, :], LN_EPS, None, ALU.add).then_inc(ready, 1)

        @block.gpsimd
        def _(pool):
            nc.gpsimd.memset(power[:, :], -0.5).then_inc(powered, 1)
            pool.wait_ge(powered, 1)
            pool.wait_ge(ready, 1)
            nc.gpsimd.tensor_tensor(K.rstd[:, :], var[:, :], power[:, :], ALU.pow).then_inc(rooted, 1)
            pool.wait_ge(rooted, 1)


def project(nc, ctx, K, name, x, weights, width, finish, norm=False, relu=False, loads=(), extra=None, extra_sb=None, stores=None):
    with Part(nc, name, ctx) as p:
        two, four = range(2), range(4)
        tiles = [p.sb(f"rows{m}", [R, D]) for m in four]
        turned_sb = [p.sb(f"turned{m}", [D, R]) for m in four]
        more = [p.sb(f"more{m}", [D, R]) for m in four] if extra is not None else None
        ps_t = [p.ps(f"ps_t{b}", [128, 512]) for b in two]
        ps_o = [p.ps(f"ps_o{m}", [128, 512]) for m in four]
        loaded, staged, turned, copied, product, done, linked = (
            p.sem(n) for n in ("loaded", "staged", "turned", "copied", "product", "done", "linked"))
        stored = p.sem("stored")
        work = finish(p)
        block = p.block()

        @block.sync
        def _(sp):
            for dst, src in loads:
                sp.dma_start(dst, src).then_inc(loaded, 16)
            if loads:
                sp.wait_ge(loaded, 16 * len(loads))
            if stores is not None:
                def store(c, m, n):
                    at_least(sp, done, c + 1)
                    sp.dma_start(stores[0][bass.ds(c.value * R, R), :], at(stores[1], c.value)).then_inc(stored, 16)
                pipeline(sp, W, [(0, store)])
                sp.wait_ge(stored, 16 * W)

        @block.vector
        def _(dve):
            def stage(c, m, n):
                w = c.value
                at_least(dve, turned, c - 3)
                row = at(x, w)
                if norm:
                    ins = nc.vector.tensor_scalar(tiles[m][:, :], row, K.mean[:, bass.ds(w, 1)], K.rstd[:, bass.ds(w, 1)],
                                                  ALU.subtract, ALU.mult)
                else:
                    ins = nc.vector.tensor_copy(tiles[m][:, :], row)
                ins.then_inc(staged, 1)
                if extra is not None:
                    at_least(dve, product, c - 3)
                    nc.vector.tensor_copy(more[m][:, :], extra_sb[:, bass.ds(w * R, R)]).then_inc(staged, 1)

            def take(c, m, n):
                at_least(dve, product, c + 1)
                count = [0]

                def link(ins):
                    count[0] += 1
                    ins.then_inc(linked, 1)
                    at_least(dve, linked, c * work.links + count[0])
                work(nc, link, c.value, ps_o[m][0:R, 0:width]).then_inc(done, 1)
                assert count[0] == work.links
            if loads:
                dve.wait_ge(loaded, 16 * len(loads))
            pipeline(dve, W, [(2, stage), (-1, take)])

        @block.tensor
        def _(pe):
            per = 2 if extra is not None else 1

            def turn(c, m, n):
                at_least(pe, staged, c * per + per)
                at_least(pe, copied, c - 1)
                nc.tensor.transpose(ps_t[m % 2][:, 0:R], tiles[m][:, :], K.ident[0:R, 0:R]).then_inc(turned, 1)

            def multiply(c, m, n):
                at_least(pe, copied, c + 1)
                at_least(pe, done, c - 3)
                ins = nc.tensor.matmul(ps_o[m][0:R, 0:width], turned_sb[m][:, :], weights, start=True, stop=extra is None)
                if extra is not None:
                    ins = nc.tensor.matmul(ps_o[m][0:R, 0:width], more[m][:, :], extra, start=False, stop=True)
                ins.then_inc(product, 1)
            if loads:
                pe.wait_ge(loaded, 16 * len(loads))
            pipeline(pe, W, [(1, turn), (0, multiply)])

        @block.scalar
        def _(act):
            def copy(c, m, n):
                at_least(act, turned, c + 1)
                at_least(act, product, c - 3)
                nc.scalar.activation(turned_sb[m][:, :], ps_t[m % 2][:, 0:R], ACT.Relu if relu else ACT.Copy).then_inc(copied, 1)
            pipeline(act, W, [(0, copy)])


class Finish:

    def __init__(self, links, f):
        self.links, self.f = links, f

    def __call__(self, nc, link, w, product):
        return self.f(nc, link, w, product)


def at(t, w):
    return t[:, bass.ds(w, 1), :].rearrange("p a d -> p (a d)")


def spread(nc, ctx, K, name, g, bias, out, at_dram, a_dram=None, relu=False, residual=None):
    make = a_dram is not None
    with Part(nc, name, ctx) as p:
        two, four = range(2), range(4)
        parts = p.sb("parts", [R, W, 3, D], BF16)
        rest = p.sb("rest", [R, W, D])
        at_sb = [p.sb(f"at{m}", [128, W, 128], BF16) for m in four]
        a_sb = [p.sb(f"a{m}", [128, NP], BF16) for m in four] if make else None
        total = [p.sb(f"total{b}", [R, D]) for b in two]
        bias_sb = p.sb("bias", [128, D])
        ps = [p.ps(f"ps{b}", [128, 512]) for b in two]
        ps_t = [p.ps(f"ps_t{r}", [128, 8, 128], BF16) for r in four] if make else None
        biased, split, product, done, chain, added, turned, copied = (
            p.sem(n) for n in ("biased", "split", "product", "done", "chain", "added", "turned", "copied"))
        a_in = [p.sem(f"a_in{m}") for m in four]
        at_out = [p.sem(f"at_out{m}") for m in four]
        block = p.block()
        ROUNDS = [(r, range(8 * r, min(8 * r + 8, W))) for r in four]

        @block.vector
        def _(dve):
            link = Chain(dve, chain)
            for _, chunks in ROUNDS:
                s = slice(chunks[0], chunks[-1] + 1)
                link(nc.vector.tensor_copy(parts[:, s, 0, :], g[:, s, :]))
                link(nc.vector.tensor_tensor(rest[:, s, :], g[:, s, :], parts[:, s, 0, :], ALU.subtract))
                link(nc.vector.tensor_copy(parts[:, s, 1, :], rest[:, s, :]))
                link(nc.vector.tensor_tensor(rest[:, s, :], rest[:, s, :], parts[:, s, 1, :], ALU.subtract))
                nc.vector.tensor_copy(parts[:, s, 2, :], rest[:, s, :]).then_inc(split, 1)
            dve.wait_ge(biased, 16)
            links = 2 + (relu or residual is not None)

            def window(c, m, n):
                b, w = m % 2, c.value
                at_least(dve, product, c + 1)
                at_least(dve, done, c - 1)
                nc.vector.tensor_reduce(total[b][:, :], ps[b][0:R, 0:3 * D].rearrange("p (c d) -> p d c", c=3), AX.X, ALU.add).then_inc(added, 1)
                at_least(dve, added, c * links + 1)
                nc.vector.tensor_tensor(total[b][:, :], total[b][:, :], at(g, w), ALU.add).then_inc(added, 1)
                at_least(dve, added, c * links + 2)
                ins = nc.vector.scalar_tensor_tensor(out=at(out, w) if links == 2 else total[b][:, :], in0=total[b][:, :],
                                                     scalar=K.dinv[:, bass.ds(w, 1)], in1=bias_sb[0:R, :], op0=ALU.mult, op1=ALU.add)
                if links == 3:
                    ins.then_inc(added, 1)
                    at_least(dve, added, c * links + 3)
                if relu:
                    ins = nc.vector.tensor_scalar(at(out, w), total[b][:, :], 0.0, None, ALU.max)
                if residual is not None:
                    ins = nc.vector.tensor_tensor(at(out, w), total[b][:, :], at(residual, w), ALU.add)
                ins.then_inc(done, 1)
            pipeline(dve, W, [(0, window)])

        @block.tensor
        def _(pe):
            def turn(r, chunks):
                def f(c, m, n):
                    if r == 0:
                        at_least(pe, a_in[m], n * 16 + 16)
                    at_least(pe, copied, c * 4 + (r - 3))
                    for k, s in enumerate(chunks):
                        ins = nc.tensor.transpose(ps_t[r][:, k, :], a_sb[m][:, s * R:s * R + 128], K.ident16[:, :])
                    ins.then_inc(turned, 1)
                return f

            def multiply(r, chunks):
                def f(c, m, n):
                    b = m % 2
                    if r == 0:
                        at_least(pe, done, c - 1)
                    if make:
                        at_least(pe, copied, c * 4 + (r + 1))
                    elif r == 0:
                        at_least(pe, a_in[m], n * 16 + 16)
                    if c.x is None and c.offset == 0:
                        pe.wait_ge(split, r + 1)
                    for s in chunks:
                        ins = nc.tensor.matmul(ps[b][0:R, 0:3 * D], at_sb[m][0:R, s, 0:R], parts[:, s, :, :].rearrange("p c d -> p (c d)"),
                                               start=(s == 0), stop=(s == W - 1), skip_group_check=True)
                    if chunks[-1] == W - 1:
                        ins.then_inc(product, 1)
                return f

            stages = []
            for r, chunks in ROUNDS:
                stages += [(1, turn(r, chunks)), (0, multiply(r, chunks))] if make else [(0, multiply(r, chunks))]
            pipeline(pe, W, stages)

        @block.sync
        def _(sp):
            sp.dma_start(bias_sb[:, :], bias.partition_broadcast(128)).then_inc(biased, 16)

            def load(c, m, n):
                if make:
                    at_least(sp, turned, c * 4 - 12)
                    sp.dma_start(a_sb[m][:, :], a_dram[bass.ds(c.value, 1), :, :].rearrange("a p n -> p (a n)")).then_inc(a_in[m], 16)
                else:
                    at_least(sp, product, c - 3)
                    sp.dma_start(at_sb[m][:, :, :].rearrange("p k r -> p (k r)"),
                                 at_dram[bass.ds(c.value, 1), :, :].rearrange("a p n -> p (a n)")).then_inc(a_in[m], 16)
            pipeline(sp, W, [(0, load)])

        if make:
            @block.scalar
            def _(act):
                def copy(c, m, n):
                    at_least(act, product, c - 3)
                    at_least(act, at_out[m], n * 16)
                    for r, chunks in ROUNDS:
                        at_least(act, turned, c * 4 + (r + 1))
                        nc.scalar.copy(at_sb[m][:, 8 * r:8 * r + len(chunks), :], ps_t[r][:, 0:len(chunks), :]).then_inc(copied, 1)
                    at_least(act, copied, c * 4 + 4)
                    act.dma_start(at_dram[bass.ds(c.value, 1), :, :].rearrange("a p n -> p (a n)"),
                                  at_sb[m][:, :, :].rearrange("p k r -> p (k r)")).then_inc(at_out[m], 16)
                pipeline(act, W, [(0, copy)])
                for m in four:
                    act.wait_ge(at_out[m], 16 * len(range(m, W, 4)))


def sums_to_degrees(nc, ctx, K):
    with Part(nc, "degree", ctx) as p:
        deg, root = p.sb("deg", [R, W]), p.sb("root", [R, W])
        ready, rooted, chain = p.sem("ready"), p.sem("rooted"), p.sem("chain")
        block = p.block()

        @block.vector
        def _(dve):
            link = Chain(dve, chain)
            link(nc.vector.tensor_reduce(deg[:, :], K.deg[0:R, :, :], AX.X, ALU.add))
            nc.vector.tensor_scalar(deg[:, :], deg[:, :], 1.0, None, ALU.add).then_inc(ready, 1)
            dve.wait_ge(rooted, 1)
            link(nc.vector.reciprocal(K.dinv[:, :], root[:, :]))

        @block.scalar
        def _(act):
            act.wait_ge(ready, 1)
            nc.scalar.activation(root[:, :], deg[:, :], ACT.Sqrt).then_inc(rooted, 1)


def norm_apply(nc, ctx, K, name, x, out, scale=None, offset=None, relu=False, add_to=None, gelu_first=False):
    with Part(nc, name, ctx) as p:
        if scale is not None:
            scale_sb, offset_sb = p.sb("scale", [128, D]), p.sb("offset", [128, D])
        loaded, chain = p.sem("loaded"), p.sem("chain")
        block = p.block()

        @block.sync
        def _(sp):
            if scale is not None:
                sp.dma_start(scale_sb[:, :], scale.partition_broadcast(128)).then_inc(loaded, 16)
                sp.dma_start(offset_sb[:, :], offset.partition_broadcast(128)).then_inc(loaded, 16)
                sp.wait_ge(loaded, 32)

        @block.vector
        def _(dve):
            link = Chain(dve, chain)
            with dve.Fori(0, NC) as i:
                link.loop(i, 1)
                for u in range(U):
                    w = i * U + u
                    last = nc.vector.tensor_scalar(at(out, w), at(x, w), K.mean[:, bass.ds(w, 1)], K.rstd[:, bass.ds(w, 1)],
                                                   ALU.subtract, ALU.mult)
                link(last)
            link.end(NC)
            if relu:
                link(nc.vector.tensor_scalar(out[:, :, :], out[:, :, :], 0.0, None, ALU.max))
            if scale is not None:
                dve.wait_ge(loaded, 32)
                link(nc.vector.tensor_tensor(out[:, :, :], out[:, :, :], scale_sb[0:R, :].unsqueeze(1).to_broadcast([R, W, D]), ALU.mult))
                link(nc.vector.tensor_tensor(out[:, :, :], out[:, :, :], offset_sb[0:R, :].unsqueeze(1).to_broadcast([R, W, D]), ALU.add))
            if add_to is not None:
                link(nc.vector.tensor_tensor(add_to[:, :, :], add_to[:, :, :], out[:, :, :], ALU.add))


def gelu_nodes(nc, ctx, K, t):
    with Part(nc, "gelu", ctx) as p:
        done = p.sem("done")
        block = p.block()

        @block.scalar
        def _(act):
            nc.scalar.activation(t[:, :, :], t[:, :, :], ACT.Gelu_apprx_tanh).then_inc(done, 1)
            act.wait_ge(done, 1)


def message_weights(nc, ctx, K, name, M, w1, b1, w2, b2, e_scale, e_offset):
    with Part(nc, name, ctx) as p:
        raw = p.sb("raw", [D, H])
        sc, of = p.sb("sc", [D, 1]), p.sb("of", [D, 1])
        of_b = p.sb("of_b", [D, R])
        b1_sb = p.sb("b1", [128, H])
        ps = p.ps("ps", [128, 512])
        loaded, ready, done, chain = (p.sem(n) for n in ("loaded", "ready", "done", "chain"))
        block = p.block()
        loads = [(M.w_sr[:, 0:H], w1[0:D, :]), (M.w_sr[:, H:2 * H], w1[D:2 * D, :]), (raw[:, :], w1[2 * D:3 * D, :]),
                 (M.w2[:, :, :], w2.rearrange("(c k) n -> k c n", k=128)), (M.b2[:, :], b2.partition_broadcast(128)),
                 (b1_sb[:, :], b1.partition_broadcast(128)),
                 (sc[:, :], e_scale.rearrange("(p a) -> p a", a=1)), (of[:, :], e_offset.rearrange("(p a) -> p a", a=1))]

        @block.sync
        def _(sp):
            for dst, src in loads:
                sp.dma_start(dst, src).then_inc(loaded, 16)
            sp.wait_ge(loaded, 16 * len(loads))

        @block.vector
        def _(dve):
            link = Chain(dve, chain)
            dve.wait_ge(loaded, 16 * len(loads))
            link(nc.vector.tensor_scalar(M.w_e[:, :], raw[:, :], sc[:, 0:1], None, ALU.mult))
            link(nc.vector.tensor_copy(M.we_h[:, :], M.w_e[:, :]))
            link(nc.vector.tensor_tensor(M.we_l[:, :], M.w_e[:, :], M.we_h[:, :].bitcast(F32), ALU.subtract))
            nc.vector.tensor_scalar(of_b[:, :], K.ones[:, 0:R], of[:, 0:1], None, ALU.mult).then_inc(ready, 1)
            dve.wait_ge(done, 1)
            link(nc.vector.tensor_tensor(M.b_r[:, :], b1_sb[0:R, :], ps[0:R, 0:H], ALU.add))

        @block.tensor
        def _(pe):
            pe.wait_ge(loaded, 16 * len(loads))
            pe.wait_ge(ready, 1)
            nc.tensor.matmul(ps[0:R, 0:H], of_b[:, :], raw[:, :], start=True, stop=True).then_inc(done, 1)


def messages(nc, ctx, K, name, M, p_dram, edges, rel_rows):
    with Part(nc, name, ctx) as p:
        four, two = range(4), range(2)
        edge = [p.sb(f"edge{m}", [D, 2, 2, 128], F32R) for m in four]
        rel_b = [p.sb(f"rel_b{m}", [128, 256]) for m in four]
        got = [p.sb(f"got{m}", [128, 2, H]) for m in four]
        idx = [p.sb(f"idx{m}", [128, 2], I32) for m in four]
        oh = [p.sb(f"oh{m}", [128, 2, R + 1], F32R) for m in four]
        oh_t = [p.sb(f"oh_t{q}", [128, 256], F32R) for q in two]
        hid = [p.sb(f"hid{h}", [128, H]) for h in two]
        hid_t = [p.sb(f"hid_t{h}", [128, 2, 128]) for h in two]
        msg_b = p.sb("msg_b", [128, 2, D])
        msg_h, msg_l = ([p.sb(f"{n}{q}", [128, 2, D], F32R) for q in two] for n in ("msg_h", "msg_l"))
        ps1 = [p.ps(f"ps1_{h}", [128, 512]) for h in two]
        ps_t = [p.ps(f"ps_t{h}", [128, 4, 128]) for h in two]
        ps2 = p.ps("ps2", [128, 2, 512])
        ps_a = [p.ps(f"ps_a{q}", [128, 512]) for q in two]
        oht_ready, oh_ready, added, biased, rest_ready, cleared = (
            p.sem(n) for n in ("oht_ready", "oh_ready", "added", "biased", "rest_ready", "cleared"))
        first, turned, second, summed, banked = (p.sem(n) for n in ("first", "turned", "second", "summed", "banked"))
        relu1, relu2, idx_ready = (p.sem(n) for n in ("relu1", "relu2", "idx_ready"))
        begun, ended = p.sem("begun"), p.sem("ended")
        rel_in = [p.sem(f"rel_in{m}") for m in four]
        e_in = [p.sem(f"e_in{m}") for m in four]
        gathered = [[p.sem(f"gathered{m}{h}") for h in two] for m in four]
        block = p.block()

        def steps(eng):
            total = eng.value_load(K.bases[0:1, W:W + 1], min_val=1, max_val=MAX_GROUPS)
            return ((total + 3) >> 2) << 2, (total + 3) >> 2

        def groups(eng, step):
            total = eng.value_load(K.bases[0:1, W:W + 1], min_val=1, max_val=MAX_GROUPS)
            with eng.Fori(0, (total + 3) >> 2) as turn:
                for k in four:
                    step(Index(turn, 4, k), k, turn)

        def nth(turn, k, lead):
            return (k + lead) % 4, Index(turn, offset=(k + lead) // 4)


        @block.sync
        def _(sp):
            def load(g, m, waits):
                if waits:
                    at_least(sp, oht_ready, g - 3)
                sp.dma_start(rel_b[m][:, :], rel_rows[bass.ds(g.value, 1), :].to_broadcast([128, 256])).then_inc(rel_in[m], 16)
                if waits:
                    at_least(sp, first, g * 2 - 6)
                sp.dma_start(edge[m][:, :, :, :].rearrange("p t c l -> p (t c l)").bitcast(F32),
                             edges[:, bass.ds((g * 2).value, 2), :, :].rearrange("p t c l -> p (t c l)")).then_inc(e_in[m], 16)

            for m in four:
                load(ZERO + m, m, False)
            groups(sp, lambda g, k, turn: load(g + 4, k, True))
            _, rounds = steps(sp)
            for m in four:
                sp.wait_ge(rel_in[m], rounds * 16 + 16)
                sp.wait_ge(e_in[m], rounds * 16 + 16)
            sp.sem_inc(ended, 1)

        @block.gpsimd
        def _(pool):
            def gather(g, m, waits):
                nc.gpsimd.tensor_copy(idx[m][:, :], K.sender[:, bass.ds((g * 2).value, 2)]).then_inc(idx_ready, 1)
                at_least(pool, idx_ready, g + 1)
                if waits:
                    pool.sem_inc(begun, 1)
                for h in two:
                    pool.indirect_dma_start(got[m][:, h, :], None, p_dram,
                                            bass.IndirectOffsetOnAxis(ap=idx[m][:, h:h + 1], axis=0)).then_inc(gathered[m][h], 16)

            def step(g, k, turn):
                at_least(pool, added, g * 2 + 2)
                pool.sem_inc(begun, 1)
                gather(g + 4, k, True)

            for m in four:
                gather(ZERO + m, m, False)
            groups(pool, step)
            _, rounds = steps(pool)
            for m in four:
                for h in two:
                    pool.wait_ge(gathered[m][h], rounds * 16 + 16)
            pool.sem_inc(begun, 1)

        @block.vector
        def _(dve):
            def columns(g, q, m, n, waits):
                at_least(dve, rel_in[m], n * 16 + 16)
                if waits:
                    at_least(dve, first, g * 2 - 2)
                nc.vector.tensor_scalar(oh_t[q][:, :], rel_b[m][:, :], K.lane_f[:, 0:1], None, ALU.is_equal).then_inc(oht_ready, 1)

            def rows(g, m):
                for h in two:
                    nc.vector.tensor_scalar(oh[m][:, h, :], K.iota_f[:, 0:R + 1], K.rel[:, bass.ds((g * 2 + h).value, 1)], None,
                                            ALU.is_equal).then_inc(oh_ready, 1)

            def add(g, m, n, h, waits):
                at_least(dve, gathered[m][h], n * 16 + 16)
                at_least(dve, first, g * 2 + (h + 1))
                if waits:
                    at_least(dve, turned, g * 2 - 1 + h)
                nc.vector.tensor_tensor(hid[h][:, :], ps1[h][:, 0:H], got[m][:, h, :], ALU.add).then_inc(added, 1)

            def low_part(g, q):
                at_least(dve, relu2, g + 2)
                nc.vector.scalar_tensor_tensor(out=msg_l[q][:, :, :].rearrange("p h d -> p (h d)"),
                                               in0=msg_b[:, :, :].rearrange("p h d -> p (h d)"), scalar=0.0,
                                               in1=msg_h[q][:, :, :].bitcast(F32).rearrange("p h d -> p (h d)"),
                                               op0=ALU.max, op1=ALU.subtract).then_inc(rest_ready, 1)

            def bank(g, q, w):
                at_least(dve, summed, g + 3)
                at_least(dve, banked, g + 3)
                nc.vector.tensor_tensor(M.agg[:, bass.ds(w * R, R)], M.agg[:, bass.ds(w * R, R)], ps_a[q][:, 0:R],
                                        ALU.add).then_inc(banked, 1)

            def step(g, k, turn):
                q = k % 2
                add(g + 1, *nth(turn, k, 1), 0, True)
                low_part(g - 1, 1 - q)
                columns(g + 2, q, *nth(turn, k, 2), True)
                rows(g + 2, (k + 2) % 4)
                w = dve.value_load(K.win_of[0:1, bass.ds(g.value, 1)], min_val=0, max_val=W - 1)
                add(g + 1, *nth(turn, k, 1), 1, True)
                at_least(dve, second, g * 2 + 3)
                at_least(dve, rest_ready, g + 1)
                nc.vector.tensor_tensor(msg_b[:, :, :], ps2[:, :, 0:D], M.b2[:, :].unsqueeze(1).to_broadcast([128, 2, D]),
                                        ALU.add).then_inc(biased, 1)
                bank(g - 1, 1 - q, w)

            nc.vector.memset(M.agg[:, :], 0.0).then_inc(cleared, 1)
            for t in (msg_b[:, :, :], msg_h[1][:, :, :].bitcast(F32), oh[3][:, :, :].bitcast(F32)):
                nc.vector.memset(t, 0.0).then_inc(cleared, 1)
            dve.wait_ge(cleared, 4)
            dve.sem_inc(oh_ready, 2)
            dve.sem_inc(banked, 2)
            dve.sem_inc(biased, 1)
            for g in two:
                columns(ZERO + g, g, g, ZERO, False)
                rows(ZERO + g, g)
            for h in two:
                add(ZERO, 0, ZERO, h, False)
            groups(dve, step)
            total, _ = steps(dve)
            low_part(Index(total, offset=-1), 1)
            w = dve.value_load(K.win_of[0:1, bass.ds(total, 1)], min_val=0, max_val=W - 1)
            dve.wait_ge(summed, total + 2)
            dve.wait_ge(banked, total + 2)
            nc.vector.tensor_tensor(M.agg[:, bass.ds(w * R, R)], M.agg[:, bass.ds(w * R, R)], ps_a[1][:, 0:R], ALU.add).then_inc(banked, 1)

        @block.tensor
        def _(pe):
            def products(g, q, m, n, h, w, waits):
                if h == 0:
                    at_least(pe, e_in[m], n * 16 + 16)
                    at_least(pe, oht_ready, g + 1)
                if waits:
                    at_least(pe, added, g * 2 - 1 + h)
                out = ps1[h][:, 0:H]
                nc.tensor.matmul(out, edge[m][:, h, 1, :], M.we_h[:, :], start=True, stop=False)
                nc.tensor.matmul(out, edge[m][:, h, 0, :], M.we_l[:, :], start=False, stop=False)
                nc.tensor.matmul(out, edge[m][:, h, 0, :], M.we_h[:, :], start=False, stop=False)
                nc.tensor.matmul(out, oh_t[q][0:R, h * 128:(h + 1) * 128], at(M.recv_l, w), start=False, stop=False)
                nc.tensor.matmul(out, oh_t[q][0:R, h * 128:(h + 1) * 128], at(M.recv_h, w), start=False, stop=True).then_inc(first, 1)

            def turn_hidden(g, h, waits):
                at_least(pe, added, g * 2 + (h + 1))
                if waits:
                    at_least(pe, relu1, g * 2 - 1 + 2 * h)
                for c in two:
                    ins = nc.tensor.transpose(ps_t[h][:, c, :], hid[h][:, c * 128:(c + 1) * 128], K.ident[:, :])
                ins.then_inc(turned, 1)

            def message(g, h):
                at_least(pe, relu1, g * 2 + (h + 1))
                if h == 0:
                    at_least(pe, biased, g + 1)
                for c in two:
                    ins = nc.tensor.matmul(ps2[:, h, 0:D], hid_t[h][:, c, :], M.w2[:, c, :], start=(c == 0), stop=(c == 1))
                ins.then_inc(second, 1)

            def sums(q, m):
                for h in two:
                    for part in (msg_l[q], msg_h[q]):
                        ins = nc.tensor.matmul(ps_a[q][:, 0:R + 1], part[:, h, :], oh[m][:, h, :],
                                               start=(h == 0 and part is msg_l[q]), stop=(h == 1 and part is msg_h[q]))
                ins.then_inc(summed, 1)

            def step(g, k, turn):
                q = k % 2
                w = pe.value_load(K.win_of[0:1, bass.ds((g + 2).value, 1)], min_val=0, max_val=W - 1)
                products(g + 1, 1 - q, *nth(turn, k, 1), 0, w, True)
                turn_hidden(g, 1, True)
                message(g, 0)
                products(g + 1, 1 - q, *nth(turn, k, 1), 1, w, True)
                turn_hidden(g + 1, 0, True)
                message(g, 1)
                at_least(pe, banked, g + 1)
                at_least(pe, rest_ready, g + 1)
                at_least(pe, oh_ready, g * 2 + 2)
                sums(1 - q, (k + 3) % 4)

            pe.sem_inc(summed, 1)
            pe.sem_inc(second, 1)
            w = pe.value_load(K.win_of[0:1, 1:2], min_val=0, max_val=W - 1)
            for h in two:
                products(ZERO, 0, 0, ZERO, h, w, False)
            turn_hidden(ZERO, 0, False)
            groups(pe, step)
            total, _ = steps(pe)
            pe.wait_ge(banked, total + 1)
            pe.wait_ge(rest_ready, total + 1)
            pe.wait_ge(oh_ready, total * 2 + 2)
            sums(1, 3)

        @block.scalar
        def _(act):
            def relu_turned(g, h, waits):
                at_least(act, turned, g * 2 + (h + 1))
                if waits:
                    at_least(act, second, g * 2 + h)
                nc.scalar.activation(hid_t[h][:, :, :], ps_t[h][:, 0:2, :], ACT.Relu).then_inc(relu1, 1)

            def step(g, k, turn):
                q = k % 2
                relu_turned(g, 1, True)
                relu_turned(g + 1, 0, True)
                at_least(act, biased, g + 2)
                at_least(act, summed, g + 1)
                nc.scalar.activation(msg_h[q][:, :, :], msg_b[:, :, :], ACT.Relu).then_inc(relu2, 1)

            act.sem_inc(relu2, 1)
            relu_turned(ZERO, 0, False)
            groups(act, step)


def attend(nc, ctx, K, h, w_row, a_dram, s_dram):
    with Part(nc, "attend", ctx) as p:
        two, four = range(2), range(4)
        w_sb = p.sb("w", [128, D])
        s_col, s_turned = p.sb("s_col", [R, W]), p.sb("s_turned", [W, R])
        low = p.sb("low", [R, 1])
        srel = p.sb("srel", [R, N])
        a_sb = [p.sb(f"a{m}", [128, NP], BF16) for m in four]
        member = p.sb("member", [R, N], BF16)
        masked = [p.sb(f"masked{m}", [R, N]) for m in four]
        wt_t = [p.sb(f"wt_t{b}", [R, W, R]) for b in two]
        prod = wt_t[0][:, :, :].rearrange("p a b -> p (a b)")
        top, ntop = ([p.sb(f"{n}{b}", [R, 1]) for b in two] for n in ("top", "ntop"))
        den, rden = ([p.sb(f"{n}{m}", [R, 1]) for m in four] for n in ("den", "rden"))
        ps_s = p.ps("ps_s", [128, 512])
        ps_t = [p.ps(f"ps_t{j}", [128, 512]) for j in four]
        ps_o = [p.ps(f"ps_o{b}", [128, 512]) for b in two]
        w_in, scored, s_ready, s_out, s_stored, s_in, chain = (p.sem(n) for n in ("w_in", "scored", "s_ready", "s_out", "s_stored", "s_in", "chain"))
        membered, maxed, topped, exped, weighted, bounded, inverted, turned, copied, product, done, begun = (
            p.sem(n) for n in ("membered", "maxed", "topped", "exped", "weighted", "bounded", "inverted", "turned",
                               "copied", "product", "done", "begun"))
        a_in = [p.sem(f"a_in{m}") for m in four]
        block = p.block()
        BANKS = [(j, range(4 * j, min(4 * j + 4, W))) for j in range(-(-W // 4))]
        NB = len(BANKS)

        @block.sync
        def _(sp):
            sp.dma_start(w_sb[:, :], w_row.to_broadcast([128, D])).then_inc(w_in, 16)
            sp.wait_ge(s_out, 1)
            sp.dma_start(s_dram.rearrange("(w p) -> w p", p=R), s_turned[:, :]).then_inc(s_stored, 16)
            sp.wait_ge(s_stored, 16)
            sp.dma_start(srel[:, :], s_dram.partition_broadcast(R)).then_inc(s_in, 16)

            def load(c, m, n):
                at_least(sp, weighted, c - 3)
                sp.dma_start(a_sb[m][:, :], a_dram[bass.ds(c.value, 1), :, :].rearrange("a p n -> p (a n)")).then_inc(a_in[m], 16)
            pipeline(sp, W, [(0, load)])

        @block.vector
        def _(dve):
            link = Chain(dve, chain)
            dve.wait_ge(w_in, 16)
            for a, n in ((0, 12), (12, W - 12)):
                part = prod[:, 0:n * D].rearrange("p (w d) -> p w d", d=D)
                link(nc.vector.tensor_tensor(part, h[:, a:a + n, :], w_sb[0:R, :].unsqueeze(1).to_broadcast([R, n, D]), ALU.mult))
                link(nc.vector.tensor_reduce(s_col[:, a:a + n], part, AX.X, ALU.add))
            dve.sem_inc(scored, 1)
            dve.wait_ge(s_ready, 1)
            nc.vector.tensor_copy(s_turned[:, :], ps_s[0:W, 0:R]).then_inc(s_out, 1)
            dve.wait_ge(s_in, 16)
            link(nc.vector.tensor_reduce(low[:, :], srel[:, :], AX.X, ALU.min))
            link(nc.vector.tensor_scalar(srel[:, :], srel[:, :], low[:, 0:1], None, ALU.subtract))

            def take_max(c, m, n):
                b = m % 2
                at_least(dve, a_in[m], n * 16 + 16)
                nc.vector.tensor_scalar(member[:, :], a_sb[m][0:R, 0:N], 1.0, None, ALU.min).then_inc(membered, 1)
                at_least(dve, membered, c + 1)
                at_least(dve, turned, c * NB - 3 * NB)
                dve.sem_inc(begun, 1)
                nc.vector.tensor_tensor_reduce(out=masked[m][:, :], in0=member[:, :], in1=srel[:, :], scale=1.0, scalar=0.0,
                                               op0=ALU.mult, op1=ALU.max, accum_out=top[b][:, 0:1]).then_inc(maxed, 1)
                at_least(dve, maxed, c + 1)
                nc.vector.tensor_scalar(ntop[b][:, :], top[b][:, :], -1.0, None, ALU.mult).then_inc(topped, 1)

            def weigh(c, m, n):
                b = m % 2
                at_least(dve, exped, c + 1)
                nc.vector.tensor_tensor_reduce(out=masked[m][:, :], in0=masked[m][:, :], in1=a_sb[m][0:R, 0:N], scale=1.0, scalar=0.0,
                                               op0=ALU.mult, op1=ALU.add, accum_out=den[m][:, 0:1]).then_inc(weighted, 1)

            def add(c, m, n):
                b, w = m % 2, c.value
                at_least(dve, weighted, c + 1)
                nc.vector.tensor_scalar(den[m][:, :], den[m][:, :], 1e-20, None, ALU.max).then_inc(bounded, 1)
                at_least(dve, bounded, c + 1)
                at_least(dve, done, c - 3)
                nc.vector.reciprocal(rden[m][:, :], den[m][:, :]).then_inc(inverted, 1)
                at_least(dve, inverted, c + 1)
                at_least(dve, product, c + 1)
                nc.vector.scalar_tensor_tensor(out=at(K.x, w), in0=ps_o[b][0:R, 0:D], scalar=rden[m][:, 0:1], in1=at(K.x, w),
                                               op0=ALU.mult, op1=ALU.add).then_inc(done, 1)
            pipeline(dve, W, [(1, take_max), (0, weigh), (-2, add)])

        @block.scalar
        def _(act):
            def exponent(c, m, n):
                b = m % 2
                at_least(act, topped, c + 1)
                nc.scalar.activation(masked[m][:, :], masked[m][:, :], ACT.Exp, bias=ntop[b][:, 0:1]).then_inc(exped, 1)

            def copy(c, m, n):
                b = m % 2
                at_least(act, product, c - 1)
                for j, chunks in BANKS:
                    at_least(act, turned, c * NB + (j + 1))
                    k = len(chunks)
                    nc.scalar.copy(wt_t[b][:, 4 * j:4 * j + k, :], ps_t[j % 4][0:R, 0:k * R].rearrange("p (k r) -> p k r", r=R)).then_inc(copied, 1)
            pipeline(act, W, [(1, exponent), (0, copy)])

        @block.tensor
        def _(pe):
            pe.wait_ge(scored, 1)
            nc.tensor.transpose(ps_s[0:W, 0:R], s_col[:, :], K.ident[0:R, 0:R]).then_inc(s_ready, 1)

            def turn(j, chunks):
                def f(c, m, n):
                    if j == 0:
                        at_least(pe, weighted, c + 1)
                    before = j - 4 if j >= 4 else max(k for k in range(NB) if k % 4 == j) - NB
                    at_least(pe, copied, c * NB + (before + 1))
                    for k, s in enumerate(chunks):
                        ins = nc.tensor.transpose(ps_t[j % 4][0:R, k * R:(k + 1) * R], masked[m][:, s * R:(s + 1) * R], K.ident[0:R, 0:R])
                    ins.then_inc(turned, 1)
                return f

            def multiply(j, chunks):
                def f(c, m, n):
                    b = m % 2
                    if j == 0:
                        at_least(pe, done, c - 1)
                    at_least(pe, copied, c * NB + (j + 1))
                    for s in chunks:
                        ins = nc.tensor.matmul(ps_o[b][0:R, 0:D], wt_t[b][:, s, :], h[:, s, :], start=(s == 0), stop=(s == W - 1),
                                               skip_group_check=True)
                    if chunks[-1] == W - 1:
                        ins.then_inc(product, 1)
                return f

            stages = []
            for j, chunks in BANKS:
                stages += [(1, turn(j, chunks)), (0, multiply(j, chunks))]
            pipeline(pe, W, stages)


class Layer:

    def __init__(self, p):
        self.w_sr, self.w_e, self.w2 = p.sb("w_sr", [D, 2 * H]), p.sb("w_e", [D, H]), p.sb("w2", [128, 2, D])
        self.we_h, self.we_l = p.sb("we_h", [D, H], F32R), p.sb("we_l", [D, H], F32R)
        self.b2, self.b_r = p.sb("b2", [128, D]), p.sb("b_r", [R, H])
        self.send, self.recv = p.sb("send", [R, W, H]), [p.sb("recv", [R, H])]
        self.recv_h, self.recv_l = p.sb("recv_h", [R, W, H], F32R), p.sb("recv_l", [R, W, H], F32R)
        self.agg = p.sb("agg", [D, N])


def scaled_by_dinv(K, g):
    return lambda p: Finish(0, lambda nc, link, w, product: nc.vector.tensor_scalar(
        at(g, w), product, K.dinv[:, bass.ds(w, 1)], None, ALU.mult))


def plus_row(out, row):
    return lambda p: Finish(0, lambda nc, link, w, product: nc.vector.tensor_tensor(at(out, w), product, row[0:R, :], ALU.add))


def into_tables(M):
    def f(nc, link, w, product):
        link(nc.vector.tensor_tensor(M.recv[0][:, :], product[:, H:2 * H], M.b_r[:, :], ALU.add))
        link(nc.vector.tensor_copy(at(M.recv_h, w), M.recv[0][:, :]))
        link(nc.vector.tensor_tensor(at(M.recv_l, w), M.recv[0][:, :], at(M.recv_h, w).bitcast(F32), ALU.subtract))
        return nc.vector.tensor_copy(at(M.send, w), product[:, 0:H])
    return lambda p: Finish(3, f)


def turn_weights(nc, ctx, K, name, w, out):
    with Part(nc, name, ctx) as p:
        raw, ps = p.sb("raw", [D, D]), p.ps("ps", [128, 512])
        loaded, turned, copied = p.sem("loaded"), p.sem("turned"), p.sem("copied")
        block = p.block()

        @block.sync
        def _(sp):
            sp.dma_start(raw[:, :], w).then_inc(loaded, 16)

        @block.tensor
        def _(pe):
            pe.wait_ge(loaded, 16)
            nc.tensor.transpose(ps[:, 0:D], raw[:, :], K.ident[:, :]).then_inc(turned, 1)

        @block.vector
        def _(dve):
            dve.wait_ge(turned, 1)
            nc.vector.tensor_copy(out[:, :], ps[:, 0:D]).then_inc(copied, 1)
            dve.wait_ge(copied, 1)


def store_result(nc, ctx, K, out):
    with Part(nc, "result", ctx) as p:
        stored = p.sem("stored")
        block = p.block()

        @block.sync
        def _(sp):
            sp.dma_start(out.rearrange("(w p) d -> p w d", p=R), K.x[:, :, :]).then_inc(stored, 16)
            sp.wait_ge(stored, 16)


def gcn(nc, ctx, K, name, at_dram, w1, b1, w2, b2, a_dram=None, turn=False):
    with Part(nc, name, ctx) as p:
        w_sb, g, hid = p.sb("w", [D, D]), p.sb("g", [R, W, D]), p.sb("hid", [R, W, D])
        norm_moments(nc, ctx, K, name + "_norm", K.x)
        for n, (w, b) in enumerate(((w1, b1), (w2, b2))):
            if turn:
                turn_weights(nc, ctx, K, f"{name}_turn{n}", w, w_sb)
            project(nc, ctx, K, f"{name}_lin{n}", hid if n else K.x, w_sb[:, :], D, scaled_by_dinv(K, g),
                    norm=not n, relu=not n, loads=() if turn else ((w_sb[:, :], w),))
            spread(nc, ctx, K, f"{name}_spread{n}", g, b, K.x if n else hid, at_dram, a_dram=None if n else a_dram,
                   relu=not n, residual=K.x if n else None)


def bass_graph_layers(nc, io, out):
    by_window = (nc.dram_tensor("src_by_window", (E, 1), I32, kind="Internal").ap(),
                 nc.dram_tensor("dst_by_window", (E, 1), I32, kind="Internal").ap(),
                 nc.dram_tensor("attr_by_window", (E, D), F32, kind="Internal").ap())
    rel_rows = nc.dram_tensor("rel_rows", (GROUPS, G), F32, kind="Internal").ap()
    a_dram = nc.dram_tensor("a_rows", (W, 128, NP), BF16, kind="Internal").ap()
    at_dram = nc.dram_tensor("a_cols", (W, 128, W * 128), BF16, kind="Internal").ap()
    edges = nc.dram_tensor("edges", (D, TILES, 2, 128), F32, kind="Internal").ap()
    p_dram = nc.dram_tensor("send_rows", (N, H), F32, kind="Internal").ap()
    s_dram = nc.dram_tensor("scores", (N,), F32, kind="Internal").ap()
    with ExitStack() as kept:
        sorting = ExitStack()
        K = Kept(nc, kept, sorting)
        with sorting, Scope(nc) as ctx:
            build_constants(nc, ctx, K)
            given = (io["src"], io["dst"], io["edge_attr_128"])
            sort_edges(nc, ctx, K, io["src"], io["dst"])
            reorder_edges(nc, ctx, K, *given, by_window)
            read_slots(nc, ctx, K, given, [t.rearrange("e a -> (e a)") for t in by_window[0:2]], rel_rows, io["x"])
            count_edges(nc, ctx, K, a_dram)
            sums_to_degrees(nc, ctx, K)
        with Scope(nc) as ctx:
            gcn(nc, ctx, K, "l0", at_dram, io["L0_gnn_W1"], io["L0_gnn_b1"], io["L0_gnn_W2"], io["L0_gnn_b2"], a_dram=a_dram)
        with Scope(nc) as ctx:
            encode_edges(nc, ctx, K, io["edge_attr_128"], by_window[2], io["L1_gnn_w_edge"], io["L1_gnn_b_edge"], edges)
        with Part(nc, "l1", None) as p:
            M = Layer(p)
            n_sb, t_sb = p.sb("n", [R, W, D]), p.sb("t", [R, W, D])
            w_sb, w2_sb, b_sb = p.sb("w", [D, D]), p.sb("w_upd", [D, D]), p.sb("b", [128, D])
            with Scope(nc) as ctx:
                norm_moments(nc, ctx, K, "l1_norm", K.x)
                project(nc, ctx, K, "l1_node", K.x, w_sb[:, :], D, plus_row(t_sb, b_sb), norm=True, relu=True,
                        loads=((w_sb[:, :], io["L1_gnn_w_node"]), (b_sb[:, :], io["L1_gnn_b_node"].partition_broadcast(128))))
                gelu_nodes(nc, ctx, K, t_sb)
                norm_moments(nc, ctx, K, "l1_norm_n", t_sb)
                norm_apply(nc, ctx, K, "l1_apply", t_sb, n_sb, scale=io["L1_gnn_ln_n_scale"], offset=io["L1_gnn_ln_n_offset"])
            for l in range(3):
                with Scope(nc) as ctx:
                    message_weights(nc, ctx, K, f"l1_w{l}", M, io["L1_gnn_msg_w1"][l], io["L1_gnn_msg_b1"][l], io["L1_gnn_msg_w2"][l],
                                    io["L1_gnn_msg_b2"][l], io["L1_gnn_ln_e_scale"], io["L1_gnn_ln_e_offset"])
                    project(nc, ctx, K, f"l1_tables{l}", n_sb, M.w_sr[:, :], 2 * H, into_tables(M), stores=(p_dram, M.send))
                    messages(nc, ctx, K, f"l1_msg{l}", M, p_dram, edges, rel_rows)
                    upd = io["L1_gnn_upd_w"][l]
                    project(nc, ctx, K, f"l1_upd{l}", n_sb, w_sb[:, :], D, plus_row(t_sb, b_sb), extra=w2_sb[:, :], extra_sb=M.agg,
                            loads=((w_sb[:, :], upd[0:D, :]), (w2_sb[:, :], upd[D:2 * D, :]),
                                   (b_sb[:, :], io["L1_gnn_upd_b"][l].partition_broadcast(128))))
                    norm_moments(nc, ctx, K, f"l1_norm{l}", t_sb)
                    norm_apply(nc, ctx, K, f"l1_add{l}", t_sb, t_sb, scale=io["L1_gnn_ln_scale"][l], offset=io["L1_gnn_ln_offset"][l],
                               add_to=n_sb)
            with Scope(nc) as ctx:
                add_nodes(nc, ctx, K, n_sb)
        with Scope(nc) as ctx, Part(nc, "l2", None) as p:
            h_sb = p.sb("h", [R, W, D])
            norm_moments(nc, ctx, K, "l2_norm", K.x)
            norm_apply(nc, ctx, K, "l2_apply", K.x, h_sb, relu=True)
            attend(nc, ctx, K, h_sb, io["L2_gnn_W"], a_dram, s_dram)
        with Scope(nc) as ctx:
            gcn(nc, ctx, K, "l3", at_dram, io["L3_gnn_W1"], io["L3_gnn_b1"], io["L3_gnn_W2"], io["L3_gnn_b2"], turn=True)
            store_result(nc, ctx, K, out)


def add_nodes(nc, ctx, K, n_sb):
    with Part(nc, "l1_out", ctx) as p:
        done = p.sem("done")
        block = p.block()

        @block.vector
        def _(dve):
            nc.vector.tensor_tensor(K.x[:, :, :], K.x[:, :, :], n_sb[:, :, :], ALU.add).then_inc(done, 1)
            dve.wait_ge(done, 1)


_INS = ["x", "src", "dst", "edge_attr_128", "L0_gnn_W1", "L0_gnn_b1", "L0_gnn_W2", "L0_gnn_b2",
        "L1_gnn_w_node", "L1_gnn_b_node", "L1_gnn_w_edge", "L1_gnn_b_edge", "L1_gnn_ln_n_scale", "L1_gnn_ln_n_offset",
        "L1_gnn_ln_e_scale", "L1_gnn_ln_e_offset", "L1_gnn_msg_w1", "L1_gnn_msg_b1", "L1_gnn_msg_w2", "L1_gnn_msg_b2",
        "L1_gnn_upd_w", "L1_gnn_upd_b", "L1_gnn_ln_scale", "L1_gnn_ln_offset", "L2_gnn_W",
        "L3_gnn_W1", "L3_gnn_b1", "L3_gnn_W2", "L3_gnn_b2"]


def kernel(**inputs):
    import numpy as np
    import concourse.bacc as bacc
    from concourse.bass_utils import run_bass_kernel_spmd

    nc = bacc.Bacc("TRN2", target_bir_lowering=False, num_devices=1)
    arrays, io = {}, {}
    for name in _INS:
        a = np.ascontiguousarray(inputs[name])
        arrays[f"in_{name}"] = a
        io[name] = nc.dram_tensor(f"in_{name}", a.shape, mybir.dt.from_np(a.dtype), kind="ExternalInput").ap()
    out = nc.dram_tensor("out_0", (N, D), F32, kind="ExternalOutput").ap()
    bass_graph_layers(nc, io, out)
    r = run_bass_kernel_spmd(nc, [arrays], core_ids=[0])
    return r.results[0]["out_0"]
```
